# Optimizing a Trainium2 kernel written in Bass

```python
import numpy as np
import jax
import jax.numpy as jnp

def _softmax(x, axis=-1):
    return jax.nn.softmax(x, axis=axis)

def _gelu(x):
    return jax.nn.gelu(x, approximate=True)

def _silu(x):
    return jax.nn.silu(x)

def _sigmoid(x):
    return jax.nn.sigmoid(x)

def _layernorm(x, axis=-1, eps=1e-05):
    m = jnp.mean(x, axis=axis, keepdims=True)
    v = jnp.var(x, axis=axis, keepdims=True)
    return (x - m) / jnp.sqrt(v + eps)

def _scatter_add(tgt, idx, src, axis=0):
    return tgt.at[idx].add(src)

def _segment_sum(src, seg, n):
    return jax.ops.segment_sum(src, seg, n)
kernel_name = 'mk_gnn_ffn_d1_gnn_r8_cc42c7'

def setup_inputs(seed: int=0):
    np.random.seed(seed)
    _w = jnp.asarray

    def _rec_inputs():
        import jax
        import jax.numpy as jnp
        _gk = jax.random.key(seed)
        x = -0.0003713 + 1 * jax.random.normal(jax.random.fold_in(_gk, 1), (6250, 256), jnp.float32)
        src = jax.random.randint(jax.random.fold_in(_gk, 2), (100000,), 0, 6250, jnp.int32)
        dst = jax.random.randint(jax.random.fold_in(_gk, 3), (100000,), 0, 6250, jnp.int32)
        _o = jnp.argsort(dst, stable=True)
        src = src[_o]
        dst = dst[_o]
        return (x, src, dst)
    x, src, dst = _rec_inputs()

    def _L0_gnn_setup():
        import jax, jax.numpy as jnp
        import numpy as np
        N_NODES = 6250
        N_EDGES = 100000
        IN_FEATS = 256
        OUT_FEATS = 256
        NUM_HEADS = 8
        FEATS_PER_HEAD = OUT_FEATS // NUM_HEADS
        LN_EPS = 1e-05
        key = jax.random.key(seed)
        ks = jax.random.split(key, 8)
        glorot = lambda k, shp: jax.random.normal(k, shp, jnp.float32) * np.sqrt(2.0 / (shp[0] + shp[-1]))
        return {'feat': jax.random.normal(ks[0], (N_NODES, IN_FEATS), jnp.float32), 'Wsrc': glorot(ks[1], (OUT_FEATS, IN_FEATS)), 'bsrc': jnp.zeros((OUT_FEATS,), jnp.float32), 'Wdst': glorot(ks[2], (OUT_FEATS, IN_FEATS)), 'bdst': jnp.zeros((OUT_FEATS,), jnp.float32), 'Wval': glorot(ks[3], (OUT_FEATS, IN_FEATS)), 'bval': jnp.zeros((OUT_FEATS,), jnp.float32), 'attn': glorot(ks[4], (1, NUM_HEADS, FEATS_PER_HEAD)), 'src': jax.random.randint(ks[5], (N_EDGES,), 0, N_NODES, jnp.int32), 'dst': jax.random.randint(ks[6], (N_EDGES,), 0, N_NODES, jnp.int32)}
    _L0_gnn_all = _L0_gnn_setup()
    _L0_gnn_in = {k: v for k, v in _L0_gnn_all.items() if k in ('Wsrc', 'bsrc', 'Wdst', 'bdst', 'Wval', 'bval', 'attn')}
    del _L0_gnn_all

    def _L0_ffn_setup():
        import jax, jax.numpy as jnp
        import numpy as np
        B, S, H, F, E, K = (8, 512, 256, 512, 16, 2)
        EPS = 1e-05
        key = jax.random.key(seed)
        ks = jax.random.split(key, 9)
        sc = 0.02
        return {'x': jax.random.normal(ks[0], (B, S, H), dtype=jnp.float32), 'gate_w': jax.random.normal(ks[1], (H, E), dtype=jnp.float32) * sc, 'gate_b': jnp.zeros((E,), dtype=jnp.float32), 'w1': jax.random.normal(ks[2], (E, H, F), dtype=jnp.float32) * sc, 'b1': jnp.zeros((E, F), dtype=jnp.float32), 'w2': jax.random.normal(ks[3], (E, F, H), dtype=jnp.float32) * sc, 'b2': jnp.zeros((E, H), dtype=jnp.float32), 'gamma': jnp.ones((H,), dtype=jnp.float32), 'beta': jnp.zeros((H,), dtype=jnp.float32)}
    _L0_ffn_all = _L0_ffn_setup()
    _L0_ffn_in = {k: v for k, v in _L0_ffn_all.items() if k in ('gate_w', 'gate_b', 'w1', 'b1', 'w2', 'b2', 'gamma', 'beta')}
    del _L0_ffn_all
    return {'x': x, 'src': src, 'dst': dst, 'L0_gnn_Wsrc': _L0_gnn_in['Wsrc'], 'L0_gnn_bsrc': _L0_gnn_in['bsrc'], 'L0_gnn_Wdst': _L0_gnn_in['Wdst'], 'L0_gnn_bdst': _L0_gnn_in['bdst'], 'L0_gnn_Wval': _L0_gnn_in['Wval'], 'L0_gnn_bval': _L0_gnn_in['bval'], 'L0_gnn_attn': _L0_gnn_in['attn'], 'L0_ffn_gate_w': _L0_ffn_in['gate_w'], 'L0_ffn_gate_b': _L0_ffn_in['gate_b'], 'L0_ffn_w1': _L0_ffn_in['w1'], 'L0_ffn_b1': _L0_ffn_in['b1'], 'L0_ffn_w2': _L0_ffn_in['w2'], 'L0_ffn_b2': _L0_ffn_in['b2'], 'L0_ffn_gamma': _L0_ffn_in['gamma'], 'L0_ffn_beta': _L0_ffn_in['beta']}

def reference(x, src, dst, L0_gnn_Wsrc, L0_gnn_bsrc, L0_gnn_Wdst, L0_gnn_bdst, L0_gnn_Wval, L0_gnn_bval, L0_gnn_attn, L0_ffn_gate_w, L0_ffn_gate_b, L0_ffn_w1, L0_ffn_b1, L0_ffn_w2, L0_ffn_b2, L0_ffn_gamma, L0_ffn_beta):
    import jax
    import jax.numpy as jnp

    def _L0_gnn_ref(feat, Wsrc, bsrc, Wdst, bdst, Wval, bval, attn, src, dst):
        import jax, jax.numpy as jnp
        import numpy as np
        N_NODES = 6250
        N_EDGES = 100000
        IN_FEATS = 256
        OUT_FEATS = 256
        NUM_HEADS = 8
        FEATS_PER_HEAD = OUT_FEATS // NUM_HEADS
        LN_EPS = 1e-05
        N = feat.shape[0]
        mu = jnp.mean(feat, axis=-1, keepdims=True)
        var = jnp.var(feat, axis=-1, keepdims=True)
        h = (feat - mu) / jnp.sqrt(var + LN_EPS)
        feat_src = (h @ Wsrc.T + bsrc).reshape(N, NUM_HEADS, FEATS_PER_HEAD)
        feat_dst = (h @ Wdst.T + bdst).reshape(N, NUM_HEADS, FEATS_PER_HEAD)
        feat_val = (h @ Wval.T + bval).reshape(N, NUM_HEADS, FEATS_PER_HEAD)
        e = jax.nn.silu(feat_src[src] + feat_dst[dst])
        score = jnp.einsum('ehf,xhf->eh', e, attn)
        smax = jax.ops.segment_max(score, dst, num_segments=N)
        a = jnp.exp(score - smax[dst])
        denom = jax.ops.segment_sum(a, dst, num_segments=N)
        a = a / denom[dst]
        msg = feat_val[src] * a[:, :, None]
        h_upd = jax.ops.segment_sum(msg, dst, num_segments=N)
        h_upd = h_upd.reshape(N, OUT_FEATS)
        h_upd = h_upd + h
        return jax.nn.silu(h_upd)

    def _L0_ffn_ref(x, gate_w, gate_b, w1, b1, w2, b2, gamma, beta):
        import jax, jax.numpy as jnp
        import numpy as np
        B, S, H, F, E, K = (8, 512, 256, 512, 16, 2)
        EPS = 1e-05
        gate_logits = x @ gate_w + gate_b
        topk_vals, topk_idx = jax.lax.top_k(gate_logits, K)
        topk_w = jax.nn.softmax(topk_vals, axis=-1)
        h = jax.nn.relu(jnp.einsum('bsh,ehf->bsef', x, w1) + b1)
        expert_out = jnp.einsum('bsef,efh->bseh', h, w2) + b2
        sel = jnp.take_along_axis(expert_out, topk_idx[:, :, :, None], axis=2)
        moe = jnp.sum(topk_w[..., None] * sel, axis=2)
        y = x + moe
        mu = jnp.mean(y, axis=-1, keepdims=True)
        var = jnp.var(y, axis=-1, keepdims=True)
        return (y - mu) / jnp.sqrt(var + EPS) * gamma + beta
    x = x + _L0_gnn_ref(_layernorm(x, axis=-1), L0_gnn_Wsrc, L0_gnn_bsrc, L0_gnn_Wdst, L0_gnn_bdst, L0_gnn_Wval, L0_gnn_bval, L0_gnn_attn, src, dst)
    x = x + _L0_ffn_ref(_layernorm(x, axis=-1)[None], L0_ffn_gate_w, L0_ffn_gate_b, L0_ffn_w1, L0_ffn_b1, L0_ffn_w2, L0_ffn_b2, L0_ffn_gamma, L0_ffn_beta)[0]
    return x

_drawn_inputs = setup_inputs


def setup_inputs(seed=0):
    import zlib

    import numpy as np

    out = dict(_drawn_inputs(seed))
    spreads = {'L0_gnn_bsrc': (0.0, 0.8),
     'L0_gnn_bdst': (0.0, 0.8),
     'L0_gnn_bval': (0.0, 0.1),
     'L0_ffn_gate_b': (0.0, 0.294),
     'L0_ffn_b1': (0.0, 0.8),
     'L0_ffn_b2': (0.0, 0.278),
     'L0_ffn_gamma': (1.0, 0.2),
     'L0_ffn_beta': (0.0, 0.1)}
    factors = {}
    for name, (base, spread) in spreads.items():
        noise = np.random.default_rng([zlib.crc32(name.encode()), seed]).standard_normal(out[name].shape)
        drawn = base * np.exp(spread * noise) if base else spread * noise
        out[name] = jnp.asarray(drawn.astype(out[name].dtype))
    for name, factor in factors.items():
        out[name] = (out[name] * factor).astype(out[name].dtype)
    return out
```

```python
from contextlib import ExitStack

import concourse.bass as bass
from concourse import mybir

F32 = mybir.dt.float32
BF16 = mybir.dt.bfloat16
I32 = mybir.dt.int32
U32 = mybir.dt.uint32
ALU = mybir.AluOpType
ACT = mybir.ActivationFunctionType
AX = mybir.AxisListType

P = 128
BIG = 1e38
EPS = 1e-5


def build_gnn_moe(nc, x, src, dst, Wsrc, bsrc, Wdst, bdst, Wval, bval, attn,
                  gate_w, gate_b, w1, b1, w2, b2, gamma, beta, out):
    N, D = x.shape
    E = src.shape[0]
    H = attn.shape[1]
    FH = D // H
    NE, _, F = w1.shape
    KB = D // P
    FB = F // P

    NT = -(-N // P)
    LAST = N - (NT - 1) * P
    J = 7
    COLS = -(-E // (P * 2 * J)) * 2 * J
    GROUPS = COLS // J
    REC = D + 2 * H
    ACC = D + H
    M1 = J + 1
    TB = 7
    NBATCH = NT // TB
    S2 = 2 * NT
    MT = 2 * (-(-(2 * NT * P + NE * (P - 1)) // (2 * P)))
    assert NT == TB * NBATCH and (NT - 3) % 2 == 0 and COLS % (2 * J) == 0 and D == 256 and F == 512

    with ExitStack() as ctx:
        def sb(name, shape, dt=F32):
            return ctx.enter_context(nc.sbuf_tensor(name, shape, dt))

        def sem(name):
            return ctx.enter_context(nc.semaphore(name))

        def dram(name, shape, dt=F32):
            return nc.dram_tensor(name, shape, dt, kind="Internal").ap()

        sv_table = dram("sv_table", [NT * P, 2 * D])
        d_table = dram("d_table", [NT * P, D])
        records = dram("records", [COLS * P, REC])
        lane_tails = dram("lane_tails", [P + 1, REC])
        expert_in = dram("expert_in", [MT * P, D])
        expert_out = dram("expert_out", [MT * P, D])

        node_x = sb("node_x", [P, NT, D])
        node_h = sb("node_h", [P, NT, D])

        src_all = sb("src_all", [P, COLS + 2 * J], I32)
        dst_all = sb("dst_all", [P, COLS + 2 * J], I32)
        same = sb("same", [P, COLS])
        dst_low = sb("dst_low", [P, COLS], BF16)
        dst_high = sb("dst_high", [P, COLS], BF16)
        idx_src = [sb(f"idx_src{b}", [P, J], I32) for b in range(2)]
        idx_dst = [sb(f"idx_dst{b}", [P, J], I32) for b in range(2)]

        sv = [sb(f"sv{b}", [P, J, 2 * D]) for b in range(2)]
        fd = [sb(f"fd{b}", [P, J, D]) for b in range(2)]
        th = sb("th", [P, J, D])
        msg = sb("msg", [P, J, ACC])
        rec = [sb(f"rec{b}", [P, J, REC]) for b in range(2)]
        carry = sb("carry", [P, ACC])
        hot_low = [sb(f"hot_low{b}", [P, J, P], BF16) for b in range(2)]
        hot_high = [sb(f"hot_high{b}", [P, J, NT], BF16) for b in range(2)]
        seg_mask = sb("seg_mask", [P, H * M1 + 1])
        score = sb("score", [P, H, M1])
        fmax = sb("fmax", [P, H * M1])
        smax = sb("smax", [P, H, M1])
        diff = sb("diff", [P, H, M1])
        wgt = sb("wgt", [P, H, M1])

        ident = sb("ident", [P, P])
        iota_p = sb("iota_p", [P, 1])
        iota_f = sb("iota_f", [P, P])
        iota_bf = sb("iota_bf", [P, P], BF16)
        attn_half = sb("attn_half", [P, D])
        stats = sb("stats", [P, NT, 6])
        mv = sb("mv", [P, NT, 2])
        rstd = sb("rstd", [P, NT])
        sd = sb("sd", [P, NT])
        ones_bf = sb("ones_bf", [P, P], BF16)
        before_bf = sb("before_bf", [P, P], BF16)
        upper = sb("upper", [P, P])
        ones = sb("ones", [P, P])
        head_of = sb("head_of", [H, D])
        prev_dst = sb("prev_dst", [P, 1], I32)
        chain = sb("chain", [P, 1])
        nflag = sb("nflag", [P, 8, NT])
        idx_last = sb("idx_last", [P, NT], I32)
        idx_tail = sb("idx_tail", [P, NT], I32)
        top_w = sb("top_w", [P, 2, NT])
        slot = sb("slot", [P, S2], I32)
        tile_expert = sb("tile_expert", [P, MT], I32)
        b1_of = sb("b1_of", [P, FB, MT])
        epsc = sb("epsc", [P, 1])

        bank = [ctx.enter_context(nc.psum_tensor(f"bank{k}", [P, 512], F32)) for k in range(8)]

        sv0f = sv[0][:, :, :].rearrange("p a b -> p (a b)")
        sv1f = sv[1][:, :, :].rearrange("p a b -> p (a b)")
        thf = th[:, :, :].rearrange("p a b -> p (a b)")
        wT = sv0f[:, 0:KB * 3 * D].rearrange("p (k o) -> p k o", k=KB)
        w_raw = sv0f[:, KB * 3 * D:2 * KB * 3 * D].rearrange("p (m k) -> p m k", k=D)
        bias3 = sv1f[:, 2048:2048 + 3 * D]
        stage = [sv1f[:, 768 * b:768 * b + 768] for b in range(2)]
        hT = [sv1f[:, 1536 + 256 * b:1792 + 256 * b].rearrange("p (k c) -> p k c", k=KB) for b in range(2)]

        h_row = [sv1f[:, 2816 + 256 * b:3072 + 256 * b] for b in range(2)]
        tailT = fd[0][:, :, :].rearrange("p a b -> p (a b)")
        aT = tailT[:, 0:KB * P].rearrange("p (k l) -> p k l", k=KB)
        mT = tailT[0:H, 256:384]
        dT = tailT[0:H, 384:512]
        chainT = tailT[:, 512:640]
        lane_mask = tailT[:, 640:768]
        lane_max = tailT[0:H, 768:896]
        lane_exp = tailT[0:H, 896:1152]
        lane_den = tailT[0:H, 1152:1280]
        chain_wide = tailT[:, 1280:1408]
        accT = fd[1][:, 0, :].rearrange("p (k l) -> p k l", k=KB)
        tail_sb = msg[:, :, :].rearrange("p a b -> p (a b)")[:, 0:REC]
        no_tail = msg[:, :, :].rearrange("p a b -> p (a b)")[0:1, REC:2 * REC]
        node_rec = [sv0f[:, 0:TB * REC].rearrange("p (a b) -> p a b", a=TB),
                    sv1f[:, 0:TB * REC].rearrange("p (a b) -> p a b", a=TB)]
        node_car = rec
        u_sb = fd[0]
        moves = sv0f[:, 1904:2016].rearrange("p (a b) -> p a b", a=TB)
        moved = sv0f[:, 2016:2128].rearrange("p (a b) -> p a b", a=TB)
        nmax = sv0f[:, 2128:2184].rearrange("p (a b) -> p a b", a=TB)
        nden = sv0f[:, 2184:2240].rearrange("p (a b) -> p a b", a=TB)

        flat = lambda t: t[:, :, :].rearrange("p a b -> p (a b)")
        fd0f, fd1f, msgf, rec0f, rec1f = flat(fd[0]), flat(fd[1]), flat(msg), flat(rec[0]), flat(rec[1])
        W = NE * S2
        chosen = fd0f[:, 0:W].rearrange("p (e s) -> p e s", e=NE)
        taken = fd1f[:, 0:W]
        running = thf[:, 0:W]
        place = sv0f[:, 0:W]
        restart = sv0f[:, W:2 * W]
        chosen_bf = rec0f[:, 0:W // 2].bitcast(BF16)
        logits = sv1f[:, 0:NT * NE].rearrange("p (t e) -> p t e", t=NT)
        top8 = msgf[:, 0:8 * NT].rearrange("p (t e) -> p t e", t=NT)
        top8_at = msgf[:, 8 * NT:16 * NT].bitcast(U32).rearrange("p (t e) -> p t e", t=NT)
        choice = msgf[:, 16 * NT:18 * NT].rearrange("p (k t) -> p k t", k=2)
        gate_w_sb = msgf[:, 1000:1000 + KB * NE].rearrange("p (k e) -> p k e", k=KB)
        gate_b_sb = msgf[:, 1032:1048]
        ends = msgf[:, 1050:1050 + 5 * NE].rearrange("p (k e) -> p k e", k=5)
        tile_of = msgf[:, 1140:1140 + MT]
        e_hot = msgf[0:NE, 1260:1260 + MT]
        b1_sb = rec0f[0:NE, 784:784 + F]
        b2_sb = rec0f[0:NE, 1296:1296 + D]
        share = rec1f[:, 0:NT * NE].rearrange("p (t e) -> p t e", t=NT)
        gamma_sb = rec1f[:, 784:784 + D]
        beta_sb = rec1f[:, 1040:1040 + D]
        share_t = rec1f[0:NE, 1296:1296 + 2 * P].rearrange("p (s c) -> p s c", s=2)
        w1_sb = [sv0f[:, 1024 * b:1024 * b + 1024].rearrange("p (k f) -> p k f", k=KB) for b in range(2)]
        w2_sb = [sv1f[:, 1024 * b:1024 * b + 1024].rearrange("p (k f) -> p k f", k=FB) for b in range(2)]
        tok = [sv0f[:, 2048 + 256 * b:2304 + 256 * b] for b in range(2)]
        tokT = [sv0f[:, 2560 + 256 * b:2816 + 256 * b].rearrange("p (k c) -> p k c", k=KB) for b in range(2)]
        hidT = [sv1f[:, 2048 + 512 * b:2560 + 512 * b].rearrange("p (k c) -> p k c", k=FB) for b in range(2)]
        eout = [thf[:, 256 * b:256 * b + 256] for b in range(2)]
        got = [[sv[b][:, :, :].rearrange("p a b -> p (a b)")[:, 1792 * k:1792 * (k + 1)].rearrange("p (t d) -> p t d", t=TB)
                for k in range(2)] for b in range(2)]

        block = ctx.enter_context(nc.Block())

        x_loaded = sem("x_loaded")
        x_padded = sem("x_padded")
        edges_padded = sem("edges_padded")
        edges_loaded = sem("edges_loaded")
        consts_loaded = sem("consts_loaded")
        consts_made = sem("consts_made")
        zeros_made = sem("zeros_made")
        zeros_stored = sem("zeros_stored")
        w_turned = sem("w_turned")
        w_kept = sem("w_kept")
        var_ready = sem("var_ready")
        sd_ready = sem("sd_ready")
        h_normed = sem("h_normed")
        row_ready = sem("row_ready")
        h_turned = sem("h_turned")
        hT_ready = sem("hT_ready")
        projected = sem("projected")
        stage_ready = sem("stage_ready")
        stage_stored = [sem(f"stage_stored{b}") for b in range(2)]
        p0 = sem("p0_vector_done")
        e0 = sem("edge_vector_done")

        idx_ready = sem("idx_ready")
        prev_set = sem("prev_set")
        prev_loaded = sem("prev_loaded")
        chain_ready = sem("chain_ready")
        tails_turned = sem("tails_turned")
        tails_kept = sem("tails_kept")
        lane_moves = sem("lane_moves")
        lane_moved = sem("lane_moved")
        lane_factors = sem("lane_factors")
        factors_wide = sem("factors_wide")
        lanes_summed = sem("lanes_summed")
        tails_back = sem("tails_back")
        tail_ready = sem("tail_ready")
        tail_stored = sem("tail_stored")
        counted = sem("counted")
        degrees_kept = sem("degrees_kept")
        degrees_summed = sem("degrees_summed")
        node_idx_ready = sem("node_idx_ready")
        node_gathered = [sem(f"node_gathered{b}") for b in range(2)]
        node_used = sem("node_used")
        moves_ready = sem("moves_ready")
        moved_ready = sem("moved_ready")
        u_ready = sem("u_ready")
        u_tanh = sem("u_tanh")
        x2_ready = sem("x2_ready")
        p1 = sem("p1_vector_done")
        ffn_loaded = sem("ffn_loaded")
        y_row = sem("y_row")
        y_turned = sem("y_turned")
        yT_ready = sem("yT_ready")
        gated = sem("gated")
        logits_ready = sem("logits_ready")
        y_ready = sem("y_ready")
        gap_ready = sem("gap_ready")
        gap_exp = sem("gap_exp")
        chosen_ready = sem("chosen_ready")
        tile_sums = sem("tile_sums")
        tile_sums_kept = sem("tile_sums_kept")
        ranks = sem("ranks")
        slot_ready = sem("slot_ready")
        e_hot_ready = sem("e_hot_ready")
        b1_turned = sem("b1_turned")
        routing_done = sem("routing_done")
        tokens_sent = sem("tokens_sent")
        tok_loaded = [sem(f"tok_loaded{b}") for b in range(2)]
        w1_loaded = [sem(f"w1_loaded{b}") for b in range(2)]
        w2_loaded = [sem(f"w2_loaded{b}") for b in range(2)]
        tok_turned = sem("tok_turned")
        tokT_ready = sem("tokT_ready")
        hidden = sem("hidden")
        hidT_ready = sem("hidT_ready")
        expert_done = sem("expert_done")
        eout_ready = sem("eout_ready")
        eout_stored = [sem(f"eout_stored{b}") for b in range(2)]
        out_gathered = [sem(f"out_gathered{b}") for b in range(2)]
        got_used = sem("got_used")
        share_turned = sem("share_turned")
        share_kept = sem("share_kept")
        b2_ready = sem("b2_ready")
        y_var = sem("y_var")
        y_sd = sem("y_sd")
        out_ready = sem("out_ready")
        out_stored = [sem(f"out_stored{b}") for b in range(2)]
        p2 = sem("p2_vector_done")
        gathers_issued = sem("gathers_issued")
        gathered = [sem(f"gathered{b}") for b in range(2)]
        z_ready = sem("z_ready")
        tanh_ready = sem("tanh_ready")
        diff_ready = sem("diff_ready")
        wgt_ready = sem("wgt_ready")
        side_ready = sem("side_ready")
        msg_used = sem("msg_used")
        rec_ready = sem("rec_ready")
        rec_stored = [sem(f"rec_stored{b}") for b in range(2)]
        hot_ready = sem("hot_ready")
        hot_used = sem("hot_used")

        def node_tiles(eng, step):
            for t in range(3):
                step(t, t % 2, t >= 2)
            with eng.Fori(0, (NT - 3) // 2) as i:
                for k in range(2):
                    step(i * 2 + (3 + k), (3 + k) % 2, True)

        def expert_tiles(eng, step):
            for i in range(2):
                step(i, i, False, False)
            with eng.Fori(1, MT // 2 - 1) as p:
                for b in range(2):
                    step(p * 2 + b, b, True, False)
            for i in (MT - 2, MT - 1):
                step(i, i % 2, True, i == MT - 1)

        def edge_groups(eng, step):
            for b in range(2):
                step(0, b, True)
            with eng.Fori(1, GROUPS // 2) as i:
                for b in range(2):
                    step(i, b, False)

        @block.sync
        def _(sp):
            sp.wait_ge(x_padded, 1)
            for c in range(8):
                sp.dma_start(node_x[:, 6 * c:6 * c + 6, :],
                             x[768 * c:768 * c + 768, :].rearrange("(t p) d -> p t d", p=P)).then_inc(x_loaded, 16)
            sp.dma_start(node_x[0:LAST, NT - 1, :], x[(NT - 1) * P:N, :]).then_inc(x_loaded, 16)
            for m, W in enumerate((Wsrc, Wval, Wdst)):
                sp.dma_start(w_raw[:, 2 * m:2 * m + 2, :],
                             W.rearrange("(o p) k -> p o k", p=P)).then_inc(consts_loaded, 16)
            for m, bb in enumerate((bsrc, bval, bdst)):
                sp.dma_start(bias3[:, m * D:(m + 1) * D],
                             bb.rearrange("(a d) -> a d", a=1).to_broadcast([P, D])).then_inc(consts_loaded, 16)
            sp.dma_start(attn_half[:, :], attn.rearrange("a h f -> a (h f)").to_broadcast([P, D])).then_inc(consts_loaded, 16)
            sp.wait_ge(prev_set, 1)
            sp.dma_start(prev_dst[1:P, :], dst[0:(P - 1) * COLS].rearrange("(p j) -> p j", j=COLS)[:, COLS - 1:COLS],
                         allow_slow_non_contiguous=True).then_inc(prev_loaded, 16)
            sp.wait_ge(edges_padded, 2)
            full = E // COLS
            for arr, t in ((src, src_all), (dst, dst_all)):
                for a, z in ((0, 112), (112, full)):
                    sp.dma_start(t[a:z, 0:COLS], arr[a * COLS:z * COLS].rearrange("(p j) -> p j", j=COLS)).then_inc(edges_loaded, 16)
                sp.dma_start(t[full:full + 1, 0:E - full * COLS],
                             arr[full * COLS:E].rearrange("(p j) -> p j", p=1)).then_inc(edges_loaded, 16)
            sp.wait_ge(zeros_made, 1)
            zw = MT * D // 19
            sp.dma_start(expert_in.rearrange("(p r) d -> p (r d)", p=P).rearrange("p (a b) -> p a b", b=zw),
                         thf[:, 0:zw].unsqueeze(1).to_broadcast([P, 19, zw])).then_inc(zeros_stored, 16)

            def store_tile(t, s, again):
                sp.wait_ge(stage_ready, t + 1)
                sp.dma_start(sv_table[bass.ds(t * P, P), :], stage[s][:, 0:2 * D]).then_inc(stage_stored[s], 16)
                sp.dma_start(d_table[bass.ds(t * P, P), :], stage[s][:, 2 * D:3 * D]).then_inc(stage_stored[s], 16)
            node_tiles(sp, store_tile)

            rv = records.rearrange("(p j) r -> p j r", p=P)

            def store_group(i, b, first):
                sp.wait_ge(side_ready, i * 2 + (b + 1))
                sp.wait_ge(rec_ready, i * 2 + (b + 1))
                sp.dma_start(rv[:, bass.ds(i * (2 * J) + b * J, J), :], rec[b][:, :, :]).then_inc(rec_stored[b], 16)
            edge_groups(sp, store_group)
            for b in range(2):
                sp.wait_ge(rec_stored[b], 16 * (GROUPS // 2))
            sp.wait_ge(tail_ready, 2)
            sp.dma_start(lane_tails[0:P, :], tail_sb).then_inc(tail_stored, 16)
            sp.dma_start(lane_tails[P:P + 1, :], no_tail).then_inc(tail_stored, 16)
            sp.wait_ge(x2_ready, NBATCH)
            sp.dma_start(gate_w_sb, gate_w.rearrange("(k p) e -> p k e", p=P)).then_inc(ffn_loaded, 16)
            sp.dma_start(gate_b_sb, gate_b.rearrange("(a e) -> a e", a=1).to_broadcast([P, NE])).then_inc(ffn_loaded, 16)
            sp.dma_start(gamma_sb, gamma.rearrange("(a e) -> a e", a=1).to_broadcast([P, D])).then_inc(ffn_loaded, 16)
            sp.dma_start(beta_sb, beta.rearrange("(a e) -> a e", a=1).to_broadcast([P, D])).then_inc(ffn_loaded, 16)
            sp.dma_start(b1_sb, b1).then_inc(ffn_loaded, 16)
            sp.dma_start(b2_sb, b2).then_inc(ffn_loaded, 16)

            sp.wait_ge(routing_done, 1)
            sp.wait_ge(tokens_sent, 16 * S2)

            def load_tok(i, b, again):
                if again:
                    sp.wait_ge(tok_turned, i - 1)
                sp.dma_start(tok[b], expert_in[bass.ds(i * P, P), :]).then_inc(tok_loaded[b], 16)

            def store_eout(i, b):
                sp.wait_ge(eout_ready, i + 1)
                sp.dma_start(expert_out[bass.ds(i * P, P), :], eout[b]).then_inc(eout_stored[b], 16)

            load_tok(0, 0, False)

            def load_expert(i, b, again, last):
                if not last:
                    load_tok(i + 1, 1 - b, again or (b == 1))
                e = sp.value_load(tile_expert[0:1, bass.ds(i, 1)], min_val=0, max_val=NE - 1)
                if again:
                    sp.wait_ge(hidden, i - 1)
                sp.dma_start(w1_sb[b].unsqueeze(1), w1[bass.ds(e, 1), :, :].rearrange("a (k p) f -> p a k f", p=P)).then_inc(w1_loaded[b], 16)
                if again:
                    sp.wait_ge(expert_done, i - 1)
                sp.dma_start(w2_sb[b].unsqueeze(1), w2[bass.ds(e, 1), :, :].rearrange("a (k p) f -> p a k f", p=P)).then_inc(w2_loaded[b], 16)
                if again:
                    store_eout(i - 2, b)
            expert_tiles(sp, load_expert)
            store_eout(MT - 2, 0)
            store_eout(MT - 1, 1)

            for c in range(NBATCH):
                sp.wait_ge(out_ready, c + 1)
                full = min(TB, (N - c * TB * P) // P)
                sp.dma_start(out[c * TB * P:(c * TB + full) * P, :].rearrange("(t p) d -> p t d", p=P),
                             got[c % 2][0][:, 0:full, :]).then_inc(out_stored[c % 2], 16)
                if full < TB:
                    sp.dma_start(out[(NT - 1) * P:N, :], got[c % 2][0][0:LAST, full, :]).then_inc(out_stored[c % 2], 16)
            sp.wait_ge(out_stored[0], 16 * ((NBATCH + 1) // 2 + 1))
            sp.wait_ge(out_stored[1], 16 * (NBATCH // 2))

        @block.gpsimd
        def _(pool):
            pool.memset(node_x[:, NT - 1, :], 0.0).then_inc(x_padded, 1)
            pool.memset(src_all[:, COLS - 352:], 0).then_inc(edges_padded, 1)
            pool.memset(dst_all[:, COLS - 352:], N).then_inc(edges_padded, 1)
            pool.memset(thf, 0.0).then_inc(zeros_made, 1)
            pool.memset(ident[:, :], 0.0).then_inc(consts_made, 1)
            pool.iota(iota_f[:, :], pattern=[[1, P]], base=0, channel_multiplier=0,
                      allow_small_or_imprecise_dtypes=True).then_inc(consts_made, 1)
            pool.iota(iota_p[:, :], pattern=[[1, 1]], base=0, channel_multiplier=1,
                      allow_small_or_imprecise_dtypes=True).then_inc(consts_made, 1)
            pool.memset(epsc[:, :], EPS).then_inc(consts_made, 1)
            pool.memset(upper[:, :], 1.0).then_inc(consts_made, 1)
            pool.memset(ones[:, :], 1.0).then_inc(consts_made, 1)
            pool.memset(head_of[:, :], 1.0).then_inc(consts_made, 1)
            pool.memset(prev_dst[:, :], -1).then_inc(prev_set, 1)
            pool.wait_ge(consts_made, 7)
            pool.affine_select(out=upper[:, :], in_=upper[:, :], compare_op=ALU.is_ge, fill=0.0,
                               base=0, pattern=[[1, P]], channel_multiplier=-1).then_inc(consts_made, 1)
            pool.affine_select(out=head_of[:, :], in_=head_of[:, :], compare_op=ALU.is_ge, fill=0.0,
                               base=0, pattern=[[1, D]], channel_multiplier=-FH).then_inc(consts_made, 1)
            pool.wait_ge(consts_made, 9)
            pool.affine_select(out=head_of[:, :], in_=head_of[:, :], compare_op=ALU.is_ge, fill=0.0,
                               base=FH - 1, pattern=[[-1, D]], channel_multiplier=FH).then_inc(consts_made, 1)
            pool.affine_select(out=ident[:, :], in_=ident[:, :], compare_op=ALU.not_equal, fill=1.0,
                               base=0, pattern=[[-1, P]], channel_multiplier=1).then_inc(consts_made, 1)
            pool.wait_ge(stage_stored[0], 16 * 2 * ((NT + 1) // 2))
            pool.wait_ge(stage_stored[1], 16 * 2 * (NT // 2))

            def gather_group(i, b, first):
                pool.wait_ge(idx_ready, i * 2 + (b + 1))
                pool.sem_inc(gathers_issued, 1)
                for j in range(J):
                    pool.indirect_dma_start(sv[b][:, j, :], None, sv_table,
                                            bass.IndirectOffsetOnAxis(idx_src[b][:, j:j + 1], 0)).then_inc(gathered[b], 16)
                    pool.indirect_dma_start(fd[b][:, j, :], None, d_table,
                                            bass.IndirectOffsetOnAxis(idx_dst[b][:, j:j + 1], 0)).then_inc(gathered[b], 16)
            edge_groups(pool, gather_group)
            pool.wait_ge(node_idx_ready, 2)
            for b in range(2):
                pool.wait_ge(rec_stored[b], 16 * (GROUPS // 2))
            pool.wait_ge(tail_stored, 32)
            for c in range(NBATCH):
                b = c % 2
                if c >= 2:
                    pool.wait_ge(node_used, c - 1)
                for k in range(TB):
                    t = c * TB + k
                    pool.indirect_dma_start(node_rec[b][:, k, :], None, records,
                                            bass.IndirectOffsetOnAxis(idx_last[:, t:t + 1], 0)).then_inc(node_gathered[b], 16)
                    pool.indirect_dma_start(node_car[b][:, k, :], None, lane_tails,
                                            bass.IndirectOffsetOnAxis(idx_tail[:, t:t + 1], 0)).then_inc(node_gathered[b], 16)
            pool.wait_ge(slot_ready, 1)
            pool.wait_ge(zeros_stored, 16)
            for s in range(S2):
                pool.indirect_dma_start(expert_in, bass.IndirectOffsetOnAxis(slot[:, s:s + 1], 0),
                                        node_h[:, s % NT, :], None).then_inc(tokens_sent, 16)
            for b in range(2):
                pool.wait_ge(eout_stored[b], 16 * (MT // 2))
            for c in range(NBATCH):
                b = c % 2
                if c >= 2:
                    pool.wait_ge(out_stored[b], 16 * (c // 2))
                for k in range(TB):
                    for h in range(2):
                        s = h * NT + c * TB + k
                        pool.indirect_dma_start(got[b][h][:, k, :], None, expert_out,
                                                bass.IndirectOffsetOnAxis(slot[:, s:s + 1], 0)).then_inc(out_gathered[b], 16)

        @block.tensor
        def _(pe):
            pe.wait_ge(consts_made, 11)
            pe.wait_ge(consts_loaded, 16 * 7)
            for m in range(3):
                for k in range(KB):
                    for o in range(2):
                        ins = pe.transpose(bank[2 * m + k][:, o * P:(o + 1) * P],
                                           w_raw[:, 2 * m + o, k * P:(k + 1) * P], ident[:, :])
                    ins.then_inc(w_turned, 1)
            pe.wait_ge(w_kept, 6)

            def project(t, s, again):
                if again:
                    pe.wait_ge(hT_ready, t - 1)
                pe.wait_ge(row_ready, t + 1)
                for k in range(KB):
                    ins = pe.transpose(bank[s][:, k * P:(k + 1) * P], h_row[s][:, k * P:(k + 1) * P], ident[:, :])
                ins.then_inc(h_turned, 1)
                pe.wait_ge(hT_ready, t + 1)
                if again:
                    pe.wait_ge(stage_ready, t - 1)
                for k in range(KB):
                    pe.matmul(bank[2 + 2 * s][:, :], hT[s][:, k, :], wT[:, k, 0:2 * D], start=(k == 0), stop=(k == KB - 1))
                for k in range(KB):
                    ins = pe.matmul(bank[3 + 2 * s][:, 0:D], hT[s][:, k, :], wT[:, k, 2 * D:3 * D],
                                    start=(k == 0), stop=(k == KB - 1))
                ins.then_inc(projected, 1)
            node_tiles(pe, project)

            def count_group(i, b, first):
                pe.wait_ge(hot_ready, i * 2 + (b + 1))
                for j in range(J):
                    ins = pe.matmul(bank[6][:, 0:NT], hot_low[b][:, j, :], hot_high[b][:, j, :],
                                    start=(first and b == 0 and j == 0), stop=False, skip_group_check=True)
                ins.then_inc(hot_used, 1)
            edge_groups(pe, count_group)
            pe.wait_ge(degrees_kept, 1)
            pe.matmul(bank[7][:, 0:NT], upper[:, :], nflag[:, 0, :], start=True, stop=True)
            pe.matmul(bank[7][:, 64:64 + NT], ones[:, :], nflag[:, 0, :], start=True, stop=True).then_inc(degrees_summed, 1)
            pe.wait_ge(rec_ready, GROUPS)
            pe.wait_ge(side_ready, GROUPS)
            pe.wait_ge(chain_ready, 1)
            tail = rec[1][:, J - 1, :]
            pe.transpose(bank[0][0:H, 0:P], tail[:, ACC:REC], ident[:, :])
            pe.transpose(bank[0][0:H, P:2 * P], tail[:, D:ACC], ident[:, :])
            pe.transpose(bank[0][:, 2 * P:3 * P], chain_wide, ident[:, :])
            for k in range(KB):
                ins = pe.transpose(bank[1][:, k * P:(k + 1) * P], tail[:, k * P:(k + 1) * P], ident[:, :])
            ins.then_inc(tails_turned, 1)
            pe.wait_ge(lane_factors, 1)
            for k in range(KB):
                ins = pe.matmul(bank[2 + k][:, 0:2 * P], head_of[:, k * P:(k + 1) * P], lane_exp, start=True, stop=True)
            ins.then_inc(factors_wide, 1)
            pe.wait_ge(lanes_summed, 1)
            for k in range(KB):
                pe.transpose(bank[4][:, k * P:(k + 1) * P], accT[:, k, :], ident[:, :])
            pe.transpose(bank[4][:, D:D + H], lane_den, ident[0:H, 0:H])
            pe.transpose(bank[4][:, ACC:REC], lane_max, ident[0:H, 0:H]).then_inc(tails_back, 1)
            pe.wait_ge(ffn_loaded, 16 * 6)

            def gate(t, s, again):
                if again:
                    pe.wait_ge(yT_ready, t - 1)
                pe.wait_ge(y_row, t + 1)
                for k in range(KB):
                    ins = pe.transpose(bank[s][:, k * P:(k + 1) * P], h_row[s][:, k * P:(k + 1) * P], ident[:, :])
                ins.then_inc(y_turned, 1)
                pe.wait_ge(yT_ready, t + 1)
                if again:
                    pe.wait_ge(logits_ready, t - 1)
                for k in range(KB):
                    ins = pe.matmul(bank[2 + s][:, 0:NE], hT[s][:, k, :], gate_w_sb[:, k, :], start=(k == 0), stop=(k == KB - 1))
                ins.then_inc(gated, 1)
            node_tiles(pe, gate)

            pe.wait_ge(chosen_ready, 1)
            q = W // 4
            for k in range(4):
                ins = pe.matmul(bank[k][:, 0:q], ones_bf[:, :], chosen_bf[:, k * q:(k + 1) * q], start=True, stop=True)
            ins.then_inc(tile_sums, 1)
            for k in range(4):
                ins = pe.matmul(bank[4 + k][:, 0:q], before_bf[:, :], chosen_bf[:, k * q:(k + 1) * q], start=True, stop=True)
            ins.then_inc(ranks, 1)
            pe.wait_ge(tile_sums_kept, 1)
            pe.wait_ge(e_hot_ready, 1)
            for k in range(FB):
                ins = pe.matmul(bank[0][:, k * MT:(k + 1) * MT], b1_sb[:, k * P:(k + 1) * P], e_hot, start=True, stop=True)
            ins.then_inc(b1_turned, 1)
            pe.wait_ge(routing_done, 1)

            def turn(i, b, again):
                if again:
                    pe.wait_ge(tokT_ready, i - 1)
                pe.wait_ge(tok_loaded[b], half16(i, b))
                for k in range(KB):
                    ins = pe.transpose(bank[b][:, k * P:(k + 1) * P], tok[b][:, k * P:(k + 1) * P], ident[:, :])
                ins.then_inc(tok_turned, 1)

            def half16(i, b):
                return (i - b) * 8 + 16

            def first_layer(i, b, again):
                pe.wait_ge(tokT_ready, i + 1)
                pe.wait_ge(w1_loaded[b], half16(i, b))
                if again:
                    pe.wait_ge(hidT_ready, i - 1)
                for f in range(FB):
                    for k in range(KB):
                        ins = pe.matmul(bank[2 + b][:, f * P:(f + 1) * P], w1_sb[b][:, k, f * P:(f + 1) * P],
                                        tokT[b][:, k, :], start=(k == 0), stop=(k == KB - 1))
                ins.then_inc(hidden, 1)

            def second_layer(i, b, again):
                pe.wait_ge(hidT_ready, i + 1)
                pe.wait_ge(w2_loaded[b], half16(i, b))
                if again:
                    pe.wait_ge(eout_ready, i - 1)
                for f in range(FB):
                    ins = pe.matmul(bank[4 + b][:, 0:D], hidT[b][:, f, :], w2_sb[b][:, f, :],
                                    start=(f == 0), stop=(f == FB - 1))
                ins.then_inc(expert_done, 1)

            turn(0, 0, False)

            def expert_step(i, b, again, last):
                if not last:
                    turn(i + 1, 1 - b, again or b == 1)
                first_layer(i, b, again)
                if again or b == 1:
                    second_layer(i - 1, 1 - b, PREV_AGAIN[0])
            PREV_AGAIN = [False]
            expert_step(0, 0, False, False)
            expert_step(1, 1, False, False)
            expert_step(2, 0, True, False)
            PREV_AGAIN[0] = True
            expert_step(3, 1, True, False)
            with pe.Fori(2, MT // 2 - 1) as p:
                for b in range(2):
                    expert_step(p * 2 + b, b, True, False)
            expert_step(MT - 2, 0, True, False)
            expert_step(MT - 1, 1, True, True)
            second_layer(MT - 1, 1, True)

            for t in range(NT):
                s = t % 2
                if t >= 2:
                    pe.wait_ge(share_kept, t - 1)
                pe.transpose(bank[s][0:NE, 0:P], share[:, t, :], ident[:, :]).then_inc(share_turned, 1)
                pe.wait_ge(share_kept, t + 1)
                if t >= 2:
                    pe.wait_ge(got_used, t - 1)
                pe.matmul(bank[2 + s][:, 0:D], share_t[:, s, :], b2_sb, start=True, stop=True).then_inc(b2_ready, 1)

        @block.scalar
        def _(act):
            for n in range(6):
                m, k = n // 2, n % 2
                act.wait_ge(w_turned, n + 1)
                act.copy(wT[:, k, m * D:(m + 1) * D], bank[n][:, 0:D]).then_inc(w_kept, 1)
            for n in range(2):
                act.wait_ge(var_ready, n + 1)
                act.activation(sd[:, :], mv[:, :, 1], ACT.Sqrt, bias=epsc[:, 0:1]).then_inc(sd_ready, 1)

            def keep_hT(t, s, again):
                if again:
                    act.wait_ge(h_turned, t - 1)
                act.wait_ge(h_normed, t + 1)
                act.copy(h_row[s], node_h[:, t, :]).then_inc(row_ready, 1)
                if again:
                    act.wait_ge(projected, t - 1)
                act.wait_ge(h_turned, t + 1)
                act.copy(hT[s].rearrange("p k c -> p (k c)"), bank[s][:, 0:2 * P]).then_inc(hT_ready, 1)
            node_tiles(act, keep_hT)

            def edge_group(i, b, first):
                act.wait_ge(z_ready, i * 2 + (b + 1))
                act.activation(th[:, :, :], fd[b][:, :, :], ACT.Tanh, scale=0.5).then_inc(tanh_ready, 1)
                if not first:
                    act.wait_ge(rec_stored[b], i * 16)
                act.wait_ge(diff_ready, i * 2 + (b + 1))
                act.activation(wgt[:, :, :], diff[:, :, :], ACT.Exp).then_inc(wgt_ready, 1)
                act.copy(rec[b][:, :, ACC:REC].rearrange("p j h -> p h j"), smax[:, :, 1:M1]).then_inc(side_ready, 1)
            edge_groups(act, edge_group)
            act.wait_ge(lane_moves, 1)
            act.activation(lane_exp, lane_exp, ACT.Exp).then_inc(lane_moved, 1)
            for c in range(NBATCH):
                act.wait_ge(moves_ready, c + 1)
                act.activation(moved, moves, ACT.Exp).then_inc(moved_ready, 1)
                act.wait_ge(u_ready, c + 1)
                act.activation(th[:, :, :], u_sb[:, :, :], ACT.Tanh, scale=0.5).then_inc(u_tanh, 1)
            act.wait_ge(var_ready, 3)
            act.activation(sd[:, :], mv[:, :, 1], ACT.Sqrt, bias=epsc[:, 0:1]).then_inc(sd_ready, 1)

            def keep_yT(t, s, again):
                if again:
                    act.wait_ge(y_turned, t - 1)
                act.wait_ge(y_ready, t + 1)
                act.copy(h_row[s], node_h[:, t, :]).then_inc(y_row, 1)
                if again:
                    act.wait_ge(gated, t - 1)
                act.wait_ge(y_turned, t + 1)
                act.copy(hT[s].rearrange("p k c -> p (k c)"), bank[s][:, 0:2 * P]).then_inc(yT_ready, 1)
            node_tiles(act, keep_yT)
            act.wait_ge(gap_ready, 1)
            act.activation(top_w[:, 1, :], top_w[:, 1, :], ACT.Exp).then_inc(gap_exp, 1)
            act.wait_ge(routing_done, 1)

            def keep_tokT(i, b, again):
                if again:
                    act.wait_ge(hidden, i - 1)
                act.wait_ge(tok_turned, i + 1)
                act.copy(tokT[b].rearrange("p k c -> p (k c)"), bank[b][:, 0:2 * P]).then_inc(tokT_ready, 1)

            keep_tokT(0, 0, False)

            def act_step(i, b, again, last):
                if not last:
                    keep_tokT(i + 1, 1 - b, again or b == 1)
                act.wait_ge(hidden, i + 1)
                if again:
                    act.wait_ge(expert_done, i - 1)
                for f in range(FB):
                    ins = act.activation(hidT[b][:, f, :], bank[2 + b][:, f * P:(f + 1) * P], ACT.Relu,
                                         bias=b1_of[:, f, bass.ds(i, 1)])
                ins.then_inc(hidT_ready, 1)
            expert_tiles(act, act_step)

            for t in range(NT):
                s = t % 2
                if t >= 2:
                    act.wait_ge(b2_ready, t - 1)
                act.wait_ge(share_turned, t + 1)
                act.copy(share_t[:, s, :], bank[s][0:NE, 0:P]).then_inc(share_kept, 1)
                if t % TB == TB - 1:
                    c = t // TB
                    act.wait_ge(y_var, c + 1)
                    act.activation(sd[:, c * TB:(c + 1) * TB], mv[:, c * TB:(c + 1) * TB, 1], ACT.Sqrt,
                                   bias=epsc[:, 0:1]).then_inc(y_sd, 1)

        @block.vector
        def _(dve):
            n0 = [0]

            def link(ins):
                n0[0] += 1
                ins.then_inc(p0, 1)
                dve.wait_ge(p0, n0[0])

            dve.wait_ge(x_loaded, 16 * 9)

            def tile_stats(v, i):
                for k in range(TB):
                    ins = dve.bn_stats(stats[:, i * TB + k, :], v[:, i * TB + k, :])
                link(ins)
                for k in range(TB):
                    ins = dve.bn_aggr(mv[:, i * TB + k, :], stats[:, i * TB + k, :])
                return ins

            for i in range(NBATCH):
                ins = tile_stats(node_x, i)
            ins.then_inc(var_ready, 1)
            dve.wait_ge(sd_ready, 1)
            link(dve.reciprocal(rstd[:, :], sd[:, :]))
            for i in range(NBATCH):
                for t in range(i * TB, (i + 1) * TB):
                    ins = dve.tensor_scalar(node_h[:, t, :], node_x[:, t, :], mv[:, t, 0:1], rstd[:, t:t + 1],
                                            ALU.subtract, ALU.mult)
                link(ins)
                ins = tile_stats(node_h, i)
            ins.then_inc(var_ready, 1)
            dve.wait_ge(sd_ready, 2)
            link(dve.reciprocal(rstd[:, :], sd[:, :]))
            with dve.Fori(0, NT) as t:
                dve.tensor_scalar(node_h[:, t, :], node_h[:, t, :], mv[:, t, 0:1], rstd[:, bass.ds(t, 1)],
                                  ALU.subtract, ALU.mult).then_inc(h_normed, 1)
            dve.wait_ge(edges_loaded, 16 * 6)
            dve.wait_ge(zeros_stored, 16)
            link(dve.memset(same[:, 0:1], 0.0))
            link(dve.tensor_tensor(same[:, 1:COLS], dst_all[:, 1:COLS], dst_all[:, 0:COLS - 1], ALU.is_equal))
            low_i = thf[:, 0:COLS].bitcast(I32)
            link(dve.tensor_single_scalar(low_i, dst_all[:, 0:COLS], P - 1, op=ALU.bitwise_and))
            link(dve.tensor_copy(dst_low[:, :], low_i))
            link(dve.tensor_single_scalar(low_i, dst_all[:, 0:COLS], 7, op=ALU.arith_shift_right))
            link(dve.tensor_copy(dst_high[:, :], low_i))
            dve.wait_ge(consts_made, 11)
            link(dve.tensor_copy(iota_bf[:, :], iota_f[:, :]))
            dve.wait_ge(consts_loaded, 16 * 7)
            link(dve.tensor_scalar(attn_half[:, :], attn_half[:, :], 0.5, None, ALU.mult))
            link(dve.memset(seg_mask[:, :], -BIG))
            link(dve.memset(smax[:, :, :], 0.0))
            link(dve.memset(rec[1][:, :, :], 0.0))

            dve.wait_ge(prev_loaded, 16)
            dve.tensor_tensor(nflag[:, 1, 0:1], dst_all[:, 0:1], prev_dst[:, :], ALU.is_equal)
            link(dve.tensor_reduce(nflag[:, 2, 0:1], same[:, 1:COLS], AX.X, ALU.min))
            link(dve.tensor_tensor(chain[:, :], nflag[:, 1, 0:1], nflag[:, 2, 0:1], ALU.mult))

            def add_bias(t, s, again):
                dve.wait_ge(projected, t + 1)
                if again:
                    dve.wait_ge(stage_stored[s], half(t) * 32)
                dve.tensor_tensor(stage[s][:, 0:2 * D], bank[2 + 2 * s][:, :], bias3[:, 0:2 * D], ALU.add)
                dve.tensor_tensor(stage[s][:, 2 * D:3 * D], bank[3 + 2 * s][:, 0:D], bias3[:, 2 * D:3 * D],
                                  ALU.add).then_inc(stage_ready, 1)
            for t in range(3):
                half = lambda t: t // 2
                add_bias(t, t % 2, t >= 2)
            with dve.Fori(0, (NT - 3) // 2) as i:
                for k in range(2):
                    half = lambda t: i + (3 + k) // 2
                    add_bias(i * 2 + (3 + k), (3 + k) % 2, True)

            dve.wait_ge(stage_stored[0], 16 * 2 * ((NT + 1) // 2))
            dve.wait_ge(stage_stored[1], 16 * 2 * (NT // 2))
            for b in range(2):
                link(dve.tensor_copy(idx_src[b][:, :], src_all[:, b * J:(b + 1) * J]))
                dve.tensor_copy(idx_dst[b][:, :], dst_all[:, b * J:(b + 1) * J]).then_inc(idx_ready, 1)
            dve.wait_ge(idx_ready, 2)

            STEPS = 13 + J - 1

            def edge_group(i, b, first):
                g1 = i * 2 + (b + 1)
                col = i * (2 * J) + b * J
                n = [0]

                def mark(ins):
                    n[0] += 1
                    ins.then_inc(e0, 1)

                def done():
                    dve.wait_ge(e0, i * (2 * STEPS) + (b * STEPS + n[0]))

                dve.wait_ge(gathered[b], i * (16 * 2 * J) + 16 * 2 * J)
                dve.tensor_tensor(fd[b][:, :, :], fd[b][:, :, :], sv[b][:, :, 0:D], ALU.add).then_inc(z_ready, 1)
                mark(dve.tensor_scalar(seg_mask[:, 0:H * M1].rearrange("p (h j) -> p h j", h=H)[:, :, 1:M1],
                                       same[:, bass.ds(col, J)].unsqueeze(1).to_broadcast([P, H, J]),
                                       BIG, -BIG, ALU.mult, ALU.add))
                mark(dve.tensor_copy(score[:, :, 0:1], smax[:, :, J:M1]))
                if not first:
                    dve.wait_ge(hot_used, g1 - 2)
                mark(dve.tensor_tensor(hot_high[b][:, :, :],
                                       iota_bf[:, 0:NT].unsqueeze(1).to_broadcast([P, J, NT]),
                                       dst_high[:, bass.ds(col, J)].unsqueeze(2).to_broadcast([P, J, NT]), ALU.is_equal))
                dve.tensor_tensor(hot_low[b][:, :, :],
                                  iota_bf[:, :].unsqueeze(1).to_broadcast([P, J, P]),
                                  dst_low[:, bass.ds(col, J)].unsqueeze(2).to_broadcast([P, J, P]),
                                  ALU.is_equal).then_inc(hot_ready, 1)
                dve.wait_ge(z_ready, g1)
                mark(dve.tensor_tensor(sv[b][:, :, 0:D], fd[b][:, :, :],
                                       attn_half[:, :].unsqueeze(1).to_broadcast([P, J, D]), ALU.mult))
                done()
                dve.wait_ge(tanh_ready, g1)
                mark(dve.scalar_tensor_tensor(out=th[:, :, :], in0=th[:, :, :], scalar=1.0, in1=sv[b][:, :, 0:D],
                                              op0=ALU.add, op1=ALU.mult))
                done()
                mark(dve.tensor_reduce(score[:, :, 1:M1].rearrange("p h j -> p j h"),
                                       th[:, :, :].rearrange("p j (h f) -> p j h f", h=H), AX.X, ALU.add))
                done()
                mark(dve.tensor_tensor_scan(fmax[:, :], seg_mask[:, 0:H * M1],
                                            score[:, :, :].rearrange("p h j -> p (h j)"), 0.0, ALU.add, ALU.max))
                done()
                if not first or b:
                    dve.wait_ge(side_ready, g1 - 1)
                mark(dve.tensor_tensor_scan(smax[:, :, :].rearrange("p h j -> p (h j)")[:, ::-1],
                                            seg_mask[:, 1:H * M1 + 1][:, ::-1],
                                            fmax[:, ::-1], 0.0, ALU.add, ALU.max))
                done()
                dve.tensor_tensor(diff[:, :, :], score[:, :, :], smax[:, :, :], ALU.subtract).then_inc(diff_ready, 1)
                dve.wait_ge(wgt_ready, g1)
                mark(dve.tensor_tensor(msg[:, :, 0:D].rearrange("p j (h f) -> p j h f", h=H),
                                       sv[b][:, :, D:2 * D].rearrange("p j (h f) -> p j h f", h=H),
                                       wgt[:, :, 1:M1].rearrange("p h j -> p j h").unsqueeze(3).to_broadcast([P, J, H, FH]),
                                       ALU.mult))
                mark(dve.tensor_copy(msg[:, :, D:ACC], wgt[:, :, 1:M1].rearrange("p h j -> p j h")))
                mark(dve.tensor_tensor(carry[:, 0:D].rearrange("p (h f) -> p h f", h=H),
                                       rec[1 - b][:, J - 1, 0:D].rearrange("p (h f) -> p h f", h=H),
                                       wgt[:, :, 0:1].to_broadcast([P, H, FH]), ALU.mult))
                mark(dve.tensor_tensor(carry[:, D:ACC], rec[1 - b][:, J - 1, D:ACC],
                                       wgt[:, :, 0], ALU.mult))
                done()
                mark(dve.tensor_copy(idx_src[b][:, :], src_all[:, bass.ds(col + 2 * J, J)] if not first else
                                     src_all[:, (b + 2) * J:(b + 3) * J]))
                done()
                dve.tensor_copy(idx_dst[b][:, :], dst_all[:, bass.ds(col + 2 * J, J)] if not first else
                                dst_all[:, (b + 2) * J:(b + 3) * J]).then_inc(idx_ready, 1)
                if not first:
                    dve.wait_ge(rec_stored[b], i * 16)
                for j in range(J):
                    ins = dve.scalar_tensor_tensor(
                        out=rec[b][:, j, 0:ACC], in0=carry[:, :] if j == 0 else rec[b][:, j - 1, 0:ACC],
                        scalar=same[:, bass.ds(col + j, 1)] if not first else same[:, b * J + j:b * J + j + 1],
                        in1=msg[:, j, :], op0=ALU.mult, op1=ALU.add)
                    if j < J - 1:
                        mark(ins)
                        done()
                    else:
                        ins.then_inc(rec_ready, 1)
                        dve.wait_ge(rec_ready, g1)
                assert n[0] == STEPS, n[0]
            edge_groups(dve, edge_group)

            m0 = [0]

            def link1(ins):
                m0[0] += 1
                ins.then_inc(p1, 1)
                dve.wait_ge(p1, m0[0])

            deg, cum, tot, incl, start, last, lane, has = (nflag[:, k, :] for k in range(8))
            dve.wait_ge(hot_used, GROUPS)
            dve.tensor_copy(deg, bank[6][:, 0:NT]).then_inc(degrees_kept, 1)
            link1(dve.tensor_copy(chain_wide, chain[:, 0:1].to_broadcast([P, P])))
            dve.drain().then_inc(chain_ready, 1)
            dve.wait_ge(degrees_summed, 1)
            link1(dve.tensor_copy(tot, bank[7][:, 64:64 + NT]))
            link1(dve.tensor_tensor_scan(incl, ones[:, 0:NT], tot, 0.0, ALU.mult, ALU.add))
            link1(dve.tensor_tensor(cum, bank[7][:, 0:NT], incl, ALU.add))
            link1(dve.tensor_tensor(cum, cum, tot, ALU.subtract))
            link1(dve.tensor_tensor(start, cum, deg, ALU.subtract))
            link1(dve.tensor_scalar(last, cum, -1.0, 0.0, ALU.add, ALU.max))
            link1(dve.tensor_scalar(lane, last, 0.5, 1.0 / COLS, ALU.add, ALU.mult))
            link1(dve.tensor_scalar(lane, lane, -0.5, None, ALU.add))
            link1(dve.tensor_scalar(lane, lane, 8388608.0, None, ALU.add))
            link1(dve.tensor_scalar(lane, lane, -8388608.0, None, ALU.add))
            link1(dve.scalar_tensor_tensor(out=start, in0=lane, scalar=float(COLS), in1=start,
                                           op0=ALU.mult, op1=ALU.is_gt))
            link1(dve.tensor_scalar(lane, lane, -1.0 - P, None, ALU.add))
            link1(dve.tensor_tensor(lane, lane, start, ALU.mult))
            link1(dve.tensor_scalar(lane, lane, float(P), None, ALU.add))
            dve.tensor_copy(idx_last[:, :], last).then_inc(node_idx_ready, 1)
            dve.tensor_copy(idx_tail[:, :], lane).then_inc(node_idx_ready, 1)
            link1(dve.tensor_scalar(has, deg, 1.0, None, ALU.min))

            dve.wait_ge(tails_turned, 1)
            dve.tensor_copy(mT, bank[0][0:H, 0:P])
            dve.tensor_copy(dT, bank[0][0:H, P:2 * P])
            dve.tensor_copy(aT.rearrange("p k l -> p (k l)"), bank[1][:, 0:2 * P])
            link1(dve.tensor_copy(chainT, bank[0][:, 2 * P:3 * P]))
            link1(dve.tensor_scalar(lane_mask, chainT, BIG, -BIG, ALU.mult, ALU.add))
            link1(dve.tensor_tensor_scan(lane_max, lane_mask[0:H, :], mT, 0.0, ALU.add, ALU.max))
            dve.memset(lane_exp[:, P:P + 1], 0.0)
            dve.tensor_tensor(lane_exp[:, 0:P], mT, lane_max, ALU.subtract)
            link1(dve.tensor_tensor(lane_exp[:, P + 1:2 * P], lane_max[:, 0:P - 1], lane_max[:, 1:P], ALU.subtract))
            dve.tensor_scalar(lane_exp[:, P:2 * P], lane_exp[:, P:2 * P], 0.0, None, ALU.min).then_inc(lane_moves, 1)
            dve.wait_ge(lane_moved, 1)
            dve.tensor_tensor(lane_exp[:, P:2 * P], lane_exp[:, P:2 * P], chainT[0:H, :], ALU.mult).then_inc(lane_factors, 1)
            dve.wait_ge(lane_factors, 1)
            link1(dve.tensor_tensor(dT, dT, lane_exp[:, 0:P], ALU.mult))
            link1(dve.tensor_tensor_scan(lane_den, lane_exp[:, P:2 * P], dT, 0.0, ALU.mult, ALU.add))
            dve.wait_ge(factors_wide, 1)
            for k in range(KB):
                ins = dve.tensor_tensor(aT[:, k, :], aT[:, k, :], bank[2 + k][:, 0:P], ALU.mult)
            link1(ins)
            for k in range(KB):
                ins = dve.tensor_tensor_scan(accT[:, k, :], bank[2 + k][:, P:2 * P], aT[:, k, :], 0.0, ALU.mult, ALU.add)
            ins.then_inc(lanes_summed, 1)
            dve.wait_ge(tails_back, 1)
            dve.tensor_copy(tail_sb, bank[4][:, 0:REC]).then_inc(tail_ready, 1)
            link1(dve.memset(no_tail, 0.0))
            dve.memset(no_tail[:, ACC:REC], -BIG).then_inc(tail_ready, 1)
            dve.wait_ge(tail_ready, 2)

            for c in range(NBATCH):
                b = c % 2
                R, C = node_rec[b], node_car[b]
                tiles = slice(c * TB, (c + 1) * TB)
                dve.wait_ge(node_gathered[b], 16 * 2 * TB * (c // 2 + 1))
                link1(dve.tensor_tensor(nmax, R[:, :, ACC:REC], C[:, :, ACC:REC], ALU.max))
                dve.tensor_tensor(moves[:, :, 0:H], R[:, :, ACC:REC], nmax, ALU.subtract)
                dve.tensor_tensor(moves[:, :, H:2 * H], C[:, :, ACC:REC], nmax, ALU.subtract).then_inc(moves_ready, 1)
                dve.wait_ge(moved_ready, c + 1)
                dve.tensor_tensor(R[:, :, D:ACC], R[:, :, D:ACC], moved[:, :, 0:H], ALU.mult)
                link1(dve.tensor_tensor(C[:, :, D:ACC], C[:, :, D:ACC], moved[:, :, H:2 * H], ALU.mult))
                link1(dve.tensor_tensor(nden, R[:, :, D:ACC], C[:, :, D:ACC], ALU.add))
                link1(dve.reciprocal(nden, nden))
                link1(dve.tensor_tensor(nden, nden, has[:, tiles].unsqueeze(2).to_broadcast([P, TB, H]), ALU.mult))
                dve.tensor_tensor(moved[:, :, 0:H], moved[:, :, 0:H], nden, ALU.mult)
                link1(dve.tensor_tensor(moved[:, :, H:2 * H], moved[:, :, H:2 * H], nden, ALU.mult))
                for part, fac in ((R, moved[:, :, 0:H]), (C, moved[:, :, H:2 * H])):
                    v = part[:, :, 0:D].rearrange("p t (h f) -> p t h f", h=H)
                    ins = dve.tensor_tensor(v, v, fac.unsqueeze(3).to_broadcast([P, TB, H, FH]), ALU.mult)
                link1(ins)
                dve.tensor_tensor(u_sb[:, :, :], R[:, :, 0:D], C[:, :, 0:D], ALU.add).then_inc(node_used, 1)
                dve.wait_ge(node_used, c + 1)
                dve.tensor_tensor(u_sb[:, :, :], u_sb[:, :, :], node_h[:, tiles, :], ALU.add).then_inc(u_ready, 1)
                dve.wait_ge(u_tanh, c + 1)
                link1(dve.scalar_tensor_tensor(out=th[:, :, :], in0=th[:, :, :], scalar=1.0, in1=u_sb[:, :, :],
                                               op0=ALU.add, op1=ALU.mult))
                dve.scalar_tensor_tensor(out=node_x[:, tiles, :], in0=th[:, :, :], scalar=0.5, in1=node_x[:, tiles, :],
                                         op0=ALU.mult, op1=ALU.add).then_inc(x2_ready, 1)
                dve.wait_ge(x2_ready, c + 1)
            k0 = [0]

            def link2(ins):
                k0[0] += 1
                ins.then_inc(p2, 1)
                dve.wait_ge(p2, k0[0])

            for i in range(NBATCH):
                for t in range(i * TB, (i + 1) * TB):
                    ins = dve.bn_stats(stats[:, t, :], node_x[:, t, :])
                link2(ins)
                for t in range(i * TB, (i + 1) * TB):
                    ins = dve.bn_aggr(mv[:, t, :], stats[:, t, :])
            ins.then_inc(var_ready, 1)
            link2(dve.tensor_tensor(before_bf[:, :], upper[:, :], ident[:, :], ALU.subtract))
            link2(dve.tensor_copy(ones_bf[:, :], ones[:, :]))
            dve.wait_ge(sd_ready, 3)
            link2(dve.reciprocal(rstd[:, :], sd[:, :]))
            with dve.Fori(0, NT) as t:
                dve.tensor_scalar(node_h[:, t, :], node_x[:, t, :], mv[:, t, 0:1], rstd[:, bass.ds(t, 1)],
                                  ALU.subtract, ALU.mult).then_inc(y_ready, 1)
            dve.wait_ge(ffn_loaded, 16 * 6)

            def keep_logits(t, s, again):
                dve.wait_ge(gated, t + 1)
                dve.tensor_tensor(logits[:, t, :], bank[2 + s][:, 0:NE], gate_b_sb, ALU.add).then_inc(logits_ready, 1)
            node_tiles(dve, keep_logits)
            dve.wait_ge(logits_ready, NT)
            for t in range(NT):
                ins = dve.max(top8[:, t, :], logits[:, t, :])
            link2(ins)
            for t in range(NT):
                ins = dve.max_index(top8_at[:, t, :], top8[:, t, :], logits[:, t, :])
            link2(ins)
            dve.tensor_tensor(top_w[:, 1, :], top8[:, :, 1], top8[:, :, 0], ALU.subtract).then_inc(gap_ready, 1)
            for k in range(2):
                ins = dve.tensor_copy(choice[:, k, :], top8_at[:, :, k])
            link2(ins)
            for k in range(2):
                link2(dve.tensor_tensor(chosen[:, :, k * NT:(k + 1) * NT],
                                        iota_f[:, 0:NE].unsqueeze(2).to_broadcast([P, NE, NT]),
                                        choice[:, k, :].unsqueeze(1).to_broadcast([P, NE, NT]), ALU.is_equal))
            dve.tensor_copy(chosen_bf, chosen.rearrange("p e s -> p (e s)")).then_inc(chosen_ready, 1)
            dve.wait_ge(gap_exp, 1)
            link2(dve.tensor_scalar(top_w[:, 0, :], top_w[:, 1, :], 1.0, None, ALU.add))
            link2(dve.reciprocal(top_w[:, 0, :], top_w[:, 0, :]))
            link2(dve.tensor_tensor(top_w[:, 1, :], top_w[:, 1, :], top_w[:, 0, :], ALU.mult))
            link2(dve.memset(restart, 1.0))
            link2(dve.memset(restart.rearrange("p (e s) -> p e s", e=NE)[:, :, 0:1], 0.0))
            dve.wait_ge(tile_sums, 1)
            q = W // 4
            for k in range(4):
                ins = dve.tensor_copy(taken[:, k * q:(k + 1) * q], bank[k][:, 0:q])
            ins.then_inc(tile_sums_kept, 1)
            dve.wait_ge(tile_sums_kept, 1)
            link2(dve.tensor_tensor_scan(running, restart, taken, 0.0, ALU.mult, ALU.add))
            need, upto, base = ends[:, 0, :], ends[:, 1, :], ends[:, 2, :]
            need_i = ends[:, 3, :].bitcast(I32)
            totals = running.rearrange("p (e s) -> p e s", e=NE)[:, :, S2 - 1]
            link2(dve.tensor_scalar(need, totals, float(P - 1), None, ALU.add))
            link2(dve.tensor_copy(need_i, need))
            link2(dve.tensor_single_scalar(need_i, need_i, 7, op=ALU.arith_shift_right))
            link2(dve.tensor_copy(need, need_i))
            link2(dve.tensor_tensor_scan(upto, ones[:, 0:NE], need, 0.0, ALU.mult, ALU.add))
            link2(dve.tensor_tensor(base, upto, need, ALU.subtract))
            link2(dve.tensor_scalar(base, base, float(P), None, ALU.mult))
            link2(dve.tensor_tensor(running, running, taken, ALU.subtract))
            dve.wait_ge(ranks, 1)
            for k in range(4):
                ins = dve.tensor_tensor(place[:, k * q:(k + 1) * q], bank[4 + k][:, 0:q], running[:, k * q:(k + 1) * q], ALU.add)
            link2(ins)
            place3 = place.rearrange("p (e s) -> p e s", e=NE)
            link2(dve.tensor_tensor(place3, place3, base.unsqueeze(2).to_broadcast([P, NE, S2]), ALU.add))
            link2(dve.tensor_tensor(place3, place3, chosen, ALU.mult))
            link2(dve.tensor_reduce(taken[:, 0:S2], place3.rearrange("p e s -> p s e"), AX.X, ALU.add))
            dve.tensor_copy(slot[:, :], taken[:, 0:S2]).then_inc(slot_ready, 1)
            dve.wait_ge(slot_ready, 1)
            ended = restart[:, 0:MT * 8]
            link2(dve.memset(tile_of, 0.0))
            for k in range(2):
                e3 = restart[:, 0:MT * 8].rearrange("p (i e) -> p i e", e=8)
                link2(dve.tensor_tensor(e3, iota_f[:, 0:MT].unsqueeze(2).to_broadcast([P, MT, 8]),
                                        upto[:, 8 * k:8 * k + 8].unsqueeze(1).to_broadcast([P, MT, 8]), ALU.is_ge))
                link2(dve.tensor_reduce(taken[:, 200:200 + MT], e3, AX.X, ALU.add))
                link2(dve.tensor_tensor(tile_of, tile_of, taken[:, 200:200 + MT], ALU.add))
            link2(dve.tensor_scalar(tile_of, tile_of, float(NE - 1), None, ALU.min))
            link2(dve.tensor_copy(tile_expert[:, :], tile_of))
            dve.tensor_scalar(e_hot, tile_of[0:NE, :], iota_p[0:NE, 0:1], None, ALU.is_equal).then_inc(e_hot_ready, 1)
            c3 = fd1f[:, 0:NT * NE].rearrange("p (e t) -> p e t", e=NE)
            c4 = fd1f[:, NT * NE:2 * NT * NE].rearrange("p (e t) -> p e t", e=NE)
            for k, v in enumerate((c3, c4)):
                link2(dve.tensor_tensor(v, chosen[:, :, k * NT:(k + 1) * NT],
                                        top_w[:, k, :].unsqueeze(1).to_broadcast([P, NE, NT]), ALU.mult))
            link2(dve.tensor_tensor(share.rearrange("p t e -> p e t"), c3, c4, ALU.add))
            dve.wait_ge(b1_turned, 1)
            dve.tensor_copy(b1_of[:, :, :].rearrange("p k i -> p (k i)"), bank[0][:, 0:FB * MT]).then_inc(routing_done, 1)

            def keep_eout(i, b, again, last):
                dve.wait_ge(expert_done, i + 1)
                if again:
                    dve.wait_ge(eout_stored[b], (i - b) * 8)
                dve.tensor_copy(eout[b], bank[4 + b][:, 0:D]).then_inc(eout_ready, 1)
            expert_tiles(dve, keep_eout)

            for c in range(NBATCH):
                b = c % 2
                g0, g1 = got[b]
                dve.wait_ge(out_gathered[b], 16 * 2 * TB * (c // 2 + 1))
                for k in range(TB):
                    t = c * TB + k
                    dve.scalar_tensor_tensor(out=g1[:, k, :], in0=g1[:, k, :], scalar=top_w[:, 1, t:t + 1],
                                             in1=node_h[:, t, :], op0=ALU.mult, op1=ALU.add)
                    dve.wait_ge(b2_ready, t + 1)
                    dve.scalar_tensor_tensor(out=g0[:, k, :], in0=g0[:, k, :], scalar=top_w[:, 0, t:t + 1],
                                             in1=bank[2 + t % 2][:, 0:D], op0=ALU.mult, op1=ALU.add).then_inc(got_used, 1)
                dve.wait_ge(got_used, (c + 1) * TB)
                link2(dve.tensor_tensor(g0, g0, g1, ALU.add))
                for k in range(TB):
                    ins = dve.bn_stats(stats[:, c * TB + k, :], g0[:, k, :])
                link2(ins)
                for k in range(TB):
                    ins = dve.bn_aggr(mv[:, c * TB + k, :], stats[:, c * TB + k, :])
                ins.then_inc(y_var, 1)
                dve.wait_ge(y_sd, c + 1)
                link2(dve.reciprocal(rstd[:, c * TB:(c + 1) * TB], sd[:, c * TB:(c + 1) * TB]))
                for k in range(TB):
                    t = c * TB + k
                    ins = dve.tensor_scalar(g0[:, k, :], g0[:, k, :], mv[:, t, 0:1], rstd[:, t:t + 1],
                                            ALU.subtract, ALU.mult)
                link2(ins)
                link2(dve.tensor_tensor(g0, g0, gamma_sb.unsqueeze(1).to_broadcast([P, TB, D]), ALU.mult))
                link2(dve.tensor_tensor(g0, g0, beta_sb.unsqueeze(1).to_broadcast([P, TB, D]), ALU.add))
                dve.tensor_tensor(g0, g0, node_x[:, c * TB:(c + 1) * TB, :], ALU.add).then_inc(out_ready, 1)


_NAMES = {"x": "x", "src": "src", "dst": "dst", "Wsrc": "L0_gnn_Wsrc", "bsrc": "L0_gnn_bsrc", "Wdst": "L0_gnn_Wdst",
          "bdst": "L0_gnn_bdst", "Wval": "L0_gnn_Wval", "bval": "L0_gnn_bval", "attn": "L0_gnn_attn",
          "gate_w": "L0_ffn_gate_w", "gate_b": "L0_ffn_gate_b", "w1": "L0_ffn_w1", "b1": "L0_ffn_b1",
          "w2": "L0_ffn_w2", "b2": "L0_ffn_b2", "gamma": "L0_ffn_gamma", "beta": "L0_ffn_beta"}


def kernel(**inputs):
    import numpy as _np
    import concourse.bacc as _bacc
    from concourse.bass_utils import run_bass_kernel_spmd as _run

    nc = _bacc.Bacc("TRN2", target_bir_lowering=False, num_devices=1)
    arrays, args = {}, {}
    for short, name in _NAMES.items():
        a = _np.ascontiguousarray(inputs[name])
        arrays[f"in_{short}"] = a
        args[short] = nc.dram_tensor(f"in_{short}", a.shape, mybir.dt.from_np(a.dtype), kind="ExternalInput").ap()
    shape = inputs["x"].shape
    out = nc.dram_tensor("out_0", shape, F32, kind="ExternalOutput").ap()
    build_gnn_moe(nc, out=out, **args)
    r = _run(nc, [arrays], core_ids=[0])
    return r.results[0]["out_0"]
```

```python
from contextlib import ExitStack

import concourse.bass as bass
from concourse import mybir

F32 = mybir.dt.float32
BF16 = mybir.dt.bfloat16
I32 = mybir.dt.int32
U32 = mybir.dt.uint32
ALU = mybir.AluOpType
ACT = mybir.ActivationFunctionType
AX = mybir.AxisListType

P = 128
BIG = 1e38
EPS = 1e-5


def build_gnn_moe(nc, x, src, dst, Wsrc, bsrc, Wdst, bdst, Wval, bval, attn,
                  gate_w, gate_b, w1, b1, w2, b2, gamma, beta, out):
    N, D = x.shape
    E = src.shape[0]
    H = attn.shape[1]
    FH = D // H
    NE, _, F = w1.shape
    KB = D // P
    FB = F // P

    NT = -(-N // P)
    LAST = N - (NT - 1) * P
    J = 4
    R = 4
    COLS = -(-E // (P * R * J)) * R * J
    GROUPS = COLS // J
    REC = D + 2 * H
    ACC = D + H
    M1 = J + 1
    TB = 7
    NBATCH = NT // TB
    S2 = 2 * NT
    GR = 3
    MT = 2 * (-(-(2 * NT * P + NE * (P - 1)) // (2 * P)))
    assert NT == TB * NBATCH and (NT - 3) % 2 == 0 and GROUPS % R == 0 and D == 256 and F == 512

    with ExitStack() as ctx:
        def sb(name, shape, dt=F32):
            return ctx.enter_context(nc.sbuf_tensor(name, shape, dt))

        def sem(name):
            return ctx.enter_context(nc.semaphore(name))

        def dram(name, shape, dt=F32):
            return nc.dram_tensor(name, shape, dt, kind="Internal").ap()

        sv_table = dram("sv_table", [NT * P, 2 * D])
        d_table = dram("d_table", [NT * P, D])
        records = dram("records", [COLS * P, REC])
        lane_tails = dram("lane_tails", [P + 1, REC])
        expert_in = dram("expert_in", [MT * P, D])
        expert_out = dram("expert_out", [MT * P, D])

        node_x = sb("node_x", [P, NT, D])
        node_h = sb("node_h", [P, NT, D])

        src_all = sb("src_all", [P, COLS + R * J], I32)
        dst_all = sb("dst_all", [P, COLS + R * J], I32)
        same = sb("same", [P, COLS + J])
        minus_low = sb("minus_low", [P, COLS])
        dst_high = sb("dst_high", [P, COLS], BF16)
        pick = sb("pick", [P, COLS + 2 * J])
        span_part = sb("span_part", [P, 1])
        few_nodes = sb("few_nodes", [P, 1], I32)
        idx_src = [sb(f"idx_src{b}", [P, J], I32) for b in range(R)]
        idx_dst = [sb(f"idx_dst{b}", [P, J], I32) for b in range(R)]

        arena = sb("arena", [P, 18200])

        def part(at, *shape):
            n = 1
            for d in shape:
                n *= d
            v = arena[:, at:at + n]
            return v if len(shape) == 1 else v.rearrange("p (a b) -> p a b", a=shape[0])

        sv = [part(b * J * 2 * D, J, 2 * D) for b in range(R)]
        fd = [part(8192 + b * J * D, J, D) for b in range(R)]
        pick_diag = [fd[b][:, 1:3, :].rearrange("p a (n c) -> p (a n) c", c=P) for b in range(R)]
        th = [part(12288, J * D), part(14368, J * D)]
        msg = part(13312, J, ACC)
        rec = [part(16024 + b * J * REC, J, REC) for b in range(2)]
        carry = sb("carry", [P, ACC])
        hot_low = [sb(f"hot_low{b}", [P, J, P], BF16) for b in range(2)]
        hot_high = [sb(f"hot_high{b}", [P, J, NT], BF16) for b in range(2)]
        seg_mask = sb("seg_mask", [P, H * M1 + 1])
        score = sb("score", [P, H, M1])
        fmax = sb("fmax", [P, H * M1])
        smax = sb("smax", [P, H, M1])
        diff = sb("diff", [P, H, M1])
        wgt = sb("wgt", [P, H, M1])

        ident = sb("ident", [P, P])
        iota_p = sb("iota_p", [P, 1])
        iota_f = sb("iota_f", [P, P])
        iota_bf = sb("iota_bf", [P, P], BF16)
        attn_col = sb("attn_col", [P, KB])
        attn_head = sb("attn_head", [P, KB, H])
        stats = sb("stats", [P, NT, 6])
        mv = sb("mv", [P, NT, 2])
        rstd = sb("rstd", [P, NT])
        sd = sb("sd", [P, NT])
        ones_bf = sb("ones_bf", [P, P], BF16)
        before_bf = sb("before_bf", [P, P], BF16)
        upper = sb("upper", [P, P])
        ones = sb("ones", [P, P])
        head_of = sb("head_of", [H, D])
        prev_dst = sb("prev_dst", [P, 1], I32)
        chain = sb("chain", [P, 1])
        nflag = sb("nflag", [P, 8, NT])
        idx_last = sb("idx_last", [P, NT], I32)
        idx_tail = sb("idx_tail", [P, NT], I32)
        top_w = sb("top_w", [P, 2, NT])
        slot = sb("slot", [P, S2], I32)
        tile_expert = sb("tile_expert", [P, MT], I32)
        b1_of = sb("b1_of", [P, FB, MT])
        epsc = sb("epsc", [P, 1])

        ZC = MT * D // (GROUPS // R - 1)
        assert ZC * (GROUPS // R - 1) == MT * D and ZC % (2 * R) == 0 and ZC // 2 <= 8 * NT
        zeros = nflag[:, :, :].rearrange("p k t -> p (k t)")[:, 0:ZC // 2]

        psum = ctx.enter_context(nc.psum_tensor("psum", [P, 8 * 512], F32))
        bank = [psum[:, 512 * k:512 * (k + 1)] for k in range(8)]
        zT = [psum[:, 1024 * q:1024 * q + J * KB * P] for q in range(2)]
        zT4 = [z.rearrange("p (j k e) -> p j k e", j=J, k=KB) for z in zT]
        score_ps = [bank[4 + q][:, 0:J * H] for q in range(2)]
        degree_ps = bank[6][:, 0:NT]

        sv0f, sv1f, fd0f, fd1f, thf, msgf, rec0f, rec1f = (
            part(at, n) for at, n in ((0, 3584), (3584, 3584), (7168, 1792), (8960, 1792), (10752, 1792),
                                      (12544, 1848), (14392, 1904), (16296, 1904)))
        wT = sv0f[:, 0:KB * 3 * D].rearrange("p (k o) -> p k o", k=KB)
        w_raw = sv0f[:, KB * 3 * D:2 * KB * 3 * D].rearrange("p (m k) -> p m k", k=D)
        bias3 = sv1f[:, 2048:2048 + 3 * D]
        stage = [sv1f[:, 768 * b:768 * b + 768] for b in range(2)]
        hT = [sv1f[:, 1536 + 256 * b:1792 + 256 * b].rearrange("p (k c) -> p k c", k=KB) for b in range(2)]

        h_row = [sv1f[:, 2816 + 256 * b:3072 + 256 * b] for b in range(2)]
        tailT = fd0f
        aT = tailT[:, 0:KB * P].rearrange("p (k l) -> p k l", k=KB)
        mT = tailT[0:H, 256:384]
        dT = tailT[0:H, 384:512]
        chainT = tailT[:, 512:640]
        lane_mask = tailT[:, 640:768]
        lane_max = tailT[0:H, 768:896]
        lane_exp = tailT[0:H, 896:1152]
        lane_den = tailT[0:H, 1152:1280]
        chain_wide = tailT[:, 1280:1408]
        accT = fd1f[:, 0:KB * P].rearrange("p (k l) -> p k l", k=KB)
        tail_sb = msgf[:, 0:REC]
        no_tail = msgf[0:1, REC:2 * REC]
        node_rec = [sv0f[:, 0:TB * REC].rearrange("p (a b) -> p a b", a=TB),
                    sv1f[:, 0:TB * REC].rearrange("p (a b) -> p a b", a=TB)]
        node_car = [rec0f.rearrange("p (a b) -> p a b", a=TB), rec1f.rearrange("p (a b) -> p a b", a=TB)]
        u_sb = fd0f.rearrange("p (a b) -> p a b", a=TB)
        u_th = thf.rearrange("p (a b) -> p a b", a=TB)
        moves = sv0f[:, 1904:2016].rearrange("p (a b) -> p a b", a=TB)
        moved = sv0f[:, 2016:2128].rearrange("p (a b) -> p a b", a=TB)
        nmax = sv0f[:, 2128:2184].rearrange("p (a b) -> p a b", a=TB)
        nden = sv0f[:, 2184:2240].rearrange("p (a b) -> p a b", a=TB)

        yT_ps = psum[:, 0:TB * D]
        yT = fd1f
        W = NE * S2
        chosen = fd0f[:, 0:W].rearrange("p (e s) -> p e s", e=NE)
        taken = fd1f[:, 0:W]
        running = thf[:, 0:W]
        place = sv0f[:, 0:W]
        restart = sv0f[:, W:2 * W]
        chosen_bf = rec0f[:, 0:W // 2].bitcast(BF16)
        logits = sv1f[:, 1904:1904 + NT * NE].rearrange("p (t e) -> p t e", t=NT)
        top8 = msgf[:, 0:8 * NT].rearrange("p (t e) -> p t e", t=NT)
        top8_at = msgf[:, 8 * NT:16 * NT].bitcast(U32).rearrange("p (t e) -> p t e", t=NT)
        choice = msgf[:, 16 * NT:18 * NT].rearrange("p (k t) -> p k t", k=2)
        gate_w_sb = msgf[:, 1000:1000 + KB * NE].rearrange("p (k e) -> p k e", k=KB)
        gate_b_sb = msgf[:, 1032:1048]
        ends = msgf[:, 1050:1050 + 5 * NE].rearrange("p (k e) -> p k e", k=5)
        tile_of = msgf[:, 1140:1140 + MT]
        e_hot = msgf[0:NE, 1260:1260 + MT]
        b1_sb = rec0f[0:NE, 784:784 + F]
        b2_sb = rec0f[0:NE, 1296:1296 + D]
        share = rec1f[:, 0:NT * NE].rearrange("p (t e) -> p t e", t=NT)
        gamma_sb = rec1f[:, 784:784 + D]
        beta_sb = rec1f[:, 1040:1040 + D]
        share_t = fd1f[0:NE, 0:TB * P]
        b2_ps = psum[:, 1024:1024 + TB * D]
        w1_sb = [sv0f[:, 1024 * b:1024 * b + 1024].rearrange("p (k f) -> p k f", k=KB) for b in range(2)]
        w2_sb = [sv1f[:, 1024 * b:1024 * b + 1024].rearrange("p (k f) -> p k f", k=FB) for b in range(2)]
        tok = [sv0f[:, 2048 + 256 * b:2304 + 256 * b] for b in range(2)]
        tokT = [sv0f[:, 2560 + 256 * b:2816 + 256 * b].rearrange("p (k c) -> p k c", k=KB) for b in range(2)]
        hidT = [sv1f[:, 2048 + 512 * b:2560 + 512 * b].rearrange("p (k c) -> p k c", k=FB) for b in range(2)]
        eout = [thf[:, 256 * b:256 * b + 256] for b in range(2)]
        fdf = part(7168, 3584)
        got = [[(sv0f, sv1f, fdf)[b][:, 1792 * k:1792 * (k + 1)].rearrange("p (t d) -> p t d", t=TB)
                for k in range(2)] for b in range(GR)]

        block = ctx.enter_context(nc.Block())

        x_loaded = [sem(f"x_loaded{c}") for c in range(NBATCH)]
        x_padded = sem("x_padded")
        edges_padded = sem("edges_padded")
        edges_loaded = sem("edges_loaded")
        weights_loaded = sem("weights_loaded")
        consts_loaded = sem("consts_loaded")
        consts_made = sem("consts_made")
        zeros_made = sem("zeros_made")
        zeros_stored = sem("zeros_stored")
        w_turned = sem("w_turned")
        w_kept = sem("w_kept")
        var_ready = sem("var_ready")
        sd_ready = sem("sd_ready")
        h_normed = sem("h_normed")
        row_ready = sem("row_ready")
        h_turned = sem("h_turned")
        hT_ready = sem("hT_ready")
        projected = sem("projected")
        stage_ready = sem("stage_ready")
        stage_stored = [sem(f"stage_stored{b}") for b in range(2)]
        p0 = sem("p0_vector_done")
        e0 = sem("edge_vector_done")

        idx_ready = sem("idx_ready")
        prev_set = sem("prev_set")
        prev_loaded = sem("prev_loaded")
        chain_ready = sem("chain_ready")
        tails_turned = sem("tails_turned")
        tails_kept = sem("tails_kept")
        lane_moves = sem("lane_moves")
        lane_moved = sem("lane_moved")
        lane_factors = sem("lane_factors")
        factors_wide = sem("factors_wide")
        lanes_summed = sem("lanes_summed")
        tails_back = sem("tails_back")
        tail_ready = sem("tail_ready")
        tail_stored = sem("tail_stored")
        counted = sem("counted")
        degrees_kept = sem("degrees_kept")
        degrees_summed = sem("degrees_summed")
        node_idx_ready = sem("node_idx_ready")
        node_gathered = [sem(f"node_gathered{b}") for b in range(2)]
        node_used = sem("node_used")
        moves_ready = sem("moves_ready")
        moved_ready = sem("moved_ready")
        u_ready = sem("u_ready")
        u_tanh = sem("u_tanh")
        x2_ready = sem("x2_ready")
        p1 = sem("p1_vector_done")
        ffn_loaded = sem("ffn_loaded")
        gate_loaded = sem("gate_loaded")
        y_turned = sem("y_turned")
        yT_ready = sem("yT_ready")
        y_var_ready = sem("y_var_ready")
        y_sd_ready = sem("y_sd_ready")
        gated = sem("gated")
        logits_ready = sem("logits_ready")
        y_ready = sem("y_ready")
        gap_ready = sem("gap_ready")
        gap_exp = sem("gap_exp")
        chosen_ready = sem("chosen_ready")
        tile_sums = sem("tile_sums")
        tile_sums_kept = sem("tile_sums_kept")
        ranks = sem("ranks")
        slot_ready = sem("slot_ready")
        e_hot_ready = sem("e_hot_ready")
        b1_turned = sem("b1_turned")
        routing_done = sem("routing_done")
        tokens_sent = [sem(f"tokens_sent{c}") for c in range(NBATCH)]
        tok_loaded = [sem(f"tok_loaded{b}") for b in range(2)]
        w1_loaded = [sem(f"w1_loaded{b}") for b in range(2)]
        w2_loaded = [sem(f"w2_loaded{b}") for b in range(2)]
        tok_turned = sem("tok_turned")
        tokT_ready = sem("tokT_ready")
        hidden = sem("hidden")
        hidT_ready = sem("hidT_ready")
        expert_done = sem("expert_done")
        eout_ready = sem("eout_ready")
        eout_stored = [sem(f"eout_stored{b}") for b in range(2)]
        out_gathered = [sem(f"out_gathered{b}") for b in range(GR)]
        share_turned = sem("share_turned")
        share_kept = sem("share_kept")
        b2_ready = sem("b2_ready")
        y_var = sem("y_var")
        y_sd = sem("y_sd")
        base_ready = sem("base_ready")
        out_ready = sem("out_ready")
        out_stored = [sem(f"out_stored{b}") for b in range(GR)]
        p2 = sem("p2_vector_done")
        gathers_issued = sem("gathers_issued")
        gathered = [sem(f"gathered{b}") for b in range(R)]
        attn_masked = sem("attn_masked")
        z_ready = sem("z_ready")
        silu_ready = sem("silu_ready")
        scored = sem("scored")
        score_read = sem("score_read")
        tanh_ready = sem("tanh_ready")
        diff_ready = sem("diff_ready")
        wgt_ready = sem("wgt_ready")
        side_ready = sem("side_ready")
        msg_used = sem("msg_used")
        rec_ready = sem("rec_ready")
        span_parts = sem("span_parts")
        span_summed = sem("span_summed")
        span_known = sem("span_known")
        pick_ready = sem("pick_ready")
        rec_stored = [sem(f"rec_stored{b}") for b in range(2)]
        squares_ready = sem("squares_ready")
        low_ready = sem("low_ready")
        hot_ready = sem("hot_ready")
        hot_used = sem("hot_used")

        def node_tiles(eng, head, tail=None):
            first, steps = 7, 6
            for t in range(first):
                head(t, t % 2, t)
                if tail and t:
                    tail(t - 1, (t - 1) % 2, t - 1)
            assert (NT - first) % steps == 0
            with eng.Fori(0, (NT - first) // steps) as i:
                for k in range(first, first + steps):
                    head(i * steps + k, k % 2, k)
                    if tail:
                        tail(i * steps + (k - 1), (k - 1) % 2, k - 1)
            if tail:
                tail(NT - 1, (NT - 1) % 2, NT - 1)

        def first_pass():
            for c in range(NBATCH + 1):
                for part_of_norm, tiles in ((0, range(0, 2)), (1, range(2, 3)), (2, range(3, 5)), (3, range(5, 7))):
                    if c < NBATCH:
                        yield "norm", part_of_norm, c
                    if c:
                        for k in tiles:
                            yield "tile", None, (c - 1) * TB + k

        def expert_tiles(eng, step):
            first, steps, rest = 4, 6, 2
            for i in range(first):
                step(i, i % 2, i, False)
            assert (MT - first - rest) % steps == 0
            with eng.Fori(0, (MT - first - rest) // steps) as p:
                for k in range(first, first + steps):
                    step(p * steps + k, k % 2, k, False)
            for i in range(MT - rest, MT):
                step(i, i % 2, i, i == MT - 1)

        def edge_groups(eng, head, tail=None):
            for g in range(R):
                head(g, g, g)
                if tail and g:
                    tail(g - 1, g - 1, g - 1)
            with eng.Fori(1, GROUPS // R) as i:
                for b in range(R):
                    head(i * R + b, b, R + b)
                    if tail:
                        tail(i * R + (b - 1) if b else (i - 1) * R + (R - 1), (b - 1) % R, R + b - 1)
            if tail:
                tail(GROUPS - 1, R - 1, GROUPS - 1)

        def by_nodes_a_group(eng, loop):
            eng.wait_ge(span_known, 1)
            few = eng.value_load(few_nodes[0:1, 0:1], min_val=0, max_val=1)
            with eng.If(few == 1):
                loop(True)
            with eng.Else():
                loop(False)

        @block.sync
        def _(sp):
            def load_x(c):
                full = min(TB, (N - c * TB * P) // P)
                sp.dma_start(node_x[:, c * TB:c * TB + full, :],
                             x[c * TB * P:(c * TB + full) * P, :].rearrange("(t p) d -> p t d", p=P)).then_inc(x_loaded[c], 16)
                if full < TB:
                    sp.wait_ge(x_padded, 1)
                    sp.dma_start(node_x[0:LAST, NT - 1, :], x[(NT - 1) * P:N, :]).then_inc(x_loaded[c], 16)
            load_x(0)
            for m, Wm in enumerate((Wsrc, Wval, Wdst)):
                sp.dma_start(w_raw[:, 2 * m:2 * m + 2, :],
                             Wm.rearrange("(o p) k -> p o k", p=P)).then_inc(weights_loaded, 16)
            load_x(1)
            for m, bb in enumerate((bsrc, bval, bdst)):
                sp.dma_start(bias3[:, m * D:(m + 1) * D],
                             bb.rearrange("(a d) -> a d", a=1).to_broadcast([P, D])).then_inc(consts_loaded, 16)
            sp.dma_start(attn_col[:, :], attn.rearrange("a h f -> (a h f)").rearrange("(k p) -> p k", p=P),
                         allow_slow_non_contiguous=True).then_inc(consts_loaded, 16)
            for c in range(2, NBATCH):
                load_x(c)
            sp.wait_ge(prev_set, 1)
            sp.dma_start(prev_dst[1:P, :], dst[0:(P - 1) * COLS].rearrange("(p j) -> p j", j=COLS)[:, COLS - 1:COLS],
                         allow_slow_non_contiguous=True).then_inc(prev_loaded, 16)
            sp.wait_ge(edges_padded, 2)
            full = E // COLS
            for arr, t in ((src, src_all), (dst, dst_all)):
                for a, z in ((0, 112), (112, full)):
                    sp.dma_start(t[a:z, 0:COLS], arr[a * COLS:z * COLS].rearrange("(p j) -> p j", j=COLS)).then_inc(edges_loaded, 16)
                sp.dma_start(t[full:full + 1, 0:E - full * COLS],
                             arr[full * COLS:E].rearrange("(p j) -> p j", p=1)).then_inc(edges_loaded, 16)
            def store_tile(t, s, least):
                sp.wait_ge(stage_ready, t + 1)
                sp.dma_start(sv_table[bass.ds(t * P, P), :], stage[s][:, 0:2 * D]).then_inc(stage_stored[s], 16)
                sp.dma_start(d_table[bass.ds(t * P, P), :], stage[s][:, 2 * D:3 * D]).then_inc(stage_stored[s], 16)
            node_tiles(sp, store_tile)

            rv = records.rearrange("(p j) r -> p j r", p=P)
            zero_rows = expert_in.rearrange("(p r) d -> p (r d)", p=P)
            sp.wait_ge(zeros_made, 1)

            def store_group(g, b, least):
                sp.wait_ge(side_ready, g + 1)
                sp.wait_ge(rec_ready, g + 1)
                sp.dma_start(rv[:, bass.ds(g * J, J), :], rec[b % 2]).then_inc(rec_stored[b % 2], 16)
                if b == 0 and least >= R:
                    sp.dma_start(zero_rows[:, bass.ds((g - R) * (ZC // R), ZC)].rearrange("p (a z) -> p a z", a=2),
                                 zeros.unsqueeze(1).to_broadcast([P, 2, ZC // 2])).then_inc(zeros_stored, 16)
            edge_groups(sp, store_group)
            for b in range(2):
                sp.wait_ge(rec_stored[b], 16 * (GROUPS // 2))
            sp.wait_ge(tail_ready, 2)
            sp.dma_start(lane_tails[0:P, :], tail_sb).then_inc(tail_stored, 16)
            sp.dma_start(lane_tails[P:P + 1, :], no_tail).then_inc(tail_stored, 16)
            sp.dma_start(gate_w_sb, gate_w.rearrange("(k p) e -> p k e", p=P)).then_inc(gate_loaded, 16)
            sp.dma_start(gate_b_sb, gate_b.rearrange("(a e) -> a e", a=1).to_broadcast([P, NE])).then_inc(gate_loaded, 16)
            sp.wait_ge(x2_ready, NBATCH)
            sp.dma_start(gamma_sb, gamma.rearrange("(a e) -> a e", a=1).to_broadcast([P, D])).then_inc(ffn_loaded, 16)
            sp.dma_start(beta_sb, beta.rearrange("(a e) -> a e", a=1).to_broadcast([P, D])).then_inc(ffn_loaded, 16)
            sp.dma_start(b1_sb, b1).then_inc(ffn_loaded, 16)
            sp.dma_start(b2_sb, b2).then_inc(ffn_loaded, 16)

            sp.wait_ge(routing_done, 1)
            for c in range(NBATCH):
                sp.wait_ge(tokens_sent[c], 16 * 2 * TB)

            def load_tok(i, b, again):
                if again:
                    sp.wait_ge(tok_turned, i - 1)
                sp.dma_start(tok[b], expert_in[bass.ds(i * P, P), :]).then_inc(tok_loaded[b], 16)

            def store_eout(i, b):
                sp.wait_ge(eout_ready, i + 1)
                sp.dma_start(expert_out[bass.ds(i * P, P), :], eout[b]).then_inc(eout_stored[b], 16)

            load_tok(0, 0, False)

            def load_expert(i, b, least, last):
                if not last:
                    load_tok(i + 1, 1 - b, least >= 1)
                e = sp.value_load(tile_expert[0:1, bass.ds(i, 1)], min_val=0, max_val=NE - 1)

                def load_weights():
                    if least >= 2:
                        sp.wait_ge(hidden, i - 1)
                    sp.dma_start(w1_sb[b].unsqueeze(1), w1[bass.ds(e, 1), :, :].rearrange("a (k p) f -> p a k f", p=P)).then_inc(w1_loaded[b], 16)
                    if least >= 2:
                        sp.wait_ge(expert_done, i - 1)
                    sp.dma_start(w2_sb[b].unsqueeze(1), w2[bass.ds(e, 1), :, :].rearrange("a (k p) f -> p a k f", p=P)).then_inc(w2_loaded[b], 16)

                if least >= 2:
                    before = sp.value_load(tile_expert[0:1, bass.ds(i - 2, 1)], min_val=0, max_val=NE - 1)
                    with sp.If(e != before):
                        load_weights()
                    with sp.Else():
                        sp.wait_ge(hidden, i - 1)
                        sp.sem_inc(w1_loaded[b], 16)
                        sp.wait_ge(expert_done, i - 1)
                        sp.sem_inc(w2_loaded[b], 16)
                    store_eout(i - 2, b)
                else:
                    load_weights()
            expert_tiles(sp, load_expert)
            store_eout(MT - 2, 0)
            store_eout(MT - 1, 1)

            for c in range(NBATCH):
                sp.wait_ge(out_ready, c + 1)
                full = min(TB, (N - c * TB * P) // P)
                sp.dma_start(out[c * TB * P:(c * TB + full) * P, :].rearrange("(t p) d -> p t d", p=P),
                             got[c % GR][0][:, 0:full, :]).then_inc(out_stored[c % GR], 16)
                if full < TB:
                    sp.dma_start(out[(NT - 1) * P:N, :], got[c % GR][0][0:LAST, full, :]).then_inc(out_stored[c % GR], 16)
            for b in range(GR):
                stores = len(range(b, NBATCH, GR)) + ((NBATCH - 1) % GR == b)
                sp.wait_ge(out_stored[b], 16 * stores)

        @block.gpsimd
        def _(pool):
            pool.memset(node_x[:, NT - 1, :], 0.0).then_inc(x_padded, 1)
            pool.memset(src_all[:, COLS - 352:], 0).then_inc(edges_padded, 1)
            pool.memset(dst_all[:, COLS - 352:], N).then_inc(edges_padded, 1)
            pool.memset(ident[:, :], 0.0).then_inc(consts_made, 1)
            pool.iota(iota_f[:, :], pattern=[[1, P]], base=0, channel_multiplier=0,
                      allow_small_or_imprecise_dtypes=True).then_inc(consts_made, 1)
            pool.iota(iota_p[:, :], pattern=[[1, 1]], base=0, channel_multiplier=1,
                      allow_small_or_imprecise_dtypes=True).then_inc(consts_made, 1)
            pool.memset(epsc[:, :], EPS).then_inc(consts_made, 1)
            pool.memset(upper[:, :], 1.0).then_inc(consts_made, 1)
            pool.memset(ones[:, :], 1.0).then_inc(consts_made, 1)
            pool.memset(head_of[:, :], 1.0).then_inc(consts_made, 1)
            pool.memset(attn_head[:, :, :], 0.5).then_inc(attn_masked, 1)
            pool.wait_ge(attn_masked, 1)
            pool.affine_select(out=attn_head[:, :, :], in_=attn_head[:, :, :], compare_op=ALU.is_ge, fill=0.0,
                               base=0, pattern=[[P, KB], [-FH, H]], channel_multiplier=1).then_inc(attn_masked, 1)
            pool.wait_ge(attn_masked, 2)
            pool.affine_select(out=attn_head[:, :, :], in_=attn_head[:, :, :], compare_op=ALU.is_ge, fill=0.0,
                               base=FH - 1, pattern=[[-P, KB], [FH, H]], channel_multiplier=-1).then_inc(attn_masked, 1)
            pool.memset(prev_dst[:, :], -1).then_inc(prev_set, 1)
            pool.wait_ge(consts_made, 7)
            pool.affine_select(out=upper[:, :], in_=upper[:, :], compare_op=ALU.is_ge, fill=0.0,
                               base=0, pattern=[[1, P]], channel_multiplier=-1).then_inc(consts_made, 1)
            pool.affine_select(out=head_of[:, :], in_=head_of[:, :], compare_op=ALU.is_ge, fill=0.0,
                               base=0, pattern=[[1, D]], channel_multiplier=-FH).then_inc(consts_made, 1)
            pool.wait_ge(consts_made, 9)
            pool.affine_select(out=head_of[:, :], in_=head_of[:, :], compare_op=ALU.is_ge, fill=0.0,
                               base=FH - 1, pattern=[[-1, D]], channel_multiplier=FH).then_inc(consts_made, 1)
            pool.affine_select(out=ident[:, :], in_=ident[:, :], compare_op=ALU.not_equal, fill=1.0,
                               base=0, pattern=[[-1, P]], channel_multiplier=1).then_inc(consts_made, 1)
            pool.wait_ge(stage_stored[0], 16 * 2 * ((NT + 1) // 2))
            pool.wait_ge(stage_stored[1], 16 * 2 * (NT // 2))

            def gather_edges(few):
                def gather_group(g, b, least):
                    pool.wait_ge(idx_ready, g + 1)
                    pool.sem_inc(gathers_issued, 1)
                    for j in range(J):
                        pool.indirect_dma_start(sv[b][:, j, :], None, sv_table,
                                                bass.IndirectOffsetOnAxis(idx_src[b][:, j:j + 1], 0)).then_inc(gathered[b], 16)
                    for j in (0, J - 1) if few else range(J):
                        pool.indirect_dma_start(fd[b][:, j, :], None, d_table,
                                                bass.IndirectOffsetOnAxis(idx_dst[b][:, j:j + 1], 0)).then_inc(gathered[b], 16)
                edge_groups(pool, gather_group)
            by_nodes_a_group(pool, gather_edges)
            pool.wait_ge(node_idx_ready, 2)
            for b in range(2):
                pool.wait_ge(rec_stored[b], 16 * (GROUPS // 2))
            pool.wait_ge(tail_stored, 32)
            for c in range(NBATCH):
                b = c % 2
                if c >= 2:
                    pool.wait_ge(node_used, c - 1)
                for k in range(TB):
                    t = c * TB + k
                    pool.indirect_dma_start(node_rec[b][:, k, :], None, records,
                                            bass.IndirectOffsetOnAxis(idx_last[:, t:t + 1], 0)).then_inc(node_gathered[b], 16)
                    pool.indirect_dma_start(node_car[b][:, k, :], None, lane_tails,
                                            bass.IndirectOffsetOnAxis(idx_tail[:, t:t + 1], 0)).then_inc(node_gathered[b], 16)
            pool.wait_ge(slot_ready, 1)
            pool.wait_ge(zeros_stored, 16 * (GROUPS // R - 1))
            for t in range(NT):
                for s in (t, NT + t):
                    pool.indirect_dma_start(expert_in, bass.IndirectOffsetOnAxis(slot[:, s:s + 1], 0),
                                            node_h[:, t, :], None).then_inc(tokens_sent[t // TB], 16)
            for b in range(2):
                pool.wait_ge(eout_stored[b], 16 * (MT // 2))
            for c in range(NBATCH):
                b = c % GR
                if c >= GR:
                    pool.wait_ge(out_stored[b], 16 * (c // GR))
                for k in range(TB):
                    for h in range(2):
                        s = h * NT + c * TB + k
                        pool.indirect_dma_start(got[b][h][:, k, :], None, expert_out,
                                                bass.IndirectOffsetOnAxis(slot[:, s:s + 1], 0)).then_inc(out_gathered[b], 16)

        @block.tensor
        def _(pe):
            pe.wait_ge(consts_made, 11)
            pe.wait_ge(weights_loaded, 16 * 3)
            for m in range(3):
                for k in range(KB):
                    for o in range(2):
                        ins = pe.transpose(bank[2 * m + k][:, o * P:(o + 1) * P],
                                           w_raw[:, 2 * m + o, k * P:(k + 1) * P], ident[:, :])
                    ins.then_inc(w_turned, 1)
            pe.wait_ge(w_kept, 6)

            def turn_tile(t, s, least):
                if least >= 2:
                    pe.wait_ge(hT_ready, t - 1)
                pe.wait_ge(row_ready, t + 1)
                for k in range(KB):
                    ins = pe.transpose(bank[s][:, k * P:(k + 1) * P], h_row[s][:, k * P:(k + 1) * P], ident[:, :])
                ins.then_inc(h_turned, 1)

            def project_tile(t, s, least):
                pe.wait_ge(hT_ready, t + 1)
                if least >= 2:
                    pe.wait_ge(stage_ready, t - 1)
                for k in range(KB):
                    pe.matmul(bank[2 + 2 * s][:, :], hT[s][:, k, :], wT[:, k, 0:2 * D], start=(k == 0), stop=(k == KB - 1))
                for k in range(KB):
                    ins = pe.matmul(bank[3 + 2 * s][:, 0:D], hT[s][:, k, :], wT[:, k, 2 * D:3 * D],
                                    start=(k == 0), stop=(k == KB - 1))
                ins.then_inc(projected, 1)
            node_tiles(pe, turn_tile, project_tile)

            pe.wait_ge(span_parts, 1)
            pe.matmul(bank[7][:, 0:1], ones[:, :], span_part[:, :], start=True, stop=True).then_inc(span_summed, 1)

            def turn_group(g, b, few, least):
                q = b % 2
                if least >= 2:
                    pe.wait_ge(silu_ready, g - 1)
                if few:
                    pe.wait_ge(pick_ready, g + 1)
                rows = J + 2 if few else 2 * J
                pe.wait_ge(gathered[b], (g - b) * (16 * rows // R) + 16 * rows)
                for j in range(J):
                    for k in range(KB):
                        to = zT4[q][:, j, k, :]
                        pe.matmul(to, sv[b][:, j, k * P:(k + 1) * P], ident[:, :],
                                  is_transpose=True, start=True, stop=False)
                        if few and j in (1, 2):
                            pe.matmul(to, fd[b][:, 0, k * P:(k + 1) * P], pick_diag[b][:, 2 * j - 2, :],
                                      start=False, stop=False)
                            ins = pe.matmul(to, fd[b][:, J - 1, k * P:(k + 1) * P], pick_diag[b][:, 2 * j - 1, :],
                                            start=False, stop=True)
                        else:
                            ins = pe.matmul(to, fd[b][:, j, k * P:(k + 1) * P], ident[:, :],
                                            is_transpose=True, start=False, stop=True)
                ins.then_inc(z_ready, 1)

            def count_degrees(g, b, first):
                pe.wait_ge(hot_ready, g + 1)
                pe.wait_ge(low_ready, g + 1)
                for j in range(J):
                    ins = pe.matmul(degree_ps, hot_low[b % 2][:, j, :], hot_high[b % 2][:, j, :],
                                    start=(first and j == 0), stop=False, skip_group_check=True)
                ins.then_inc(hot_used, 1)

            def score_group(g, b, least):
                q = b % 2
                if least >= 2:
                    pe.wait_ge(score_read, g - 1)
                pe.wait_ge(silu_ready, g + 1)
                for j in range(J):
                    for k in range(KB):
                        ins = pe.matmul(score_ps[q][:, j * H:(j + 1) * H], th[q][:, (j * KB + k) * P:(j * KB + k + 1) * P],
                                        attn_head[:, k, :], start=(k == 0), stop=(k == KB - 1))
                ins.then_inc(scored, 1)
                if least >= 1:
                    count_degrees(g - 1, b - 1, least == 1)

            def score_edges(few):
                edge_groups(pe, lambda g, b, least: turn_group(g, b, few, least), score_group)
                count_degrees(GROUPS - 1, R - 1, False)
            by_nodes_a_group(pe, score_edges)
            pe.wait_ge(degrees_kept, 1)
            pe.matmul(bank[7][:, 0:NT], upper[:, :], nflag[:, 0, :], start=True, stop=True)
            pe.matmul(bank[7][:, 64:64 + NT], ones[:, :], nflag[:, 0, :], start=True, stop=True).then_inc(degrees_summed, 1)
            pe.wait_ge(rec_ready, GROUPS)
            pe.wait_ge(side_ready, GROUPS)
            pe.wait_ge(chain_ready, 1)
            tail = rec[1][:, J - 1, :]
            pe.transpose(bank[0][0:H, 0:P], tail[:, ACC:REC], ident[:, :])
            pe.transpose(bank[0][0:H, P:2 * P], tail[:, D:ACC], ident[:, :])
            pe.transpose(bank[0][:, 2 * P:3 * P], chain_wide, ident[:, :])
            for k in range(KB):
                ins = pe.transpose(bank[1][:, k * P:(k + 1) * P], tail[:, k * P:(k + 1) * P], ident[:, :])
            ins.then_inc(tails_turned, 1)
            pe.wait_ge(lane_factors, 1)
            for k in range(KB):
                ins = pe.matmul(bank[2 + k][:, 0:2 * P], head_of[:, k * P:(k + 1) * P], lane_exp, start=True, stop=True)
            ins.then_inc(factors_wide, 1)
            pe.wait_ge(lanes_summed, 1)
            for k in range(KB):
                pe.transpose(bank[4][:, k * P:(k + 1) * P], accT[:, k, :], ident[:, :])
            pe.transpose(bank[4][:, D:D + H], lane_den, ident[0:H, 0:H])
            pe.transpose(bank[4][:, ACC:REC], lane_max, ident[0:H, 0:H]).then_inc(tails_back, 1)
            pe.wait_ge(gate_loaded, 32)
            for c in range(NBATCH):
                pe.wait_ge(y_ready, c + 1)
                if c:
                    pe.wait_ge(yT_ready, c)
                for t in range(TB):
                    for k in range(KB):
                        ins = pe.transpose(yT_ps[:, t * D + k * P:t * D + (k + 1) * P],
                                           node_h[:, c * TB + t, k * P:(k + 1) * P], ident[:, :])
                ins.then_inc(y_turned, 1)
                pe.wait_ge(yT_ready, c + 1)
                if c:
                    pe.wait_ge(logits_ready, c)
                for t in range(TB):
                    for k in range(KB):
                        ins = pe.matmul(bank[5][:, t * NE:(t + 1) * NE], yT[:, t * D + k * P:t * D + (k + 1) * P],
                                        gate_w_sb[:, k, :], start=(k == 0), stop=(k == KB - 1))
                ins.then_inc(gated, 1)

            pe.wait_ge(chosen_ready, 1)
            q = W // 4
            for k in range(4):
                ins = pe.matmul(bank[k][:, 0:q], ones_bf[:, :], chosen_bf[:, k * q:(k + 1) * q], start=True, stop=True)
            ins.then_inc(tile_sums, 1)
            for k in range(4):
                ins = pe.matmul(bank[4 + k][:, 0:q], before_bf[:, :], chosen_bf[:, k * q:(k + 1) * q], start=True, stop=True)
            ins.then_inc(ranks, 1)
            pe.wait_ge(tile_sums_kept, 1)
            pe.wait_ge(ffn_loaded, 16 * 4)
            pe.wait_ge(e_hot_ready, 1)
            for k in range(FB):
                ins = pe.matmul(bank[0][:, k * MT:(k + 1) * MT], b1_sb[:, k * P:(k + 1) * P], e_hot, start=True, stop=True)
            ins.then_inc(b1_turned, 1)
            pe.wait_ge(routing_done, 1)

            for c in range(NBATCH):
                if c:
                    pe.wait_ge(share_kept, c)
                for k in range(TB):
                    ins = pe.transpose(psum[0:NE, k * P:(k + 1) * P], share[:, c * TB + k, :], ident[:, :])
                ins.then_inc(share_turned, 1)
                pe.wait_ge(share_kept, c + 1)
                if c:
                    pe.wait_ge(base_ready, c)
                for k in range(TB):
                    ins = pe.matmul(b2_ps[:, k * D:(k + 1) * D], share_t[:, k * P:(k + 1) * P], b2_sb, start=True, stop=True)
                ins.then_inc(b2_ready, 1)
            pe.wait_ge(base_ready, NBATCH)

            def turn(i, b, again):
                if again:
                    pe.wait_ge(tokT_ready, i - 1)
                pe.wait_ge(tok_loaded[b], half16(i, b))
                for k in range(KB):
                    ins = pe.transpose(bank[b][:, k * P:(k + 1) * P], tok[b][:, k * P:(k + 1) * P], ident[:, :])
                ins.then_inc(tok_turned, 1)

            def half16(i, b):
                return (i - b) * 8 + 16

            def first_layer(i, b, again):
                pe.wait_ge(tokT_ready, i + 1)
                pe.wait_ge(w1_loaded[b], half16(i, b))
                if again:
                    pe.wait_ge(hidT_ready, i - 1)
                for f in range(FB):
                    for k in range(KB):
                        ins = pe.matmul(bank[2 + b][:, f * P:(f + 1) * P], w1_sb[b][:, k, f * P:(f + 1) * P],
                                        tokT[b][:, k, :], start=(k == 0), stop=(k == KB - 1))
                ins.then_inc(hidden, 1)

            def second_layer(i, b, again):
                pe.wait_ge(hidT_ready, i + 1)
                pe.wait_ge(w2_loaded[b], half16(i, b))
                if again:
                    pe.wait_ge(eout_ready, i - 1)
                for f in range(FB):
                    ins = pe.matmul(bank[4 + b][:, 0:D], hidT[b][:, f, :], w2_sb[b][:, f, :],
                                    start=(f == 0), stop=(f == FB - 1))
                ins.then_inc(expert_done, 1)

            turn(0, 0, False)

            def expert_step(i, b, least, last):
                if not last:
                    turn(i + 1, 1 - b, least >= 1)
                first_layer(i, b, least >= 2)
                if least >= 1:
                    second_layer(i - 1, 1 - b, least >= 3)
            expert_tiles(pe, expert_step)
            second_layer(MT - 1, 1, True)

        @block.scalar
        def _(act):
            def keep_weights():
                for n in range(6):
                    m, k = n // 2, n % 2
                    act.wait_ge(w_turned, n + 1)
                    act.copy(wT[:, k, m * D:(m + 1) * D], bank[n][:, 0:D]).then_inc(w_kept, 1)

            def keep_row(t):
                s = t % 2
                if t >= 2:
                    act.wait_ge(h_turned, t - 1)
                act.wait_ge(h_normed, t + 1)
                act.copy(h_row[s], node_h[:, t, :]).then_inc(row_ready, 1)

            def keep_hT(t):
                s = t % 2
                if t >= 2:
                    act.wait_ge(projected, t - 1)
                act.wait_ge(h_turned, t + 1)
                act.copy(hT[s].rearrange("p k c -> p (k c)"), bank[s][:, 0:2 * P]).then_inc(hT_ready, 1)

            act.wait_ge(consts_made, 4)
            roots = 0
            for kind, piece, at in first_pass():
                if kind == "norm" and piece in (1, 3):
                    roots += 1
                    act.wait_ge(var_ready, roots)
                    tiles = slice(at * TB, (at + 1) * TB)
                    act.activation(sd[:, tiles], mv[:, tiles, 1], ACT.Sqrt, bias=epsc[:, 0:1]).then_inc(sd_ready, 1)
                    if roots == 2:
                        keep_weights()
                elif kind == "tile":
                    keep_row(at)
                    if at:
                        keep_hT(at - 1)
            keep_hT(NT - 1)

            def place_picks(g, b):
                for n in range(J):
                    ins = act.activation(pick_diag[b][:, n, :], ident[:, :], ACT.Copy,
                                         scale=pick[:, bass.ds(g * J + n, 1)])
                ins.then_inc(pick_ready, 1)

            def tanh_group(g, b, few, least):
                q = b % 2
                if least >= 2:
                    act.wait_ge(scored, g - 1)
                act.wait_ge(z_ready, g + 1)
                act.activation(th[q], zT[q], ACT.Tanh, scale=0.5).then_inc(tanh_ready, 1)
                if few:
                    place_picks(g + 2, (b + 2) % R)

            def exp_group(g, b, least):
                q = b % 2
                if least >= 2:
                    act.wait_ge(rec_stored[q], (g - q) * 8)
                act.wait_ge(diff_ready, g + 1)
                act.activation(wgt[:, :, :], diff[:, :, :], ACT.Exp).then_inc(wgt_ready, 1)
                act.copy(rec[q][:, :, ACC:REC].rearrange("p j h -> p h j"), smax[:, :, 1:M1]).then_inc(side_ready, 1)
                if least >= 2:
                    act.wait_ge(hot_used, g - 1)
                for j in range(J):
                    ins = act.activation(hot_low[q][:, j, :], iota_f[:, :], ACT.Square,
                                         bias=minus_low[:, bass.ds(g * J + j, 1)])
                ins.then_inc(squares_ready, 1)
                act.wait_ge(squares_ready, g + 1)
                act.activation(hot_low[q][:, :, :], hot_low[q][:, :, :], ACT.Relu, scale=-2.0, bias=ones[:, 0:1]).then_inc(low_ready, 1)

            def weigh_edges(few):
                if few:
                    act.wait_ge(consts_made, 11)
                    for g in range(2):
                        place_picks(g, g)
                edge_groups(act, lambda g, b, least: tanh_group(g, b, few, least), exp_group)
            by_nodes_a_group(act, weigh_edges)
            act.wait_ge(lane_moves, 1)
            act.activation(lane_exp, lane_exp, ACT.Exp).then_inc(lane_moved, 1)
            for c in range(NBATCH + 1):
                if c < NBATCH:
                    act.wait_ge(moves_ready, c + 1)
                    act.activation(moved, moves, ACT.Exp).then_inc(moved_ready, 1)
                    act.wait_ge(u_ready, c + 1)
                    act.activation(u_th, u_sb, ACT.Tanh, scale=0.5).then_inc(u_tanh, 1)
                if c:
                    tiles = slice((c - 1) * TB, c * TB)
                    act.wait_ge(y_var_ready, c)
                    act.activation(sd[:, tiles], mv[:, tiles, 1], ACT.Sqrt, bias=epsc[:, 0:1]).then_inc(y_sd_ready, 1)
                    act.wait_ge(y_turned, c)
                    if c > 1:
                        act.wait_ge(gated, c - 1)
                    act.copy(yT, yT_ps).then_inc(yT_ready, 1)
            act.wait_ge(gap_ready, 1)
            act.activation(top_w[:, 1, :], top_w[:, 1, :], ACT.Exp).then_inc(gap_exp, 1)
            act.wait_ge(routing_done, 1)

            for c in range(NBATCH):
                if c:
                    act.wait_ge(b2_ready, c)
                act.wait_ge(share_turned, c + 1)
                act.copy(share_t, psum[0:NE, 0:TB * P]).then_inc(share_kept, 1)

            def keep_tokT(i, b, again):
                if again:
                    act.wait_ge(hidden, i - 1)
                act.wait_ge(tok_turned, i + 1)
                act.copy(tokT[b].rearrange("p k c -> p (k c)"), bank[b][:, 0:2 * P]).then_inc(tokT_ready, 1)

            keep_tokT(0, 0, False)

            def act_step(i, b, least, last):
                if not last:
                    keep_tokT(i + 1, 1 - b, least >= 1)
                act.wait_ge(hidden, i + 1)
                if least >= 2:
                    act.wait_ge(expert_done, i - 1)
                for f in range(FB):
                    ins = act.activation(hidT[b][:, f, :], bank[2 + b][:, f * P:(f + 1) * P], ACT.Relu,
                                         bias=b1_of[:, f, bass.ds(i, 1)])
                ins.then_inc(hidT_ready, 1)
            expert_tiles(act, act_step)

            for c in range(NBATCH):
                act.wait_ge(y_var, c + 1)
                act.activation(sd[:, c * TB:(c + 1) * TB], mv[:, c * TB:(c + 1) * TB, 1], ACT.Sqrt,
                               bias=epsc[:, 0:1]).then_inc(y_sd, 1)

        @block.vector
        def _(dve):
            n0 = [0]

            def link(ins):
                n0[0] += 1
                ins.then_inc(p0, 1)
                dve.wait_ge(p0, n0[0])

            def tile_stats(v, tiles):
                for t in tiles:
                    ins = dve.bn_stats(stats[:, t, :], v[:, t, :])
                link(ins)
                for t in tiles:
                    ins = dve.bn_aggr(mv[:, t, :], stats[:, t, :])
                ins.then_inc(var_ready, 1)

            def normalize(v, to, tiles, roots):
                dve.wait_ge(sd_ready, roots)
                link(dve.reciprocal(rstd[:, tiles.start:tiles.stop], sd[:, tiles.start:tiles.stop]))
                for t in tiles:
                    ins = dve.tensor_scalar(to[:, t, :], v[:, t, :], mv[:, t, 0:1], rstd[:, t:t + 1],
                                            ALU.subtract, ALU.mult)
                return ins

            def add_bias(t):
                s = t % 2
                dve.wait_ge(projected, t + 1)
                if t >= 2:
                    dve.wait_ge(stage_stored[s], t // 2 * 32)
                dve.tensor_tensor(stage[s][:, 0:2 * D], bank[2 + 2 * s][:, :], bias3[:, 0:2 * D], ALU.add)
                dve.tensor_tensor(stage[s][:, 2 * D:3 * D], bank[3 + 2 * s][:, 0:D], bias3[:, 2 * D:3 * D],
                                  ALU.add).then_inc(stage_ready, 1)

            def edge_flags():
                dve.wait_ge(edges_loaded, 16 * 6)
                link(dve.memset(same[:, 0:1], 0.0))
                link(dve.memset(same[:, COLS:], 0.0))
                link(dve.tensor_tensor(same[:, 1:COLS], dst_all[:, 1:COLS], dst_all[:, 0:COLS - 1], ALU.is_equal))
                low_f = thf[:, 0:COLS]
                low_i = low_f.bitcast(I32)
                link(dve.tensor_single_scalar(low_i, dst_all[:, 0:COLS], P - 1, op=ALU.bitwise_and))
                link(dve.tensor_copy(minus_low[:, :], low_i))
                link(dve.tensor_scalar(minus_low[:, :], minus_low[:, :], -1.0, None, ALU.mult))
                link(dve.tensor_single_scalar(low_i, dst_all[:, 0:COLS], 7, op=ALU.arith_shift_right))
                link(dve.tensor_copy(dst_high[:, :], low_i))
                dve.wait_ge(consts_made, 11)
                link(dve.tensor_copy(iota_bf[:, :], iota_f[:, :]))
                dve.wait_ge(consts_loaded, 16 * 4)
                dve.wait_ge(attn_masked, 3)
                link(dve.tensor_tensor(attn_head[:, :, :], attn_head[:, :, :],
                                       attn_col[:, :].unsqueeze(2).to_broadcast([P, KB, H]), ALU.mult))
                link(dve.memset(seg_mask[:, :], -BIG))
                link(dve.memset(smax[:, :, :], 0.0))
                link(dve.memset(rec[1], 0.0))

                dve.wait_ge(prev_loaded, 16)
                dve.tensor_tensor(nflag[:, 1, 0:1], dst_all[:, 0:1], prev_dst[:, :], ALU.is_equal)
                link(dve.tensor_reduce(nflag[:, 2, 0:1], same[:, 1:COLS], AX.X, ALU.min))
                link(dve.tensor_tensor(chain[:, :], nflag[:, 1, 0:1], nflag[:, 2, 0:1], ALU.mult))

                s4 = same[:, 0:COLS].rearrange("p (g j) -> p g j", j=J)
                p4 = pick[:, 0:COLS].rearrange("p (g j) -> p g j", j=J)
                link(dve.tensor_copy(p4[:, :, 0], s4[:, :, 1]))
                link(dve.tensor_tensor(p4[:, :, 2], s4[:, :, 1], s4[:, :, 2], ALU.mult))
                for k in (0, 2):
                    link(dve.tensor_scalar(p4[:, :, k + 1], p4[:, :, k], -1.0, 1.0, ALU.mult, ALU.add))
                link(dve.memset(pick[:, COLS:], 0.0))
                link(dve.tensor_tensor(low_f[:, 0:GROUPS], s4[:, :, 1], s4[:, :, 2], ALU.add))
                link(dve.tensor_tensor(low_f[:, 0:GROUPS], low_f[:, 0:GROUPS], s4[:, :, 3], ALU.add))
                link(dve.tensor_reduce(span_part[:, :], low_f[:, 0:GROUPS], AX.X, ALU.min))
                dve.tensor_scalar(span_part[:, :], span_part[:, :], 2.0, None, ALU.is_ge).then_inc(span_parts, 1)
                dve.memset(zeros, 0.0).then_inc(zeros_made, 1)


            for kind, piece, at in first_pass():
                if kind == "tile":
                    if at == 0:
                        dve.wait_ge(consts_loaded, 16 * 4)
                    add_bias(at)
                    continue
                tiles = range(at * TB, (at + 1) * TB)
                if piece == 0:
                    dve.wait_ge(x_loaded[at], 16 if at < NBATCH - 1 else 32)
                    tile_stats(node_x, tiles)
                elif piece == 1:
                    link(normalize(node_x, node_h, tiles, 2 * at + 1))
                elif piece == 2:
                    tile_stats(node_h, tiles)
                else:
                    normalize(node_h, node_h, tiles, 2 * at + 2).then_inc(h_normed, TB)
                if (piece, at) == (3, 3):
                    edge_flags()

            dve.wait_ge(span_summed, 1)
            link(dve.tensor_scalar(few_nodes[:, :], bank[7][:, 0:1], P - 0.5, None, ALU.is_ge))
            dve.drain().then_inc(span_known, 1)
            dve.wait_ge(stage_stored[0], 16 * 2 * ((NT + 1) // 2))
            dve.wait_ge(stage_stored[1], 16 * 2 * (NT // 2))
            for b in range(R):
                link(dve.tensor_copy(idx_src[b][:, :], src_all[:, b * J:(b + 1) * J]))
                dve.tensor_copy(idx_dst[b][:, :], dst_all[:, b * J:(b + 1) * J]).then_inc(idx_ready, 1)
            dve.wait_ge(idx_ready, R)

            def silu_group(g, b):
                q = b % 2
                dve.wait_ge(tanh_ready, g + 1)
                dve.scalar_tensor_tensor(out=th[q], in0=th[q], scalar=1.0, in1=zT[q],
                                         op0=ALU.add, op1=ALU.mult).then_inc(silu_ready, 1)

            STEPS = 2 + 4 + J + 3
            n = [0]

            def mark(ins):
                n[0] += 1
                ins.then_inc(e0, 1)
                return n[0]

            def done(g, count):
                dve.wait_ge(e0, g * STEPS + 2 + count)

            def cols(v, at, n):
                return v[:, bass.ds(at, n)]

            def open_group(g):
                mark(dve.tensor_scalar(seg_mask[:, 0:H * M1].rearrange("p (h j) -> p h j", h=H)[:, :, 1:M1],
                                       cols(same, g * J, J).unsqueeze(1).to_broadcast([P, H, J]),
                                       BIG, -BIG, ALU.mult, ALU.add))
                mark(dve.tensor_copy(score[:, :, 0:1], smax[:, :, J:M1]))

            def maxima_group(g, b, least):
                q = b % 2
                n[0] = 0
                dve.wait_ge(scored, g + 1)
                dve.tensor_copy(score[:, :, 1:M1].rearrange("p h j -> p j h"),
                                score_ps[q].rearrange("p (j h) -> p j h", h=H)).then_inc(score_read, 1)
                done(g, 0)
                dve.wait_ge(score_read, g + 1)
                at = mark(dve.tensor_tensor_scan(fmax[:, :], seg_mask[:, 0:H * M1],
                                                 score[:, :, :].rearrange("p h j -> p (h j)"), 0.0, ALU.add, ALU.max))
                done(g, at)
                if least >= 1:
                    dve.wait_ge(side_ready, g)
                at = mark(dve.tensor_tensor_scan(smax[:, :, :].rearrange("p h j -> p (h j)")[:, ::-1],
                                                 seg_mask[:, 1:H * M1 + 1][:, ::-1],
                                                 fmax[:, ::-1], 0.0, ALU.add, ALU.max))
                done(g, at)
                dve.tensor_tensor(diff[:, :, :], score[:, :, :], smax[:, :, :], ALU.subtract).then_inc(diff_ready, 1)

            def sum_group(g, b, least):
                q = b % 2
                col = g * J
                dve.wait_ge(wgt_ready, g + 1)
                mark(dve.tensor_tensor(msg[:, :, 0:D].rearrange("p j (h f) -> p j h f", h=H),
                                       sv[b][:, :, D:2 * D].rearrange("p j (h f) -> p j h f", h=H),
                                       wgt[:, :, 1:M1].rearrange("p h j -> p j h").unsqueeze(3).to_broadcast([P, J, H, FH]),
                                       ALU.mult))
                mark(dve.tensor_copy(msg[:, :, D:ACC], wgt[:, :, 1:M1].rearrange("p h j -> p j h")))
                if least >= 1:
                    dve.wait_ge(rec_ready, g)
                mark(dve.tensor_tensor(carry[:, D:ACC], rec[1 - q][:, J - 1, D:ACC],
                                       wgt[:, :, 0], ALU.mult))
                placed = mark(dve.tensor_tensor(carry[:, 0:D].rearrange("p (h f) -> p h f", h=H),
                                                rec[1 - q][:, J - 1, 0:D].rearrange("p (h f) -> p h f", h=H),
                                                wgt[:, :, 0:1].to_broadcast([P, H, FH]), ALU.mult))
                if least >= 2:
                    dve.wait_ge(hot_used, g - 1)
                    dve.wait_ge(rec_stored[q], (g - q) * 8)

                def high_half(a, z):
                    return dve.tensor_tensor(hot_high[q][:, a:z, :],
                                             iota_bf[:, 0:NT].unsqueeze(1).to_broadcast([P, z - a, NT]),
                                             cols(dst_high, col + a, z - a).unsqueeze(2).to_broadcast([P, z - a, NT]),
                                             ALU.is_equal)

                mark(high_half(0, J // 2))
                for j in range(J):
                    done(g, placed)
                    ins = dve.scalar_tensor_tensor(
                        out=rec[q][:, j, 0:ACC], in0=carry[:, :] if j == 0 else rec[q][:, j - 1, 0:ACC],
                        scalar=cols(same, col + j, 1), in1=msg[:, j, :], op0=ALU.mult, op1=ALU.add)
                    if j < J - 1:
                        placed = mark(ins)
                    else:
                        ins.then_inc(rec_ready, 1)
                    if j == 0:
                        high_half(J // 2, J).then_inc(hot_ready, 1)
                    if j == 1:
                        mark(dve.tensor_copy(idx_src[b][:, :], cols(src_all, col + R * J, J)))
                        dve.tensor_copy(idx_dst[b][:, :], cols(dst_all, col + R * J, J)).then_inc(idx_ready, 1)
                    if j == 2:
                        dve.wait_ge(diff_ready, g + 1)
                        open_group(g + 1)
                assert n[0] == STEPS, n[0]

            def edge_step(g, b, least):
                if least >= 1:
                    maxima_group(g - 1, (b - 1) % R, least - 1)
                silu_group(g, b)
                if least >= 1:
                    sum_group(g - 1, (b - 1) % R, least - 1)
            open_group(0)
            edge_groups(dve, edge_step)
            maxima_group(GROUPS - 1, R - 1, GROUPS - 1)
            sum_group(GROUPS - 1, R - 1, GROUPS - 1)
            dve.wait_ge(rec_ready, GROUPS)

            m0 = [0]

            def link1(ins):
                m0[0] += 1
                ins.then_inc(p1, 1)
                dve.wait_ge(p1, m0[0])

            deg, cum, tot, incl, start, last, lane, has = (nflag[:, k, :] for k in range(8))
            dve.wait_ge(hot_used, GROUPS)
            dve.wait_ge(zeros_stored, 16 * (GROUPS // R - 1))
            dve.tensor_copy(deg, bank[6][:, 0:NT]).then_inc(degrees_kept, 1)
            link1(dve.tensor_copy(chain_wide, chain[:, 0:1].to_broadcast([P, P])))
            dve.drain().then_inc(chain_ready, 1)
            dve.wait_ge(degrees_summed, 1)
            link1(dve.tensor_copy(tot, bank[7][:, 64:64 + NT]))
            link1(dve.tensor_tensor_scan(incl, ones[:, 0:NT], tot, 0.0, ALU.mult, ALU.add))
            link1(dve.tensor_tensor(cum, bank[7][:, 0:NT], incl, ALU.add))
            link1(dve.tensor_tensor(cum, cum, tot, ALU.subtract))
            link1(dve.tensor_tensor(start, cum, deg, ALU.subtract))
            link1(dve.tensor_scalar(last, cum, -1.0, 0.0, ALU.add, ALU.max))
            link1(dve.tensor_scalar(lane, last, 0.5, 1.0 / COLS, ALU.add, ALU.mult))
            link1(dve.tensor_scalar(lane, lane, -0.5, None, ALU.add))
            link1(dve.tensor_scalar(lane, lane, 8388608.0, None, ALU.add))
            link1(dve.tensor_scalar(lane, lane, -8388608.0, None, ALU.add))
            link1(dve.scalar_tensor_tensor(out=start, in0=lane, scalar=float(COLS), in1=start,
                                           op0=ALU.mult, op1=ALU.is_gt))
            link1(dve.tensor_scalar(lane, lane, -1.0 - P, None, ALU.add))
            link1(dve.tensor_tensor(lane, lane, start, ALU.mult))
            link1(dve.tensor_scalar(lane, lane, float(P), None, ALU.add))
            dve.tensor_copy(idx_last[:, :], last).then_inc(node_idx_ready, 1)
            dve.tensor_copy(idx_tail[:, :], lane).then_inc(node_idx_ready, 1)
            link1(dve.tensor_scalar(has, deg, 1.0, None, ALU.min))

            dve.wait_ge(tails_turned, 1)
            dve.tensor_copy(mT, bank[0][0:H, 0:P])
            dve.tensor_copy(dT, bank[0][0:H, P:2 * P])
            dve.tensor_copy(aT.rearrange("p k l -> p (k l)"), bank[1][:, 0:2 * P])
            link1(dve.tensor_copy(chainT, bank[0][:, 2 * P:3 * P]))
            link1(dve.tensor_scalar(lane_mask, chainT, BIG, -BIG, ALU.mult, ALU.add))
            link1(dve.tensor_tensor_scan(lane_max, lane_mask[0:H, :], mT, 0.0, ALU.add, ALU.max))
            dve.memset(lane_exp[:, P:P + 1], 0.0)
            dve.tensor_tensor(lane_exp[:, 0:P], mT, lane_max, ALU.subtract)
            link1(dve.tensor_tensor(lane_exp[:, P + 1:2 * P], lane_max[:, 0:P - 1], lane_max[:, 1:P], ALU.subtract))
            dve.tensor_scalar(lane_exp[:, P:2 * P], lane_exp[:, P:2 * P], 0.0, None, ALU.min).then_inc(lane_moves, 1)
            dve.wait_ge(lane_moved, 1)
            dve.tensor_tensor(lane_exp[:, P:2 * P], lane_exp[:, P:2 * P], chainT[0:H, :], ALU.mult).then_inc(lane_factors, 1)
            dve.wait_ge(lane_factors, 1)
            link1(dve.tensor_tensor(dT, dT, lane_exp[:, 0:P], ALU.mult))
            link1(dve.tensor_tensor_scan(lane_den, lane_exp[:, P:2 * P], dT, 0.0, ALU.mult, ALU.add))
            dve.wait_ge(factors_wide, 1)
            for k in range(KB):
                ins = dve.tensor_tensor(aT[:, k, :], aT[:, k, :], bank[2 + k][:, 0:P], ALU.mult)
            link1(ins)
            for k in range(KB):
                ins = dve.tensor_tensor_scan(accT[:, k, :], bank[2 + k][:, P:2 * P], aT[:, k, :], 0.0, ALU.mult, ALU.add)
            ins.then_inc(lanes_summed, 1)
            dve.wait_ge(tails_back, 1)
            dve.tensor_copy(tail_sb, bank[4][:, 0:REC]).then_inc(tail_ready, 1)
            link1(dve.memset(no_tail, 0.0))
            dve.memset(no_tail[:, ACC:REC], -BIG).then_inc(tail_ready, 1)
            dve.wait_ge(tail_ready, 2)

            k0 = [0]

            def link2(ins):
                k0[0] += 1
                ins.then_inc(p2, 1)
                dve.wait_ge(p2, k0[0])

            def join(c):
                b = c % 2
                own, before = node_rec[b], node_car[b]
                dve.wait_ge(node_gathered[b], 16 * 2 * TB * (c // 2 + 1))
                link1(dve.tensor_tensor(nmax, own[:, :, ACC:REC], before[:, :, ACC:REC], ALU.max))
                dve.tensor_tensor(moves[:, :, 0:H], own[:, :, ACC:REC], nmax, ALU.subtract)
                dve.tensor_tensor(moves[:, :, H:2 * H], before[:, :, ACC:REC], nmax, ALU.subtract).then_inc(moves_ready, 1)
                dve.wait_ge(moved_ready, c + 1)
                dve.tensor_tensor(own[:, :, D:ACC], own[:, :, D:ACC], moved[:, :, 0:H], ALU.mult)
                link1(dve.tensor_tensor(before[:, :, D:ACC], before[:, :, D:ACC], moved[:, :, H:2 * H], ALU.mult))
                link1(dve.tensor_tensor(nden, own[:, :, D:ACC], before[:, :, D:ACC], ALU.add))
                link1(dve.reciprocal(nden, nden))
                link1(dve.tensor_tensor(nden, nden, has[:, c * TB:(c + 1) * TB].unsqueeze(2).to_broadcast([P, TB, H]), ALU.mult))
                dve.tensor_tensor(moved[:, :, 0:H], moved[:, :, 0:H], nden, ALU.mult)
                link1(dve.tensor_tensor(moved[:, :, H:2 * H], moved[:, :, H:2 * H], nden, ALU.mult))
                for rows, fac in ((own, moved[:, :, 0:H]), (before, moved[:, :, H:2 * H])):
                    v = rows[:, :, 0:D].rearrange("p t (h f) -> p t h f", h=H)
                    ins = dve.tensor_tensor(v, v, fac.unsqueeze(3).to_broadcast([P, TB, H, FH]), ALU.mult)
                link1(ins)
                dve.tensor_tensor(u_sb, own[:, :, 0:D], before[:, :, 0:D], ALU.add).then_inc(node_used, 1)
                dve.wait_ge(node_used, c + 1)
                dve.tensor_tensor(u_sb, u_sb, node_h[:, c * TB:(c + 1) * TB, :], ALU.add).then_inc(u_ready, 1)

            def residual(c):
                dve.wait_ge(u_tanh, c + 1)
                link1(dve.scalar_tensor_tensor(out=u_th, in0=u_th, scalar=1.0, in1=u_sb, op0=ALU.add, op1=ALU.mult))
                v = node_x[:, c * TB:(c + 1) * TB, :]
                dve.scalar_tensor_tensor(out=v, in0=u_th, scalar=0.5, in1=v, op0=ALU.mult, op1=ALU.add).then_inc(x2_ready, 1)
                dve.wait_ge(x2_ready, c + 1)
                for t in range(c * TB, (c + 1) * TB):
                    ins = dve.bn_stats(stats[:, t, :], node_x[:, t, :])
                link1(ins)
                for t in range(c * TB, (c + 1) * TB):
                    ins = dve.bn_aggr(mv[:, t, :], stats[:, t, :])
                ins.then_inc(y_var_ready, 1)

            def expert_input(c):
                dve.wait_ge(y_sd_ready, c + 1)
                link1(dve.reciprocal(rstd[:, c * TB:(c + 1) * TB], sd[:, c * TB:(c + 1) * TB]))
                for t in range(c * TB, (c + 1) * TB):
                    ins = dve.tensor_scalar(node_h[:, t, :], node_x[:, t, :], mv[:, t, 0:1], rstd[:, t:t + 1],
                                            ALU.subtract, ALU.mult)
                ins.then_inc(y_ready, 1)

            def top_two(c):
                dve.wait_ge(gated, c + 1)
                tiles = range(c * TB, (c + 1) * TB)
                dve.tensor_tensor(logits[:, c * TB:(c + 1) * TB, :],
                                  bank[5][:, 0:TB * NE].rearrange("p (t e) -> p t e", t=TB),
                                  gate_b_sb.unsqueeze(1).to_broadcast([P, TB, NE]), ALU.add).then_inc(logits_ready, 1)
                dve.wait_ge(logits_ready, c + 1)
                for t in tiles:
                    ins = dve.max(top8[:, t, :], logits[:, t, :])
                link1(ins)
                for t in tiles:
                    ins = dve.max_index(top8_at[:, t, :], top8[:, t, :], logits[:, t, :])
                return ins

            dve.wait_ge(gate_loaded, 32)
            for c in range(NBATCH + 2):
                if 1 <= c <= NBATCH:
                    residual(c - 1)
                if c < NBATCH:
                    join(c)
                if 1 <= c <= NBATCH:
                    expert_input(c - 1)
                if c >= 2:
                    ins = top_two(c - 2)
            link1(ins)
            link2(dve.tensor_tensor(before_bf[:, :], upper[:, :], ident[:, :], ALU.subtract))
            link2(dve.tensor_copy(ones_bf[:, :], ones[:, :]))
            dve.tensor_tensor(top_w[:, 1, :], top8[:, :, 1], top8[:, :, 0], ALU.subtract).then_inc(gap_ready, 1)
            for k in range(2):
                ins = dve.tensor_copy(choice[:, k, :], top8_at[:, :, k])
            link2(ins)
            for k in range(2):
                link2(dve.tensor_tensor(chosen[:, :, k * NT:(k + 1) * NT],
                                        iota_f[:, 0:NE].unsqueeze(2).to_broadcast([P, NE, NT]),
                                        choice[:, k, :].unsqueeze(1).to_broadcast([P, NE, NT]), ALU.is_equal))
            dve.tensor_copy(chosen_bf, chosen.rearrange("p e s -> p (e s)")).then_inc(chosen_ready, 1)
            dve.wait_ge(gap_exp, 1)
            link2(dve.tensor_scalar(top_w[:, 0, :], top_w[:, 1, :], 1.0, None, ALU.add))
            link2(dve.reciprocal(top_w[:, 0, :], top_w[:, 0, :]))
            link2(dve.tensor_tensor(top_w[:, 1, :], top_w[:, 1, :], top_w[:, 0, :], ALU.mult))
            link2(dve.memset(restart, 1.0))
            link2(dve.memset(restart.rearrange("p (e s) -> p e s", e=NE)[:, :, 0:1], 0.0))
            dve.wait_ge(tile_sums, 1)
            q = W // 4
            for k in range(4):
                ins = dve.tensor_copy(taken[:, k * q:(k + 1) * q], bank[k][:, 0:q])
            ins.then_inc(tile_sums_kept, 1)
            dve.wait_ge(tile_sums_kept, 1)
            link2(dve.tensor_tensor_scan(running, restart, taken, 0.0, ALU.mult, ALU.add))
            need, upto, base = ends[:, 0, :], ends[:, 1, :], ends[:, 2, :]
            need_i = ends[:, 3, :].bitcast(I32)
            totals = running.rearrange("p (e s) -> p e s", e=NE)[:, :, S2 - 1]
            link2(dve.tensor_scalar(need, totals, float(P - 1), None, ALU.add))
            link2(dve.tensor_copy(need_i, need))
            link2(dve.tensor_single_scalar(need_i, need_i, 7, op=ALU.arith_shift_right))
            link2(dve.tensor_copy(need, need_i))
            link2(dve.tensor_tensor_scan(upto, ones[:, 0:NE], need, 0.0, ALU.mult, ALU.add))
            link2(dve.tensor_tensor(base, upto, need, ALU.subtract))
            link2(dve.tensor_scalar(base, base, float(P), None, ALU.mult))
            link2(dve.tensor_tensor(running, running, taken, ALU.subtract))
            dve.wait_ge(ranks, 1)
            for k in range(4):
                ins = dve.tensor_tensor(place[:, k * q:(k + 1) * q], bank[4 + k][:, 0:q], running[:, k * q:(k + 1) * q], ALU.add)
            link2(ins)
            place3 = place.rearrange("p (e s) -> p e s", e=NE)
            link2(dve.tensor_tensor(place3, place3, base.unsqueeze(2).to_broadcast([P, NE, S2]), ALU.add))
            link2(dve.tensor_tensor(place3, place3, chosen, ALU.mult))
            link2(dve.tensor_reduce(taken[:, 0:S2], place3.rearrange("p e s -> p s e"), AX.X, ALU.add))
            dve.tensor_copy(slot[:, :], taken[:, 0:S2]).then_inc(slot_ready, 1)
            dve.wait_ge(slot_ready, 1)
            ended = restart[:, 0:MT * 8]
            link2(dve.memset(tile_of, 0.0))
            for k in range(2):
                e3 = restart[:, 0:MT * 8].rearrange("p (i e) -> p i e", e=8)
                link2(dve.tensor_tensor(e3, iota_f[:, 0:MT].unsqueeze(2).to_broadcast([P, MT, 8]),
                                        upto[:, 8 * k:8 * k + 8].unsqueeze(1).to_broadcast([P, MT, 8]), ALU.is_ge))
                link2(dve.tensor_reduce(taken[:, 200:200 + MT], e3, AX.X, ALU.add))
                link2(dve.tensor_tensor(tile_of, tile_of, taken[:, 200:200 + MT], ALU.add))
            link2(dve.tensor_scalar(tile_of, tile_of, float(NE - 1), None, ALU.min))
            link2(dve.tensor_copy(tile_expert[:, :], tile_of))
            dve.tensor_scalar(e_hot, tile_of[0:NE, :], iota_p[0:NE, 0:1], None, ALU.is_equal).then_inc(e_hot_ready, 1)
            c3 = fd1f[:, 0:NT * NE].rearrange("p (e t) -> p e t", e=NE)
            c4 = fd1f[:, NT * NE:2 * NT * NE].rearrange("p (e t) -> p e t", e=NE)
            for k, v in enumerate((c3, c4)):
                link2(dve.tensor_tensor(v, chosen[:, :, k * NT:(k + 1) * NT],
                                        top_w[:, k, :].unsqueeze(1).to_broadcast([P, NE, NT]), ALU.mult))
            link2(dve.tensor_tensor(share.rearrange("p t e -> p e t"), c3, c4, ALU.add))
            dve.wait_ge(b1_turned, 1)
            dve.tensor_copy(b1_of[:, :, :].rearrange("p k i -> p (k i)"), bank[0][:, 0:FB * MT]).then_inc(routing_done, 1)

            dve.wait_ge(ffn_loaded, 16 * 4)
            link2(dve.tensor_tensor(node_x[:, :, :], node_x[:, :, :],
                                    beta_sb.unsqueeze(1).to_broadcast([P, NT, D]), ALU.add))
            for c in range(NBATCH):
                dve.wait_ge(b2_ready, c + 1)
                dve.wait_ge(tokens_sent[c], 16 * 2 * TB)
                v = node_h[:, c * TB:(c + 1) * TB, :]
                dve.tensor_tensor(v, v, b2_ps.rearrange("p (t d) -> p t d", t=TB), ALU.add).then_inc(base_ready, 1)
            dve.wait_ge(base_ready, NBATCH)

            def keep_eout(i, b, least, last):
                dve.wait_ge(expert_done, i + 1)
                if least >= 2:
                    dve.wait_ge(eout_stored[b], (i - b) * 8)
                dve.tensor_copy(eout[b], bank[4 + b][:, 0:D]).then_inc(eout_ready, 1)
            expert_tiles(dve, keep_eout)

            for c in range(NBATCH + 1):
                if c < NBATCH:
                    g0, g1 = got[c % GR]
                    tiles = range(c * TB, (c + 1) * TB)
                    dve.wait_ge(out_gathered[c % GR], 16 * 2 * TB * (c // GR + 1))
                    for k, t in enumerate(tiles):
                        ins = dve.scalar_tensor_tensor(out=g1[:, k, :], in0=g1[:, k, :], scalar=top_w[:, 1, t:t + 1],
                                                       in1=node_h[:, t, :], op0=ALU.mult, op1=ALU.add)
                    link2(ins)
                    for k, t in enumerate(tiles):
                        ins = dve.scalar_tensor_tensor(out=g0[:, k, :], in0=g0[:, k, :], scalar=top_w[:, 0, t:t + 1],
                                                       in1=g1[:, k, :], op0=ALU.mult, op1=ALU.add)
                    link2(ins)
                    for k, t in enumerate(tiles):
                        ins = dve.bn_stats(stats[:, t, :], g0[:, k, :])
                    link2(ins)
                    for t in tiles:
                        ins = dve.bn_aggr(mv[:, t, :], stats[:, t, :])
                    ins.then_inc(y_var, 1)
                if c:
                    g0 = got[(c - 1) % GR][0]
                    tiles = range((c - 1) * TB, c * TB)
                    dve.wait_ge(y_sd, c)
                    link2(dve.reciprocal(rstd[:, tiles.start:tiles.stop], sd[:, tiles.start:tiles.stop]))
                    for k, t in enumerate(tiles):
                        ins = dve.scalar_tensor_tensor(out=g0[:, k, :], in0=g0[:, k, :], scalar=mv[:, t, 0:1],
                                                       in1=gamma_sb, op0=ALU.subtract, op1=ALU.mult)
                    link2(ins)
                    for k, t in enumerate(tiles):
                        ins = dve.scalar_tensor_tensor(out=g0[:, k, :], in0=g0[:, k, :], scalar=rstd[:, t:t + 1],
                                                       in1=node_x[:, t, :], op0=ALU.mult, op1=ALU.add)
                    ins.then_inc(out_ready, 1)


_NAMES = {"x": "x", "src": "src", "dst": "dst", "Wsrc": "L0_gnn_Wsrc", "bsrc": "L0_gnn_bsrc", "Wdst": "L0_gnn_Wdst",
          "bdst": "L0_gnn_bdst", "Wval": "L0_gnn_Wval", "bval": "L0_gnn_bval", "attn": "L0_gnn_attn",
          "gate_w": "L0_ffn_gate_w", "gate_b": "L0_ffn_gate_b", "w1": "L0_ffn_w1", "b1": "L0_ffn_b1",
          "w2": "L0_ffn_w2", "b2": "L0_ffn_b2", "gamma": "L0_ffn_gamma", "beta": "L0_ffn_beta"}


def kernel(**inputs):
    import numpy as _np
    import concourse.bacc as _bacc
    from concourse.bass_utils import run_bass_kernel_spmd as _run

    nc = _bacc.Bacc("TRN2", target_bir_lowering=False, num_devices=1)
    arrays, args = {}, {}
    for short, name in _NAMES.items():
        a = _np.ascontiguousarray(inputs[name])
        arrays[f"in_{short}"] = a
        args[short] = nc.dram_tensor(f"in_{short}", a.shape, mybir.dt.from_np(a.dtype), kind="ExternalInput").ap()
    shape = inputs["x"].shape
    out = nc.dram_tensor("out_0", shape, F32, kind="ExternalOutput").ap()
    build_gnn_moe(nc, out=out, **args)
    r = _run(nc, [arrays], core_ids=[0])
    return r.results[0]["out_0"]
```

```python
from contextlib import ExitStack

import concourse.bass as bass
from concourse import mybir

F32 = mybir.dt.float32
BF16 = mybir.dt.bfloat16
I32 = mybir.dt.int32
U32 = mybir.dt.uint32
ALU = mybir.AluOpType
ACT = mybir.ActivationFunctionType
AX = mybir.AxisListType

P = 128
BIG = 1e38
EPS = 1e-5


def build_gnn_moe(nc, x, src, dst, Wsrc, bsrc, Wdst, bdst, Wval, bval, attn,
                  gate_w, gate_b, w1, b1, w2, b2, gamma, beta, out):
    N, D = x.shape
    E = src.shape[0]
    H = attn.shape[1]
    FH = D // H
    NE, _, F = w1.shape
    KB = D // P
    FB = F // P

    NT = -(-N // P)
    LAST = N - (NT - 1) * P
    J = 4
    R = 4
    COLS = -(-E // (P * R * J)) * R * J
    GROUPS = COLS // J
    REC = D + 2 * H
    ACC = D + H
    M1 = J + 1
    TB = 7
    NBATCH = NT // TB
    S2 = 2 * NT
    WR = 3
    ER = 3
    GR = 3
    MT = 2 * (-(-(2 * NT * P + NE * (P - 1)) // (2 * P)))
    assert NT == TB * NBATCH and (NT - 3) % 2 == 0 and GROUPS % R == 0 and D == 256 and F == 512

    with ExitStack() as ctx:
        def sb(name, shape, dt=F32):
            return ctx.enter_context(nc.sbuf_tensor(name, shape, dt))

        def sem(name):
            return ctx.enter_context(nc.semaphore(name))

        def dram(name, shape, dt=F32):
            return nc.dram_tensor(name, shape, dt, kind="Internal").ap()

        sv_table = dram("sv_table", [NT * P, 2 * D])
        d_table = dram("d_table", [NT * P, D])
        d_pairs = dram("d_pairs", [NT * P, 2 * D])
        records = dram("records", [COLS * P, REC])
        lane_tails = dram("lane_tails", [P + 1, REC])
        expert_in = dram("expert_in", [MT * P, D + 1])
        results = dram("results", [(MT + S2) * P, D])

        node_x = sb("node_x", [P, NT, D])
        node_rows = sb("node_rows", [P, NT, D + 1])
        node_h = node_rows[:, :, 0:D]

        src_all = sb("src_all", [P, COLS + R * J], I32)
        dst_all = sb("dst_all", [P, COLS + R * J], I32)
        same = sb("same", [P, COLS + J])
        minus_low = sb("minus_low", [P, COLS])
        dst_high = sb("dst_high", [P, COLS], BF16)
        PK = 2 * (J - 1)
        pick = sb("pick", [P, (GROUPS + 3) * PK])
        span_part = sb("span_part", [P, 1])
        few_nodes = sb("few_nodes", [P, 1], I32)
        idx_src = [sb(f"idx_src{b}", [P, J], I32) for b in range(R)]
        idx_dst = [sb(f"idx_dst{b}", [P, J], I32) for b in range(R)]

        arena = sb("arena", [P, 18200])

        def part(at, *shape):
            n = 1
            for d in shape:
                n *= d
            v = arena[:, at:at + n]
            return v if len(shape) == 1 else v.rearrange("p (a b) -> p a b", a=shape[0])

        sv = [part(b * J * 2 * D, J, 2 * D) for b in range(R)]
        fd = [part(8192 + b * J * D, J, D) for b in range(R)]
        more_diag = sb("more_diag", [P, 2, PK - J, P])

        def pick_diag(b, n):
            if n < J:
                return fd[b][:, 2 + n // 2, (n % 2) * P:(n % 2 + 1) * P]
            return more_diag[:, b % 2, n - J, :]
        th = [part(12288, J * D), part(14368, J * D)]
        msg = part(13312, J, ACC)
        rec = [part(16024 + b * J * REC, J, REC) for b in range(2)]
        carry = sb("carry", [P, ACC])
        hot_low = [sb(f"hot_low{b}", [P, J, P], BF16) for b in range(2)]
        hot_high = [sb(f"hot_high{b}", [P, J, NT], BF16) for b in range(2)]
        seg_mask = sb("seg_mask", [P, H * M1 + 1])
        score = sb("score", [P, H, M1])
        fmax = sb("fmax", [P, H * M1])
        smax = sb("smax", [P, H, M1])
        diff = sb("diff", [P, H, M1])
        wgt = sb("wgt", [P, H, M1])

        ident = sb("ident", [P, P])
        iota_p = sb("iota_p", [P, 1])
        iota_f = sb("iota_f", [P, P])
        iota_bf = sb("iota_bf", [P, P], BF16)
        attn_col = sb("attn_col", [P, KB])
        attn_head = sb("attn_head", [P, KB, H])
        stats = sb("stats", [P, NT, 6])
        mv = sb("mv", [P, NT, 2])
        rstd = sb("rstd", [P, NT])
        sd = sb("sd", [P, NT])
        ones_bf = sb("ones_bf", [P, P], BF16)
        before_bf = sb("before_bf", [P, P], BF16)
        upper = sb("upper", [P, P])
        ones = sb("ones", [P, P])
        head_of = sb("head_of", [H, D])
        prev_dst = sb("prev_dst", [P, 1], I32)
        chain = sb("chain", [P, 1])
        nflag = sb("nflag", [P, 8, NT])
        idx_last = sb("idx_last", [P, NT], I32)
        idx_tail = sb("idx_tail", [P, NT], I32)
        top_w = sb("top_w", [P, 2, NT])
        spare_row = sb("spare_row", [P, MT])
        result_row = [sb(f"result_row{w}", [P, 1], I32) for w in range(2 * ER)]
        slot = sb("slot", [P, S2], I32)
        tile_expert = sb("tile_expert", [P, MT], I32)
        b1_of = sb("b1_of", [P, FB, MT])
        epsc = sb("epsc", [P, 1])

        ZC = MT * D // (GROUPS // R - 1)
        assert ZC * (GROUPS // R - 1) == MT * D and ZC % (2 * R) == 0 and ZC // 2 <= 8 * NT
        zeros = nflag[:, :, :].rearrange("p k t -> p (k t)")[:, 0:ZC // 2]

        psum = ctx.enter_context(nc.psum_tensor("psum", [P, 8 * 512], F32))
        bank = [psum[:, 512 * k:512 * (k + 1)] for k in range(8)]
        zT = [psum[:, 1024 * q:1024 * q + J * KB * P] for q in range(2)]
        zT4 = [z.rearrange("p (j k e) -> p j k e", j=J, k=KB) for z in zT]
        score_ps = [bank[4 + q][:, 0:J * H] for q in range(2)]
        degree_ps = bank[6][:, 0:NT]

        sv0f, sv1f, fd0f, fd1f, thf, msgf, rec0f, rec1f = (
            part(at, n) for at, n in ((0, 3584), (3584, 3584), (7168, 1792), (8960, 1792), (10752, 1792),
                                      (12544, 1848), (14392, 1904), (16296, 1904)))
        wT = sv0f[:, 0:KB * 3 * D].rearrange("p (k o) -> p k o", k=KB)
        w_raw = sv0f[:, KB * 3 * D:2 * KB * 3 * D].rearrange("p (m k) -> p m k", k=D)
        bias3 = sv1f[:, 2048:2048 + 3 * D]
        stage = [sv1f[:, 768 * b:768 * b + 768] for b in range(2)]
        hT = [sv1f[:, 1536 + 256 * b:1792 + 256 * b].rearrange("p (k c) -> p k c", k=KB) for b in range(2)]

        h_row = [sv1f[:, 2816 + 256 * b:3072 + 256 * b] for b in range(2)]
        tailT = fd0f
        aT = tailT[:, 0:KB * P].rearrange("p (k l) -> p k l", k=KB)
        mT = tailT[0:H, 256:384]
        dT = tailT[0:H, 384:512]
        chainT = tailT[:, 512:640]
        lane_mask = tailT[:, 640:768]
        lane_max = tailT[0:H, 768:896]
        lane_exp = tailT[0:H, 896:1152]
        lane_den = tailT[0:H, 1152:1280]
        chain_wide = tailT[:, 1280:1408]
        accT = fd1f[:, 0:KB * P].rearrange("p (k l) -> p k l", k=KB)
        tail_sb = msgf[:, 0:REC]
        no_tail = msgf[0:1, REC:2 * REC]
        node_rec = [sv0f[:, 0:TB * REC].rearrange("p (a b) -> p a b", a=TB),
                    sv1f[:, 0:TB * REC].rearrange("p (a b) -> p a b", a=TB)]
        node_car = [rec0f.rearrange("p (a b) -> p a b", a=TB), rec1f.rearrange("p (a b) -> p a b", a=TB)]
        u_sb = fd0f.rearrange("p (a b) -> p a b", a=TB)
        u_th = thf.rearrange("p (a b) -> p a b", a=TB)
        moves = sv0f[:, 1904:2016].rearrange("p (a b) -> p a b", a=TB)
        moved = sv0f[:, 2016:2128].rearrange("p (a b) -> p a b", a=TB)
        nmax = sv0f[:, 2128:2184].rearrange("p (a b) -> p a b", a=TB)
        nden = sv0f[:, 2184:2240].rearrange("p (a b) -> p a b", a=TB)

        yT_ps = psum[:, 0:TB * D]
        yT = fd1f
        W = NE * S2
        chosen = fd0f[:, 0:W].rearrange("p (e s) -> p e s", e=NE)
        taken = fd1f[:, 0:W]
        running = thf[:, 0:W]
        place = sv0f[:, 0:W]
        restart = sv0f[:, W:2 * W]
        chosen_bf = rec0f[:, 0:W // 2].bitcast(BF16)
        logits = sv1f[:, 1904:1904 + NT * NE].rearrange("p (t e) -> p t e", t=NT)
        top8 = msgf[:, 0:8 * NT].rearrange("p (t e) -> p t e", t=NT)
        top8_at = msgf[:, 8 * NT:16 * NT].bitcast(U32).rearrange("p (t e) -> p t e", t=NT)
        choice = msgf[:, 16 * NT:18 * NT].rearrange("p (k t) -> p k t", k=2)
        gate_w_sb = msgf[:, 1000:1000 + KB * NE].rearrange("p (k e) -> p k e", k=KB)
        gate_b_sb = msgf[:, 1032:1048]
        ends = msgf[:, 1050:1050 + 5 * NE].rearrange("p (k e) -> p k e", k=5)
        tile_of = msgf[:, 1140:1140 + MT]
        e_hot = msgf[0:NE, 1260:1260 + MT]
        b1_sb = rec0f[0:NE, 784:784 + F]
        b2_sb = rec0f[0:NE, 1296:1296 + D]
        share = rec1f[:, 0:NT * NE].rearrange("p (t e) -> p t e", t=NT)
        gamma_sb = rec1f[:, 784:784 + D]
        beta_sb = rec1f[:, 1040:1040 + D]
        share_t = fd1f[0:NE, 0:TB * P]
        b2_ps = psum[:, 1024:1024 + TB * D]
        w1_sb = [v[:, 0:KB * F].rearrange("p (k f) -> p k f", k=KB) for v in (sv0f, sv0f[:, KB * F:], part(7168, KB * F))]
        w2_sb = [v[:, 0:FB * D].rearrange("p (k f) -> p k f", k=FB) for v in (sv1f, sv1f[:, FB * D:], msgf)]
        tok = [part(9984 + (D + 1) * b, D + 1) for b in range(2)]
        tokT = [sv0f[:, 2560 + 256 * b:2816 + 256 * b].rearrange("p (k c) -> p k c", k=KB) for b in range(2)]
        hidT = [sv1f[:, 2048 + 512 * b:2560 + 512 * b].rearrange("p (k c) -> p k c", k=FB) for b in range(2)]
        eout = [thf[:, D * b:D * (b + 1)] for b in range(ER)]
        fdf = part(7168, 3584)
        got = [[(sv0f, sv1f, fdf)[b][:, 1792 * k:1792 * (k + 1)].rearrange("p (t d) -> p t d", t=TB)
                for k in range(2)] for b in range(GR)]

        sizes = (2, 5, 7, 7, 7, 7, 7, 5, 2)
        assert sum(sizes) == NT and max(sizes) <= TB
        last_batches = [(sum(sizes[:c]), sum(sizes[:c + 1])) for c in range(len(sizes))]

        block = ctx.enter_context(nc.Block())

        x_loaded = [sem(f"x_loaded{c}") for c in range(NBATCH)]
        x_padded = sem("x_padded")
        edges_padded = sem("edges_padded")
        edges_loaded = sem("edges_loaded")
        weights_loaded = sem("weights_loaded")
        consts_loaded = sem("consts_loaded")
        consts_made = sem("consts_made")
        zeros_made = sem("zeros_made")
        zeros_stored = sem("zeros_stored")
        w_turned = sem("w_turned")
        w_kept = sem("w_kept")
        var_ready = sem("var_ready")
        sd_ready = sem("sd_ready")
        h_normed = sem("h_normed")
        row_ready = sem("row_ready")
        h_turned = sem("h_turned")
        hT_ready = sem("hT_ready")
        projected = sem("projected")
        stage_ready = sem("stage_ready")
        stage_stored = [sem(f"stage_stored{b}") for b in range(2)]
        p0 = sem("p0_vector_done")
        e0 = sem("edge_vector_done")

        idx_ready = sem("idx_ready")
        prev_set = sem("prev_set")
        prev_loaded = sem("prev_loaded")
        chain_ready = sem("chain_ready")
        tails_turned = sem("tails_turned")
        lane_moves = sem("lane_moves")
        lane_moved = sem("lane_moved")
        lane_factors = sem("lane_factors")
        factors_wide = sem("factors_wide")
        lanes_summed = sem("lanes_summed")
        tails_back = sem("tails_back")
        tail_ready = sem("tail_ready")
        tail_stored = sem("tail_stored")
        counted = sem("counted")
        degrees_kept = sem("degrees_kept")
        degrees_summed = sem("degrees_summed")
        node_idx_ready = sem("node_idx_ready")
        node_gathered = [sem(f"node_gathered{b}") for b in range(2)]
        node_used = sem("node_used")
        moves_ready = sem("moves_ready")
        moved_ready = sem("moved_ready")
        u_ready = sem("u_ready")
        u_tanh = sem("u_tanh")
        x2_ready = sem("x2_ready")
        p1 = sem("p1_vector_done")
        ffn_loaded = sem("ffn_loaded")
        gate_loaded = sem("gate_loaded")
        y_turned = sem("y_turned")
        yT_ready = sem("yT_ready")
        y_var_ready = sem("y_var_ready")
        y_sd_ready = sem("y_sd_ready")
        y_moves_ready = sem("y_moves_ready")
        gated = sem("gated")
        logits_ready = sem("logits_ready")
        y_ready = sem("y_ready")
        gap_ready = sem("gap_ready")
        gap_exp = sem("gap_exp")
        chosen_ready = sem("chosen_ready")
        tile_sums = sem("tile_sums")
        tile_sums_kept = sem("tile_sums_kept")
        ranks = sem("ranks")
        slot_ready = sem("slot_ready")
        e_hot_ready = sem("e_hot_ready")
        b1_turned = sem("b1_turned")
        routing_done = sem("routing_done")
        first_sent = [sem(f"first_sent{c}") for c in range(NBATCH)]
        second_rows = sem("second_rows")
        tokens_sent = [sem(f"tokens_sent{c}") for c in range(NBATCH)]
        rows_known = sem("rows_known")
        eout_issued = sem("eout_issued")
        tok_loaded = [sem(f"tok_loaded{b}") for b in range(2)]
        w1_loaded = [sem(f"w1_loaded{b}") for b in range(WR)]
        w2_loaded = [sem(f"w2_loaded{b}") for b in range(WR)]
        tok_turned = sem("tok_turned")
        tokT_ready = sem("tokT_ready")
        hidden = sem("hidden")
        hidT_ready = sem("hidT_ready")
        expert_done = sem("expert_done")
        eout_ready = sem("eout_ready")
        eout_stored = [sem(f"eout_stored{b}") for b in range(ER)]
        out_gathered = [sem(f"out_gathered{b}") for b in range(GR)]
        share_turned = sem("share_turned")
        share_kept = sem("share_kept")
        b2_ready = sem("b2_ready")
        y_var = sem("y_var")
        y_sd = sem("y_sd")
        base_ready = sem("base_ready")
        out_ready = sem("out_ready")
        out_stored = [sem(f"out_stored{b}") for b in range(GR)]
        p2 = sem("p2_vector_done")
        gathers_issued = sem("gathers_issued")
        gathered = [sem(f"gathered{b}") for b in range(R)]
        attn_masked = sem("attn_masked")
        z_ready = sem("z_ready")
        silu_ready = sem("silu_ready")
        scored = sem("scored")
        score_read = sem("score_read")
        tanh_ready = sem("tanh_ready")
        diff_ready = sem("diff_ready")
        wgt_ready = sem("wgt_ready")
        side_ready = sem("side_ready")
        rec_ready = sem("rec_ready")
        span_parts = sem("span_parts")
        span_summed = sem("span_summed")
        span_known = sem("span_known")
        pick_ready = sem("pick_ready")
        rec_stored = [sem(f"rec_stored{b}") for b in range(2)]
        squares_ready = sem("squares_ready")
        low_ready = sem("low_ready")
        hot_ready = sem("hot_ready")
        hot_used = sem("hot_used")

        def node_tiles(eng, head, tail=None):
            first, steps = 7, 6
            for t in range(first):
                head(t, t % 2, t)
                if tail and t:
                    tail(t - 1, (t - 1) % 2, t - 1)
            assert (NT - first) % steps == 0
            with eng.Fori(0, (NT - first) // steps) as i:
                for k in range(first, first + steps):
                    head(i * steps + k, k % 2, k)
                    if tail:
                        tail(i * steps + (k - 1), (k - 1) % 2, k - 1)
            if tail:
                tail(NT - 1, (NT - 1) % 2, NT - 1)

        def first_pass():
            for c in range(NBATCH + 1):
                for part_of_norm, tiles in ((0, range(0, 2)), (1, range(2, 3)), (2, range(3, 5)), (3, range(5, 7))):
                    if c < NBATCH:
                        yield "norm", part_of_norm, c
                    if c:
                        for k in tiles:
                            yield "tile", None, (c - 1) * TB + k

        def expert_tiles(eng, step):
            first, steps, rest = 4, 6, 2

            def turns_of(i):
                return lambda n, off=0: ((i + off) % n, (i + off) // n)

            def turns_in(p, k):
                return lambda n, off=0: ((k + off) % n, p * (steps // n) + (k + off) // n)

            for i in range(first):
                step(i, turns_of(i), i, False)
            assert (MT - first - rest) % steps == 0
            with eng.Fori(0, (MT - first - rest) // steps) as p:
                for k in range(first, first + steps):
                    step(p * steps + k, turns_in(p, k), k, False)
            for i in range(MT - rest, MT):
                step(i, turns_of(i), i, i == MT - 1)

        def edge_groups(eng, head, tail=None):
            for g in range(R):
                head(g, g, g)
                if tail and g:
                    tail(g - 1, g - 1, g - 1)
            with eng.Fori(1, GROUPS // R) as i:
                for b in range(R):
                    head(i * R + b, b, R + b)
                    if tail:
                        tail(i * R + (b - 1) if b else (i - 1) * R + (R - 1), (b - 1) % R, R + b - 1)
            if tail:
                tail(GROUPS - 1, R - 1, GROUPS - 1)

        def by_nodes_a_group(eng, loop):
            eng.wait_ge(span_known, 1)
            few = eng.value_load(few_nodes[0:1, 0:1], min_val=0, max_val=1)
            with eng.If(few == 1):
                loop(True)
            with eng.Else():
                loop(False)

        @block.sync
        def _(sp):
            def load_x(c):
                full = min(TB, (N - c * TB * P) // P)
                sp.dma_start(node_x[:, c * TB:c * TB + full, :],
                             x[c * TB * P:(c * TB + full) * P, :].rearrange("(t p) d -> p t d", p=P)).then_inc(x_loaded[c], 16)
                if full < TB:
                    sp.wait_ge(x_padded, 1)
                    sp.dma_start(node_x[0:LAST, NT - 1, :], x[(NT - 1) * P:N, :]).then_inc(x_loaded[c], 16)
            load_x(0)
            for m, Wm in enumerate((Wsrc, Wval, Wdst)):
                sp.dma_start(w_raw[:, 2 * m:2 * m + 2, :],
                             Wm.rearrange("(o p) k -> p o k", p=P)).then_inc(weights_loaded, 16)
            load_x(1)
            for m, bb in enumerate((bsrc, bval, bdst)):
                sp.dma_start(bias3[:, m * D:(m + 1) * D],
                             bb.rearrange("(a d) -> a d", a=1).to_broadcast([P, D])).then_inc(consts_loaded, 16)
            sp.dma_start(attn_col[:, :], attn.rearrange("a h f -> (a h f)").rearrange("(k p) -> p k", p=P),
                         allow_slow_non_contiguous=True).then_inc(consts_loaded, 16)
            for c in range(2, NBATCH):
                load_x(c)
            sp.wait_ge(prev_set, 1)
            sp.dma_start(prev_dst[1:P, :], dst[0:(P - 1) * COLS].rearrange("(p j) -> p j", j=COLS)[:, COLS - 1:COLS],
                         allow_slow_non_contiguous=True).then_inc(prev_loaded, 16)
            sp.wait_ge(edges_padded, 2)
            full = E // COLS
            for arr, t in ((src, src_all), (dst, dst_all)):
                for a, z in ((0, 112), (112, full)):
                    sp.dma_start(t[a:z, 0:COLS], arr[a * COLS:z * COLS].rearrange("(p j) -> p j", j=COLS)).then_inc(edges_loaded, 16)
                sp.dma_start(t[full:full + 1, 0:E - full * COLS],
                             arr[full * COLS:E].rearrange("(p j) -> p j", p=1)).then_inc(edges_loaded, 16)
            def store_tile(t, s, least):
                sp.wait_ge(stage_ready, t + 1)
                sp.dma_start(sv_table[bass.ds(t * P, P), :], stage[s][:, 0:2 * D]).then_inc(stage_stored[s], 16)
                sp.dma_start(d_table[bass.ds(t * P, P), :], stage[s][:, 2 * D:3 * D]).then_inc(stage_stored[s], 16)
                sp.dma_start(d_pairs[bass.ds(t * P, P), 0:D], stage[s][:, 2 * D:3 * D]).then_inc(stage_stored[s], 16)
                if least == 0:
                    sp.dma_start(d_pairs[0:P - 1, D:2 * D], stage[s][1:P, 2 * D:3 * D]).then_inc(stage_stored[s], 16)
                else:
                    sp.dma_start(d_pairs[bass.ds(t * P - 1, P), D:2 * D], stage[s][:, 2 * D:3 * D]).then_inc(stage_stored[s], 16)
            node_tiles(sp, store_tile)

            rv = records.rearrange("(p j) r -> p j r", p=P)
            zero_rows = expert_in.rearrange("(p r) d -> p (r d)", p=P)
            sp.wait_ge(zeros_made, 1)
            sp.dma_start(zero_rows[:, MT * D:], zeros[:, 0:MT]).then_inc(zeros_stored, 16)

            def store_group(g, b, least):
                sp.wait_ge(side_ready, g + 1)
                sp.wait_ge(rec_ready, g + 1)
                sp.dma_start(rv[:, bass.ds(g * J, J), :], rec[b % 2]).then_inc(rec_stored[b % 2], 16)
                if b == 0 and least >= R:
                    sp.dma_start(zero_rows[:, bass.ds((g - R) * (ZC // R), ZC)].rearrange("p (a z) -> p a z", a=2),
                                 zeros.unsqueeze(1).to_broadcast([P, 2, ZC // 2])).then_inc(zeros_stored, 16)
            edge_groups(sp, store_group)
            for b in range(2):
                sp.wait_ge(rec_stored[b], 16 * (GROUPS // 2))
            sp.wait_ge(tail_ready, 2)
            sp.dma_start(lane_tails[0:P, :], tail_sb).then_inc(tail_stored, 16)
            sp.dma_start(lane_tails[P:P + 1, :], no_tail).then_inc(tail_stored, 16)
            sp.dma_start(gate_w_sb, gate_w.rearrange("(k p) e -> p k e", p=P)).then_inc(gate_loaded, 16)
            sp.dma_start(gate_b_sb, gate_b.rearrange("(a e) -> a e", a=1).to_broadcast([P, NE])).then_inc(gate_loaded, 16)
            sp.wait_ge(x2_ready, NBATCH)
            sp.dma_start(gamma_sb, gamma.rearrange("(a e) -> a e", a=1).to_broadcast([P, D])).then_inc(ffn_loaded, 16)
            sp.dma_start(beta_sb, beta.rearrange("(a e) -> a e", a=1).to_broadcast([P, D])).then_inc(ffn_loaded, 16)
            sp.dma_start(b1_sb, b1).then_inc(ffn_loaded, 16)
            sp.dma_start(b2_sb, b2).then_inc(ffn_loaded, 16)

            sp.wait_ge(routing_done, 1)

            def load_weights(i, w, least):
                e = sp.value_load(tile_expert[0:1, bass.ds(i, 1)], min_val=0, max_val=NE - 1)

                def load_them():
                    if least >= WR:
                        sp.wait_ge(hidden, i - WR + 1)
                    sp.dma_start(w1_sb[w].unsqueeze(1), w1[bass.ds(e, 1), :, :].rearrange("a (k p) f -> p a k f", p=P)).then_inc(w1_loaded[w], 16)
                    if least >= WR:
                        sp.wait_ge(expert_done, i - WR + 1)
                    sp.dma_start(w2_sb[w].unsqueeze(1), w2[bass.ds(e, 1), :, :].rearrange("a (k p) f -> p a k f", p=P)).then_inc(w2_loaded[w], 16)

                if least < WR:
                    load_them()
                else:
                    before = sp.value_load(tile_expert[0:1, bass.ds(i - WR, 1)], min_val=0, max_val=NE - 1)
                    with sp.If(e != before):
                        load_them()
                    with sp.Else():
                        sp.wait_ge(hidden, i - WR + 1)
                        sp.sem_inc(w1_loaded[w], 16)
                        sp.wait_ge(expert_done, i - WR + 1)
                        sp.sem_inc(w2_loaded[w], 16)

            for i in range(WR):
                load_weights(i, i, 0)
            for c in range(NBATCH):
                sp.wait_ge(tokens_sent[c], 16 * TB)

            def load_tok(i, b, again):
                if again:
                    sp.wait_ge(tok_turned, i - 1)
                    sp.wait_ge(rows_known, i - 1)
                sp.dma_start(tok[b], expert_in[bass.ds(i * P, P), :]).then_inc(tok_loaded[b], 16)

            load_tok(0, 0, False)

            def load_expert(i, turns, least, last):
                if not last:
                    load_tok(i + 1, turns(2, 1)[0], least >= 1)
                if least >= WR:
                    load_weights(i, turns(WR)[0], least)
            expert_tiles(sp, load_expert)

            for c, (a, z) in enumerate(last_batches):
                sp.wait_ge(out_ready, c + 1)
                full = min(z, N // P) - a
                sp.dma_start(out[a * P:(a + full) * P, :].rearrange("(t p) d -> p t d", p=P),
                             got[c % GR][0][:, 0:full, :]).then_inc(out_stored[c % GR], 16)
                if z == NT:
                    sp.dma_start(out[(NT - 1) * P:N, :], got[c % GR][0][0:LAST, full, :]).then_inc(out_stored[c % GR], 16)
            for b in range(GR):
                stores = len(sizes[b::GR]) + ((len(sizes) - 1) % GR == b)
                sp.wait_ge(out_stored[b], 16 * stores)

        @block.gpsimd
        def _(pool):
            pool.memset(node_x[:, NT - 1, :], 0.0).then_inc(x_padded, 1)
            pool.memset(src_all[:, COLS - 352:], 0).then_inc(edges_padded, 1)
            pool.memset(dst_all[:, COLS - 352:], N).then_inc(edges_padded, 1)
            pool.memset(ident[:, :], 0.0).then_inc(consts_made, 1)
            pool.iota(iota_f[:, :], pattern=[[1, P]], base=0, channel_multiplier=0,
                      allow_small_or_imprecise_dtypes=True).then_inc(consts_made, 1)
            pool.iota(iota_p[:, :], pattern=[[1, 1]], base=0, channel_multiplier=1,
                      allow_small_or_imprecise_dtypes=True).then_inc(consts_made, 1)
            pool.memset(epsc[:, :], EPS).then_inc(consts_made, 1)
            pool.memset(upper[:, :], 1.0).then_inc(consts_made, 1)
            pool.memset(ones[:, :], 1.0).then_inc(consts_made, 1)
            pool.memset(head_of[:, :], 1.0).then_inc(consts_made, 1)
            pool.memset(attn_head[:, :, :], 0.5).then_inc(attn_masked, 1)
            pool.wait_ge(attn_masked, 1)
            pool.affine_select(out=attn_head[:, :, :], in_=attn_head[:, :, :], compare_op=ALU.is_ge, fill=0.0,
                               base=0, pattern=[[P, KB], [-FH, H]], channel_multiplier=1).then_inc(attn_masked, 1)
            pool.wait_ge(attn_masked, 2)
            pool.affine_select(out=attn_head[:, :, :], in_=attn_head[:, :, :], compare_op=ALU.is_ge, fill=0.0,
                               base=FH - 1, pattern=[[-P, KB], [FH, H]], channel_multiplier=-1).then_inc(attn_masked, 1)
            pool.memset(prev_dst[:, :], -1).then_inc(prev_set, 1)
            pool.wait_ge(consts_made, 7)
            pool.affine_select(out=upper[:, :], in_=upper[:, :], compare_op=ALU.is_ge, fill=0.0,
                               base=0, pattern=[[1, P]], channel_multiplier=-1).then_inc(consts_made, 1)
            pool.affine_select(out=head_of[:, :], in_=head_of[:, :], compare_op=ALU.is_ge, fill=0.0,
                               base=0, pattern=[[1, D]], channel_multiplier=-FH).then_inc(consts_made, 1)
            pool.wait_ge(consts_made, 9)
            pool.affine_select(out=head_of[:, :], in_=head_of[:, :], compare_op=ALU.is_ge, fill=0.0,
                               base=FH - 1, pattern=[[-1, D]], channel_multiplier=FH).then_inc(consts_made, 1)
            pool.affine_select(out=ident[:, :], in_=ident[:, :], compare_op=ALU.not_equal, fill=1.0,
                               base=0, pattern=[[-1, P]], channel_multiplier=1).then_inc(consts_made, 1)
            pool.wait_ge(stage_stored[0], 16 * 4 * ((NT + 1) // 2))
            pool.wait_ge(stage_stored[1], 16 * 4 * (NT // 2))

            def gather_edges(few):
                def gather_group(g, b, least):
                    pool.wait_ge(idx_ready, g + 1)
                    pool.sem_inc(gathers_issued, 1)
                    for j in range(J):
                        pool.indirect_dma_start(sv[b][:, j, :], None, sv_table,
                                                bass.IndirectOffsetOnAxis(idx_src[b][:, j:j + 1], 0)).then_inc(gathered[b], 16)
                    if few:
                        pool.indirect_dma_start(fd[b][:, 0:2, :].rearrange("p a d -> p (a d)"), None, d_pairs[0:NT * P - 1, :],
                                                bass.IndirectOffsetOnAxis(idx_dst[b][:, 0:1], 0)).then_inc(gathered[b], 16)
                        return
                    for j in range(J):
                        pool.indirect_dma_start(fd[b][:, j, :], None, d_table,
                                                bass.IndirectOffsetOnAxis(idx_dst[b][:, j:j + 1], 0)).then_inc(gathered[b], 16)
                edge_groups(pool, gather_group)
            by_nodes_a_group(pool, gather_edges)
            pool.wait_ge(node_idx_ready, 2)
            for b in range(2):
                pool.wait_ge(rec_stored[b], 16 * (GROUPS // 2))
            for c in range(NBATCH):
                b = c % 2
                if c >= 2:
                    pool.wait_ge(node_used, c - 1)
                for k in range(TB):
                    t = c * TB + k
                    pool.indirect_dma_start(node_rec[b][:, k, :], None, records,
                                            bass.IndirectOffsetOnAxis(idx_last[:, t:t + 1], 0)).then_inc(node_gathered[b], 16)
                if c == 0:
                    pool.wait_ge(tail_stored, 32)
                for k in range(TB):
                    t = c * TB + k
                    pool.indirect_dma_start(node_car[b][:, k, :], None, lane_tails,
                                            bass.IndirectOffsetOnAxis(idx_tail[:, t:t + 1], 0)).then_inc(node_gathered[b], 16)
            pool.wait_ge(slot_ready, 1)
            pool.wait_ge(zeros_stored, 16 * (GROUPS // R))
            for h in range(2):
                for t in range(NT):
                    if h and t % TB == 0:
                        pool.wait_ge(second_rows, t // TB + 1)
                    s = h * NT + t
                    pool.indirect_dma_start(expert_in, bass.IndirectOffsetOnAxis(slot[:, s:s + 1], 0),
                                            node_rows[:, t, :], None).then_inc((first_sent, tokens_sent)[h][t // TB], 16)

            def send_results(i, turns, least, last):
                b, w = turns(ER)[0], turns(2 * ER)[0]
                pool.wait_ge(eout_ready, i + 1)
                pool.sem_inc(eout_issued, 1)
                pool.indirect_dma_start(results, bass.IndirectOffsetOnAxis(result_row[w][:, 0:1], 0),
                                        eout[b], None).then_inc(eout_stored[b], 16)
            expert_tiles(pool, send_results)

            assert MT % ER == 0
            for b in range(ER):
                pool.wait_ge(eout_stored[b], 16 * (MT // ER))
            for c, (a, z) in enumerate(last_batches):
                b = c % GR
                if c >= GR:
                    pool.wait_ge(out_stored[b], 16 * (c // GR))
                for h in range(2):
                    at = (MT + h * NT + a) * P
                    pool.dma_start(got[b][h][:, 0:z - a, :],
                                   results[at:at + (z - a) * P, :].rearrange("(t p) d -> p t d", p=P)).then_inc(out_gathered[b], 16)

        @block.tensor
        def _(pe):
            pe.wait_ge(consts_made, 11)
            pe.wait_ge(weights_loaded, 16 * 3)
            for m in range(3):
                for k in range(KB):
                    for o in range(2):
                        ins = pe.transpose(bank[2 * m + k][:, o * P:(o + 1) * P],
                                           w_raw[:, 2 * m + o, k * P:(k + 1) * P], ident[:, :])
                    ins.then_inc(w_turned, 1)
            pe.wait_ge(w_kept, 6)

            def turn_tile(t, s, least):
                if least >= 2:
                    pe.wait_ge(hT_ready, t - 1)
                pe.wait_ge(row_ready, t + 1)
                for k in range(KB):
                    ins = pe.transpose(bank[s][:, k * P:(k + 1) * P], h_row[s][:, k * P:(k + 1) * P], ident[:, :])
                ins.then_inc(h_turned, 1)

            def project_tile(t, s, least):
                pe.wait_ge(hT_ready, t + 1)
                if least >= 2:
                    pe.wait_ge(stage_ready, t - 1)
                for k in range(KB):
                    pe.matmul(bank[2 + 2 * s][:, :], hT[s][:, k, :], wT[:, k, 0:2 * D], start=(k == 0), stop=(k == KB - 1))
                for k in range(KB):
                    ins = pe.matmul(bank[3 + 2 * s][:, 0:D], hT[s][:, k, :], wT[:, k, 2 * D:3 * D],
                                    start=(k == 0), stop=(k == KB - 1))
                ins.then_inc(projected, 1)
            node_tiles(pe, turn_tile, project_tile)

            pe.wait_ge(span_parts, 1)
            pe.matmul(bank[7][:, 0:1], ones[:, :], span_part[:, :], start=True, stop=True).then_inc(span_summed, 1)

            def turn_group(g, b, few, least):
                q = b % 2
                if least >= 2:
                    pe.wait_ge(silu_ready, g - 1)
                if few:
                    pe.wait_ge(pick_ready, g + 1)
                rows = J + 1 if few else 2 * J
                pe.wait_ge(gathered[b], (g - b) * (16 * rows // R) + 16 * rows)
                for j in range(J):
                    for k in range(KB):
                        to = zT4[q][:, j, k, :]
                        pe.matmul(to, sv[b][:, j, k * P:(k + 1) * P], ident[:, :],
                                  is_transpose=True, start=True, stop=False)
                        if few and j:
                            pe.matmul(to, fd[b][:, 0, k * P:(k + 1) * P], pick_diag(b, 2 * j - 2),
                                      start=False, stop=False)
                            ins = pe.matmul(to, fd[b][:, 1, k * P:(k + 1) * P], pick_diag(b, 2 * j - 1),
                                            start=False, stop=True)
                        else:
                            ins = pe.matmul(to, fd[b][:, j, k * P:(k + 1) * P], ident[:, :],
                                            is_transpose=True, start=False, stop=True)
                ins.then_inc(z_ready, 1)

            def count_degrees(g, b, first):
                pe.wait_ge(hot_ready, g + 1)
                pe.wait_ge(low_ready, g + 1)
                for j in range(J):
                    ins = pe.matmul(degree_ps, hot_low[b % 2][:, j, :], hot_high[b % 2][:, j, :],
                                    start=(first and j == 0), stop=False, skip_group_check=True)
                ins.then_inc(hot_used, 1)

            def score_group(g, b, least):
                q = b % 2
                if least >= 2:
                    pe.wait_ge(score_read, g - 1)
                pe.wait_ge(silu_ready, g + 1)
                for j in range(J):
                    for k in range(KB):
                        ins = pe.matmul(score_ps[q][:, j * H:(j + 1) * H], th[q][:, (j * KB + k) * P:(j * KB + k + 1) * P],
                                        attn_head[:, k, :], start=(k == 0), stop=(k == KB - 1))
                ins.then_inc(scored, 1)
                if least >= 1:
                    count_degrees(g - 1, b - 1, least == 1)

            def score_edges(few):
                edge_groups(pe, lambda g, b, least: turn_group(g, b, few, least), score_group)
                count_degrees(GROUPS - 1, R - 1, False)
            by_nodes_a_group(pe, score_edges)
            pe.wait_ge(degrees_kept, 1)
            pe.matmul(bank[7][:, 0:NT], upper[:, :], nflag[:, 0, :], start=True, stop=True)
            pe.matmul(bank[7][:, 64:64 + NT], ones[:, :], nflag[:, 0, :], start=True, stop=True).then_inc(degrees_summed, 1)
            pe.wait_ge(rec_ready, GROUPS)
            pe.wait_ge(side_ready, GROUPS)
            pe.wait_ge(chain_ready, 1)
            tail = rec[1][:, J - 1, :]
            pe.transpose(bank[0][0:H, 0:P], tail[:, ACC:REC], ident[:, :])
            pe.transpose(bank[0][0:H, P:2 * P], tail[:, D:ACC], ident[:, :])
            pe.transpose(bank[0][:, 2 * P:3 * P], chain_wide, ident[:, :])
            for k in range(KB):
                ins = pe.transpose(bank[1][:, k * P:(k + 1) * P], tail[:, k * P:(k + 1) * P], ident[:, :])
            ins.then_inc(tails_turned, 1)
            pe.wait_ge(lane_factors, 1)
            for k in range(KB):
                ins = pe.matmul(bank[2 + k][:, 0:2 * P], head_of[:, k * P:(k + 1) * P], lane_exp, start=True, stop=True)
            ins.then_inc(factors_wide, 1)
            pe.wait_ge(lanes_summed, 1)
            for k in range(KB):
                pe.transpose(bank[4][:, k * P:(k + 1) * P], accT[:, k, :], ident[:, :])
            pe.transpose(bank[4][:, D:D + H], lane_den, ident[0:H, 0:H])
            pe.transpose(bank[4][:, ACC:REC], lane_max, ident[0:H, 0:H]).then_inc(tails_back, 1)
            pe.wait_ge(gate_loaded, 32)
            for c in range(NBATCH):
                pe.wait_ge(y_ready, c + 1)
                if c:
                    pe.wait_ge(yT_ready, c)
                for t in range(TB):
                    for k in range(KB):
                        ins = pe.transpose(yT_ps[:, t * D + k * P:t * D + (k + 1) * P],
                                           node_h[:, c * TB + t, k * P:(k + 1) * P], ident[:, :])
                ins.then_inc(y_turned, 1)
                pe.wait_ge(yT_ready, c + 1)
                if c:
                    pe.wait_ge(logits_ready, c)
                for t in range(TB):
                    for k in range(KB):
                        ins = pe.matmul(bank[5][:, t * NE:(t + 1) * NE], yT[:, t * D + k * P:t * D + (k + 1) * P],
                                        gate_w_sb[:, k, :], start=(k == 0), stop=(k == KB - 1))
                ins.then_inc(gated, 1)

            pe.wait_ge(chosen_ready, 1)
            q = W // 4
            for k in range(4):
                ins = pe.matmul(bank[k][:, 0:q], ones_bf[:, :], chosen_bf[:, k * q:(k + 1) * q], start=True, stop=True)
            ins.then_inc(tile_sums, 1)
            for k in range(4):
                ins = pe.matmul(bank[4 + k][:, 0:q], before_bf[:, :], chosen_bf[:, k * q:(k + 1) * q], start=True, stop=True)
            ins.then_inc(ranks, 1)
            pe.wait_ge(tile_sums_kept, 1)
            pe.wait_ge(ffn_loaded, 16 * 4)
            pe.wait_ge(e_hot_ready, 1)
            for k in range(FB):
                ins = pe.matmul(bank[0][:, k * MT:(k + 1) * MT], b1_sb[:, k * P:(k + 1) * P], e_hot, start=True, stop=True)
            ins.then_inc(b1_turned, 1)
            pe.wait_ge(routing_done, 1)

            for c in range(NBATCH):
                if c:
                    pe.wait_ge(share_kept, c)
                for k in range(TB):
                    ins = pe.transpose(psum[0:NE, k * P:(k + 1) * P], share[:, c * TB + k, :], ident[:, :])
                ins.then_inc(share_turned, 1)
                pe.wait_ge(share_kept, c + 1)
                if c:
                    pe.wait_ge(base_ready, c)
                for k in range(TB):
                    ins = pe.matmul(b2_ps[:, k * D:(k + 1) * D], share_t[:, k * P:(k + 1) * P], b2_sb, start=True, stop=True)
                ins.then_inc(b2_ready, 1)

            def turn(i, turns, again):
                b, before = turns
                if again:
                    pe.wait_ge(tokT_ready, i - 1)
                pe.wait_ge(tok_loaded[b], before * 16 + 16)
                for k in range(KB):
                    ins = pe.transpose(bank[b][:, k * P:(k + 1) * P], tok[b][:, k * P:(k + 1) * P], ident[:, :])
                ins.then_inc(tok_turned, 1)

            def first_layer(i, b, weights, again):
                w, before = weights
                pe.wait_ge(tokT_ready, i + 1)
                pe.wait_ge(w1_loaded[w], before * 16 + 16)
                if again:
                    pe.wait_ge(hidT_ready, i - 1)
                for f in range(FB):
                    for k in range(KB):
                        ins = pe.matmul(bank[2 + b][:, f * P:(f + 1) * P], w1_sb[w][:, k, f * P:(f + 1) * P],
                                        tokT[b][:, k, :], start=(k == 0), stop=(k == KB - 1))
                ins.then_inc(hidden, 1)

            def second_layer(i, b, weights, again):
                w, before = weights
                pe.wait_ge(hidT_ready, i + 1)
                pe.wait_ge(w2_loaded[w], before * 16 + 16)
                if again:
                    pe.wait_ge(eout_ready, i - 1)
                for f in range(FB):
                    ins = pe.matmul(bank[4 + b][:, 0:D], hidT[b][:, f, :], w2_sb[w][:, f, :],
                                    start=(f == 0), stop=(f == FB - 1))
                ins.then_inc(expert_done, 1)

            turn(0, (0, 0), False)
            pe.wait_ge(base_ready, NBATCH)

            def expert_step(i, turns, least, last):
                if not last:
                    turn(i + 1, turns(2, 1), least >= 1)
                first_layer(i, turns(2)[0], turns(WR), least >= 2)
                if least >= 1:
                    second_layer(i - 1, turns(2, -1)[0], turns(WR, -1), least >= 3)
            expert_tiles(pe, expert_step)
            second_layer(MT - 1, (MT - 1) % 2, ((MT - 1) % WR, (MT - 1) // WR), True)

        @block.scalar
        def _(act):
            def keep_weights():
                for n in range(6):
                    m, k = n // 2, n % 2
                    act.wait_ge(w_turned, n + 1)
                    act.copy(wT[:, k, m * D:(m + 1) * D], bank[n][:, 0:D]).then_inc(w_kept, 1)

            def keep_row(t):
                s = t % 2
                if t >= 2:
                    act.wait_ge(h_turned, t - 1)
                act.wait_ge(h_normed, t + 1)
                act.copy(h_row[s], node_h[:, t, :]).then_inc(row_ready, 1)

            def keep_hT(t):
                s = t % 2
                if t >= 2:
                    act.wait_ge(projected, t - 1)
                act.wait_ge(h_turned, t + 1)
                act.copy(hT[s].rearrange("p k c -> p (k c)"), bank[s][:, 0:2 * P]).then_inc(hT_ready, 1)

            act.wait_ge(consts_made, 4)
            roots = 0
            def take_root(at):
                tiles = slice(at * TB, (at + 1) * TB)
                act.activation(sd[:, tiles], mv[:, tiles, 1], ACT.Sqrt, bias=epsc[:, 0:1]).then_inc(sd_ready, 1)

            def keep_tile(t):
                keep_row(t)
                if t:
                    keep_hT(t - 1)

            for c in range(NBATCH + 1):
                for k in range(TB):
                    if c:
                        keep_tile((c - 1) * TB + k)
                    if c < NBATCH and k in (2, 5):
                        roots += 1
                        act.wait_ge(var_ready, roots)
                        take_root(c)
                        if roots == 2:
                            keep_weights()
            keep_hT(NT - 1)

            def place_picks(g, b):
                for n in range(PK):
                    ins = act.activation(pick_diag(b, n), ident[:, :], ACT.Copy,
                                         scale=pick[:, bass.ds(g * PK + n, 1)])
                ins.then_inc(pick_ready, 1)

            def tanh_group(g, b, few, least):
                q = b % 2
                if least >= 2:
                    act.wait_ge(scored, g - 1)
                act.wait_ge(z_ready, g + 1)
                act.activation(th[q], zT[q], ACT.Tanh, scale=0.5).then_inc(tanh_ready, 1)
                if few and least == 0:
                    place_picks(2, 2)

            def exp_group(g, b, few, least):
                q = b % 2
                act.wait_ge(scored, g + 1)
                if least >= 1:
                    act.wait_ge(diff_ready, g)
                act.copy(score[:, :, 1:M1].rearrange("p h j -> p j h"),
                         score_ps[q].rearrange("p (j h) -> p j h", h=H)).then_inc(score_read, 1)
                act.wait_ge(diff_ready, g + 1)
                act.activation(wgt[:, :, :], diff[:, :, :], ACT.Exp)
                if least >= 1:
                    act.wait_ge(rec_ready, g)
                act.activation(msg[:, :, D:ACC].rearrange("p j h -> p h j"), diff[:, :, 1:M1], ACT.Exp).then_inc(wgt_ready, 1)
                if least >= 2:
                    act.wait_ge(rec_stored[q], (g - q) * 8)
                act.copy(rec[q][:, :, ACC:REC].rearrange("p j h -> p h j"), smax[:, :, 1:M1]).then_inc(side_ready, 1)
                if least >= 2:
                    act.wait_ge(hot_used, g - 1)
                for j in range(J):
                    ins = act.activation(hot_low[q][:, j, :], iota_f[:, :], ACT.Square,
                                         bias=minus_low[:, bass.ds(g * J + j, 1)])
                ins.then_inc(squares_ready, 1)
                act.wait_ge(squares_ready, g + 1)
                act.activation(hot_low[q][:, :, :], hot_low[q][:, :, :], ACT.Relu, scale=-2.0, bias=ones[:, 0:1]).then_inc(low_ready, 1)
                if few:
                    place_picks(g + 3, (b + 3) % R)

            def weigh_edges(few):
                if few:
                    act.wait_ge(consts_made, 11)
                    for g in range(2):
                        place_picks(g, g)
                edge_groups(act, lambda g, b, least: tanh_group(g, b, few, least),
                            lambda g, b, least: exp_group(g, b, few, least))
            by_nodes_a_group(act, weigh_edges)
            act.wait_ge(lane_moves, 1)
            act.activation(lane_exp, lane_exp, ACT.Exp).then_inc(lane_moved, 1)
            for c in range(NBATCH + 1):
                tiles = slice((c - 1) * TB, c * TB)
                if c < NBATCH:
                    act.wait_ge(moves_ready, c + 1)
                    act.activation(moved, moves, ACT.Exp).then_inc(moved_ready, 1)
                if c:
                    act.wait_ge(y_var_ready, c)
                    act.activation(sd[:, tiles], mv[:, tiles, 1], ACT.Sqrt, bias=epsc[:, 0:1]).then_inc(y_sd_ready, 1)
                if c < NBATCH:
                    act.wait_ge(u_ready, c + 1)
                    act.activation(u_th, u_sb, ACT.Tanh, scale=0.5).then_inc(u_tanh, 1)
                if c:
                    act.wait_ge(y_moves_ready, c)
                    for t in range(tiles.start, tiles.stop):
                        ins = act.activation(node_h[:, t, :], node_x[:, t, :], ACT.Identity,
                                             scale=rstd[:, t:t + 1], bias=sd[:, t:t + 1])
                    ins.then_inc(y_ready, 1)
                    act.wait_ge(y_turned, c)
                    if c > 1:
                        act.wait_ge(gated, c - 1)
                    act.copy(yT, yT_ps).then_inc(yT_ready, 1)
            act.wait_ge(gap_ready, 1)
            act.activation(top_w[:, 1, :], top_w[:, 1, :], ACT.Exp).then_inc(gap_exp, 1)
            act.wait_ge(routing_done, 1)

            for c in range(NBATCH):
                if c:
                    act.wait_ge(b2_ready, c)
                act.wait_ge(share_turned, c + 1)
                act.copy(share_t, psum[0:NE, 0:TB * P]).then_inc(share_kept, 1)

            def keep_tokT(i, b, again):
                if again:
                    act.wait_ge(hidden, i - 1)
                act.wait_ge(tok_turned, i + 1)
                act.copy(tokT[b].rearrange("p k c -> p (k c)"), bank[b][:, 0:2 * P]).then_inc(tokT_ready, 1)

            keep_tokT(0, 0, False)

            def act_step(i, turns, least, last):
                b = turns(2)[0]
                if not last:
                    keep_tokT(i + 1, 1 - b, least >= 1)
                act.wait_ge(hidden, i + 1)
                if least >= 2:
                    act.wait_ge(expert_done, i - 1)
                for f in range(FB):
                    ins = act.activation(hidT[b][:, f, :], bank[2 + b][:, f * P:(f + 1) * P], ACT.Relu,
                                         bias=b1_of[:, f, bass.ds(i, 1)])
                ins.then_inc(hidT_ready, 1)
            expert_tiles(act, act_step)

            for c, (a, z) in enumerate(last_batches):
                act.wait_ge(y_var, c + 1)
                act.activation(sd[:, a:z], mv[:, a:z, 1], ACT.Sqrt,
                               bias=epsc[:, 0:1]).then_inc(y_sd, 1)

        @block.vector
        def _(dve):
            n0 = [0]

            def link(ins):
                n0[0] += 1
                ins.then_inc(p0, 1)
                dve.wait_ge(p0, n0[0])

            def tile_stats(v, tiles):
                for t in tiles:
                    ins = dve.bn_stats(stats[:, t, :], v[:, t, :])
                link(ins)
                for t in tiles:
                    ins = dve.bn_aggr(mv[:, t, :], stats[:, t, :])
                ins.then_inc(var_ready, 1)

            def normalize(v, to, tiles, roots):
                dve.wait_ge(sd_ready, roots)
                link(dve.reciprocal(rstd[:, tiles.start:tiles.stop], sd[:, tiles.start:tiles.stop]))
                for t in tiles:
                    ins = dve.tensor_scalar(to[:, t, :], v[:, t, :], mv[:, t, 0:1], rstd[:, t:t + 1],
                                            ALU.subtract, ALU.mult)
                return ins

            def add_bias(t):
                s = t % 2
                dve.wait_ge(projected, t + 1)
                if t >= 2:
                    dve.wait_ge(stage_stored[s], t // 2 * 64)
                dve.tensor_tensor(stage[s][:, 0:2 * D], bank[2 + 2 * s][:, :], bias3[:, 0:2 * D], ALU.add)
                dve.tensor_tensor(stage[s][:, 2 * D:3 * D], bank[3 + 2 * s][:, 0:D], bias3[:, 2 * D:3 * D],
                                  ALU.add).then_inc(stage_ready, 1)

            def edge_flags():
                dve.wait_ge(edges_loaded, 16 * 6)
                link(dve.memset(same[:, 0:1], 0.0))
                link(dve.memset(same[:, COLS:], 0.0))
                link(dve.tensor_tensor(same[:, 1:COLS], dst_all[:, 1:COLS], dst_all[:, 0:COLS - 1], ALU.is_equal))
                yield
                low_f = thf[:, 0:COLS]
                low_i = low_f.bitcast(I32)
                link(dve.tensor_single_scalar(low_i, dst_all[:, 0:COLS], P - 1, op=ALU.bitwise_and))
                yield
                link(dve.tensor_copy(minus_low[:, :], low_i))
                link(dve.tensor_scalar(minus_low[:, :], minus_low[:, :], -1.0, None, ALU.mult))
                yield
                link(dve.tensor_single_scalar(low_i, dst_all[:, 0:COLS], 7, op=ALU.arith_shift_right))
                link(dve.tensor_copy(dst_high[:, :], low_i))
                yield
                dve.wait_ge(consts_made, 11)
                link(dve.tensor_copy(iota_bf[:, :], iota_f[:, :]))
                dve.wait_ge(consts_loaded, 16 * 4)
                dve.wait_ge(attn_masked, 3)
                link(dve.tensor_tensor(attn_head[:, :, :], attn_head[:, :, :],
                                       attn_col[:, :].unsqueeze(2).to_broadcast([P, KB, H]), ALU.mult))
                link(dve.memset(seg_mask[:, :], -BIG))
                link(dve.memset(smax[:, :, :], 0.0))
                link(dve.memset(rec[1], 0.0))

                yield
                dve.wait_ge(prev_loaded, 16)
                dve.tensor_tensor(nflag[:, 1, 0:1], dst_all[:, 0:1], prev_dst[:, :], ALU.is_equal)
                link(dve.tensor_reduce(nflag[:, 2, 0:1], same[:, 1:COLS], AX.X, ALU.min))
                link(dve.tensor_tensor(chain[:, :], nflag[:, 1, 0:1], nflag[:, 2, 0:1], ALU.mult))

                yield
                s4 = same[:, 0:COLS].rearrange("p (g j) -> p g j", j=J)
                p6 = pick[:, 0:GROUPS * PK].rearrange("p (g n) -> p g n", n=PK)
                d4 = dst_all[:, 0:COLS].rearrange("p (g j) -> p g j", j=J)
                link(dve.tensor_copy(p6[:, :, 0], s4[:, :, 1]))
                for j in range(2, J):
                    link(dve.tensor_tensor(p6[:, :, 2 * j - 2], p6[:, :, 2 * j - 4], s4[:, :, j], ALU.mult))
                yield
                for j in range(1, J):
                    link(dve.tensor_scalar(p6[:, :, 2 * j - 1], p6[:, :, 2 * j - 2], -1.0, 1.0, ALU.mult, ALU.add))
                yield
                link(dve.memset(pick[:, GROUPS * PK:], 0.0))
                link(dve.tensor_tensor(low_i[:, 0:GROUPS], d4[:, :, J - 1], d4[:, :, 0], ALU.subtract))
                link(dve.tensor_copy(low_f[:, GROUPS:2 * GROUPS], low_i[:, 0:GROUPS]))
                link(dve.tensor_reduce(span_part[:, :], low_f[:, GROUPS:2 * GROUPS], AX.X, ALU.max))
                dve.tensor_scalar(span_part[:, :], span_part[:, :], 1.0, None, ALU.is_le).then_inc(span_parts, 1)
                dve.memset(zeros, 0.0).then_inc(zeros_made, 1)
                yield

            flags = edge_flags()

            for kind, piece, at in first_pass():
                if kind == "tile":
                    if at == 0:
                        dve.wait_ge(consts_loaded, 16 * 4)
                    add_bias(at)
                    if at >= NT - 9:
                        next(flags)
                    continue
                tiles = range(at * TB, (at + 1) * TB)
                if piece == 0:
                    dve.wait_ge(x_loaded[at], 16 if at < NBATCH - 1 else 32)
                    tile_stats(node_x, tiles)
                elif piece == 1:
                    link(normalize(node_x, node_h, tiles, 2 * at + 1))
                elif piece == 2:
                    tile_stats(node_h, tiles)
                else:
                    normalize(node_h, node_h, tiles, 2 * at + 2).then_inc(h_normed, TB)

            dve.wait_ge(span_summed, 1)
            link(dve.tensor_scalar(few_nodes[:, :], bank[7][:, 0:1], P - 0.5, None, ALU.is_ge))
            dve.drain().then_inc(span_known, 1)
            dve.wait_ge(stage_stored[0], 16 * 4 * ((NT + 1) // 2))
            dve.wait_ge(stage_stored[1], 16 * 4 * (NT // 2))
            for b in range(R):
                link(dve.tensor_copy(idx_src[b][:, :], src_all[:, b * J:(b + 1) * J]))
                dve.tensor_copy(idx_dst[b][:, :], dst_all[:, b * J:(b + 1) * J]).then_inc(idx_ready, 1)
            dve.wait_ge(idx_ready, R)

            def silu_group(g, b):
                q = b % 2
                dve.wait_ge(tanh_ready, g + 1)
                dve.scalar_tensor_tensor(out=th[q], in0=th[q], scalar=1.0, in1=zT[q],
                                         op0=ALU.add, op1=ALU.mult).then_inc(silu_ready, 1)

            STEPS = 2 + 3 + J + 3
            n = [0]

            def mark(ins):
                n[0] += 1
                ins.then_inc(e0, 1)
                return n[0]

            def done(g, count):
                dve.wait_ge(e0, g * STEPS + 2 + count)

            def cols(v, at, n):
                return v[:, bass.ds(at, n)]

            def open_group(g):
                mark(dve.tensor_scalar(seg_mask[:, 0:H * M1].rearrange("p (h j) -> p h j", h=H)[:, :, 1:M1],
                                       cols(same, g * J, J).unsqueeze(1).to_broadcast([P, H, J]),
                                       BIG, -BIG, ALU.mult, ALU.add))
                mark(dve.tensor_copy(score[:, :, 0:1], smax[:, :, J:M1]))

            def maxima_group(g, b, least):
                q = b % 2
                n[0] = 0
                done(g, 0)
                dve.wait_ge(score_read, g + 1)
                at = mark(dve.tensor_tensor_scan(fmax[:, :], seg_mask[:, 0:H * M1],
                                                 score[:, :, :].rearrange("p h j -> p (h j)"), 0.0, ALU.add, ALU.max))
                done(g, at)
                if least >= 1:
                    dve.wait_ge(side_ready, g)
                at = mark(dve.tensor_tensor_scan(smax[:, :, :].rearrange("p h j -> p (h j)")[:, ::-1],
                                                 seg_mask[:, 1:H * M1 + 1][:, ::-1],
                                                 fmax[:, ::-1], 0.0, ALU.add, ALU.max))
                done(g, at)
                dve.tensor_tensor(diff[:, :, :], score[:, :, :], smax[:, :, :], ALU.subtract).then_inc(diff_ready, 1)

            def sum_group(g, b, least):
                q = b % 2
                col = g * J
                dve.wait_ge(wgt_ready, g + 1)
                mark(dve.tensor_tensor(msg[:, :, 0:D].rearrange("p j (h f) -> p j h f", h=H),
                                       sv[b][:, :, D:2 * D].rearrange("p j (h f) -> p j h f", h=H),
                                       wgt[:, :, 1:M1].rearrange("p h j -> p j h").unsqueeze(3).to_broadcast([P, J, H, FH]),
                                       ALU.mult))
                mark(dve.tensor_copy(idx_src[b][:, :], cols(src_all, col + R * J, J)))
                dve.tensor_copy(idx_dst[b][:, :], cols(dst_all, col + R * J, J)).then_inc(idx_ready, 1)
                if least >= 1:
                    dve.wait_ge(rec_ready, g)
                mark(dve.tensor_tensor(carry[:, D:ACC], rec[1 - q][:, J - 1, D:ACC],
                                       wgt[:, :, 0], ALU.mult))
                placed = mark(dve.tensor_tensor(carry[:, 0:D].rearrange("p (h f) -> p h f", h=H),
                                                rec[1 - q][:, J - 1, 0:D].rearrange("p (h f) -> p h f", h=H),
                                                wgt[:, :, 0:1].to_broadcast([P, H, FH]), ALU.mult))
                if least >= 2:
                    dve.wait_ge(hot_used, g - 1)
                    dve.wait_ge(rec_stored[q], (g - q) * 8)

                def high_half(a, z):
                    return dve.tensor_tensor(hot_high[q][:, a:z, :],
                                             iota_bf[:, 0:NT].unsqueeze(1).to_broadcast([P, z - a, NT]),
                                             cols(dst_high, col + a, z - a).unsqueeze(2).to_broadcast([P, z - a, NT]),
                                             ALU.is_equal)

                mark(high_half(0, J // 2))
                for j in range(J):
                    done(g, placed)
                    ins = dve.scalar_tensor_tensor(
                        out=rec[q][:, j, 0:ACC], in0=carry[:, :] if j == 0 else rec[q][:, j - 1, 0:ACC],
                        scalar=cols(same, col + j, 1), in1=msg[:, j, :], op0=ALU.mult, op1=ALU.add)
                    if j < J - 1:
                        placed = mark(ins)
                    else:
                        ins.then_inc(rec_ready, 1)
                    if j == 0:
                        high_half(J // 2, J).then_inc(hot_ready, 1)
                    if j == 1:
                        dve.wait_ge(diff_ready, g + 1)
                        open_group(g + 1)
                assert n[0] == STEPS, n[0]

            def edge_step(g, b, least):
                if least >= 1:
                    maxima_group(g - 1, (b - 1) % R, least - 1)
                silu_group(g, b)
                if least >= 1:
                    sum_group(g - 1, (b - 1) % R, least - 1)
            open_group(0)
            edge_groups(dve, edge_step)
            maxima_group(GROUPS - 1, R - 1, GROUPS - 1)
            sum_group(GROUPS - 1, R - 1, GROUPS - 1)
            dve.wait_ge(rec_ready, GROUPS)

            m0 = [0]

            def link1(ins):
                m0[0] += 1
                ins.then_inc(p1, 1)
                dve.wait_ge(p1, m0[0])

            deg, cum, tot, incl, start, last, lane, has = (nflag[:, k, :] for k in range(8))
            dve.wait_ge(hot_used, GROUPS)
            dve.wait_ge(zeros_stored, 16 * (GROUPS // R))
            dve.tensor_copy(deg, bank[6][:, 0:NT]).then_inc(degrees_kept, 1)
            link1(dve.tensor_copy(chain_wide, chain[:, 0:1].to_broadcast([P, P])))
            dve.drain().then_inc(chain_ready, 1)
            dve.wait_ge(degrees_summed, 1)
            link1(dve.tensor_copy(tot, bank[7][:, 64:64 + NT]))
            link1(dve.tensor_tensor_scan(incl, ones[:, 0:NT], tot, 0.0, ALU.mult, ALU.add))
            link1(dve.tensor_tensor(cum, bank[7][:, 0:NT], incl, ALU.add))
            link1(dve.tensor_tensor(cum, cum, tot, ALU.subtract))
            link1(dve.tensor_tensor(start, cum, deg, ALU.subtract))
            link1(dve.tensor_scalar(last, cum, -1.0, 0.0, ALU.add, ALU.max))
            link1(dve.tensor_scalar(lane, last, 0.5, 1.0 / COLS, ALU.add, ALU.mult))
            link1(dve.tensor_scalar(lane, lane, -0.5, None, ALU.add))
            link1(dve.tensor_scalar(lane, lane, 8388608.0, None, ALU.add))
            link1(dve.tensor_scalar(lane, lane, -8388608.0, None, ALU.add))
            link1(dve.scalar_tensor_tensor(out=start, in0=lane, scalar=float(COLS), in1=start,
                                           op0=ALU.mult, op1=ALU.is_gt))
            link1(dve.tensor_scalar(lane, lane, -1.0 - P, None, ALU.add))
            link1(dve.tensor_tensor(lane, lane, start, ALU.mult))
            link1(dve.tensor_scalar(lane, lane, float(P), None, ALU.add))
            dve.tensor_copy(idx_last[:, :], last).then_inc(node_idx_ready, 1)
            dve.tensor_copy(idx_tail[:, :], lane).then_inc(node_idx_ready, 1)
            link1(dve.tensor_scalar(has, deg, 1.0, None, ALU.min))

            dve.wait_ge(tails_turned, 1)
            dve.tensor_copy(mT, bank[0][0:H, 0:P])
            dve.tensor_copy(dT, bank[0][0:H, P:2 * P])
            dve.tensor_copy(aT.rearrange("p k l -> p (k l)"), bank[1][:, 0:2 * P])
            link1(dve.tensor_copy(chainT, bank[0][:, 2 * P:3 * P]))
            link1(dve.tensor_scalar(lane_mask, chainT, BIG, -BIG, ALU.mult, ALU.add))
            link1(dve.tensor_tensor_scan(lane_max, lane_mask[0:H, :], mT, 0.0, ALU.add, ALU.max))
            dve.memset(lane_exp[:, P:P + 1], 0.0)
            dve.tensor_tensor(lane_exp[:, 0:P], mT, lane_max, ALU.subtract)
            link1(dve.tensor_tensor(lane_exp[:, P + 1:2 * P], lane_max[:, 0:P - 1], lane_max[:, 1:P], ALU.subtract))
            dve.tensor_scalar(lane_exp[:, P:2 * P], lane_exp[:, P:2 * P], 0.0, None, ALU.min).then_inc(lane_moves, 1)
            dve.wait_ge(lane_moved, 1)
            dve.tensor_tensor(lane_exp[:, P:2 * P], lane_exp[:, P:2 * P], chainT[0:H, :], ALU.mult).then_inc(lane_factors, 1)
            dve.wait_ge(lane_factors, 1)
            link1(dve.tensor_tensor(dT, dT, lane_exp[:, 0:P], ALU.mult))
            link1(dve.tensor_tensor_scan(lane_den, lane_exp[:, P:2 * P], dT, 0.0, ALU.mult, ALU.add))
            dve.wait_ge(factors_wide, 1)
            for k in range(KB):
                ins = dve.tensor_tensor(aT[:, k, :], aT[:, k, :], bank[2 + k][:, 0:P], ALU.mult)
            link1(ins)
            for k in range(KB):
                ins = dve.tensor_tensor_scan(accT[:, k, :], bank[2 + k][:, P:2 * P], aT[:, k, :], 0.0, ALU.mult, ALU.add)
            ins.then_inc(lanes_summed, 1)
            dve.wait_ge(tails_back, 1)
            dve.tensor_copy(tail_sb, bank[4][:, 0:REC]).then_inc(tail_ready, 1)
            link1(dve.memset(no_tail, 0.0))
            dve.memset(no_tail[:, ACC:REC], -BIG).then_inc(tail_ready, 1)
            dve.wait_ge(tail_ready, 2)

            k0 = [0]

            def link2(ins):
                k0[0] += 1
                ins.then_inc(p2, 1)
                dve.wait_ge(p2, k0[0])

            def join(c):
                b = c % 2
                own, before = node_rec[b], node_car[b]
                dve.wait_ge(node_gathered[b], 16 * 2 * TB * (c // 2 + 1))
                link1(dve.tensor_tensor(nmax, own[:, :, ACC:REC], before[:, :, ACC:REC], ALU.max))
                dve.tensor_tensor(moves[:, :, 0:H], own[:, :, ACC:REC], nmax, ALU.subtract)
                dve.tensor_tensor(moves[:, :, H:2 * H], before[:, :, ACC:REC], nmax, ALU.subtract).then_inc(moves_ready, 1)
                dve.wait_ge(moved_ready, c + 1)
                dve.tensor_tensor(own[:, :, D:ACC], own[:, :, D:ACC], moved[:, :, 0:H], ALU.mult)
                link1(dve.tensor_tensor(before[:, :, D:ACC], before[:, :, D:ACC], moved[:, :, H:2 * H], ALU.mult))
                link1(dve.tensor_tensor(nden, own[:, :, D:ACC], before[:, :, D:ACC], ALU.add))
                link1(dve.reciprocal(nden, nden))
                link1(dve.tensor_tensor(nden, nden, has[:, c * TB:(c + 1) * TB].unsqueeze(2).to_broadcast([P, TB, H]), ALU.mult))
                dve.tensor_tensor(moved[:, :, 0:H], moved[:, :, 0:H], nden, ALU.mult)
                link1(dve.tensor_tensor(moved[:, :, H:2 * H], moved[:, :, H:2 * H], nden, ALU.mult))
                for rows, fac in ((own, moved[:, :, 0:H]), (before, moved[:, :, H:2 * H])):
                    v = rows[:, :, 0:D].rearrange("p t (h f) -> p t h f", h=H)
                    ins = dve.tensor_tensor(v, v, fac.unsqueeze(3).to_broadcast([P, TB, H, FH]), ALU.mult)
                link1(ins)
                dve.tensor_tensor(u_sb, own[:, :, 0:D], before[:, :, 0:D], ALU.add).then_inc(node_used, 1)
                dve.wait_ge(node_used, c + 1)
                dve.tensor_tensor(u_sb, u_sb, node_h[:, c * TB:(c + 1) * TB, :], ALU.add).then_inc(u_ready, 1)

            def residual(c):
                dve.wait_ge(u_tanh, c + 1)
                link1(dve.scalar_tensor_tensor(out=u_th, in0=u_th, scalar=1.0, in1=u_sb, op0=ALU.add, op1=ALU.mult))
                v = node_x[:, c * TB:(c + 1) * TB, :]
                dve.scalar_tensor_tensor(out=v, in0=u_th, scalar=0.5, in1=v, op0=ALU.mult, op1=ALU.add).then_inc(x2_ready, 1)
                dve.wait_ge(x2_ready, c + 1)
                for t in range(c * TB, (c + 1) * TB):
                    ins = dve.bn_stats(stats[:, t, :], node_x[:, t, :])
                link1(ins)
                for t in range(c * TB, (c + 1) * TB):
                    ins = dve.bn_aggr(mv[:, t, :], stats[:, t, :])
                ins.then_inc(y_var_ready, 1)

            def expert_input(c):
                dve.wait_ge(y_sd_ready, c + 1)
                tiles = slice(c * TB, (c + 1) * TB)
                link1(dve.reciprocal(rstd[:, tiles], sd[:, tiles]))
                dve.scalar_tensor_tensor(out=sd[:, tiles], in0=mv[:, tiles, 0], scalar=-1.0, in1=rstd[:, tiles],
                                         op0=ALU.mult, op1=ALU.mult).then_inc(y_moves_ready, 1)

            def top_two(c):
                dve.wait_ge(gated, c + 1)
                tiles = range(c * TB, (c + 1) * TB)
                dve.tensor_tensor(logits[:, c * TB:(c + 1) * TB, :],
                                  bank[5][:, 0:TB * NE].rearrange("p (t e) -> p t e", t=TB),
                                  gate_b_sb.unsqueeze(1).to_broadcast([P, TB, NE]), ALU.add).then_inc(logits_ready, 1)
                dve.wait_ge(logits_ready, c + 1)
                for t in tiles:
                    ins = dve.max(top8[:, t, :], logits[:, t, :])
                link1(ins)
                for t in tiles:
                    ins = dve.max_index(top8_at[:, t, :], top8[:, t, :], logits[:, t, :])
                return ins

            dve.wait_ge(gate_loaded, 32)
            for c in range(NBATCH + 2):
                if 1 <= c <= NBATCH:
                    residual(c - 1)
                if c < NBATCH:
                    join(c)
                if 1 <= c <= NBATCH:
                    expert_input(c - 1)
                if c == NBATCH + 1:
                    link2(dve.tensor_tensor(before_bf[:, :], upper[:, :], ident[:, :], ALU.subtract))
                    link2(dve.tensor_copy(ones_bf[:, :], ones[:, :]))
                    own_row = node_rows[:, :, D]
                    link2(dve.tensor_scalar(own_row, iota_f[:, 0:NT], float(P), iota_p[:, 0:1], ALU.mult, ALU.add))
                    link2(dve.tensor_scalar(own_row, own_row, float(MT * P), None, ALU.add))
                    link2(dve.tensor_scalar(spare_row[:, :], iota_f[:, 0:MT], float(P), iota_p[:, 0:1], ALU.mult, ALU.add))
                    link2(dve.memset(restart, 1.0))
                    link2(dve.memset(restart.rearrange("p (e s) -> p e s", e=NE)[:, :, 0:1], 0.0))
                if c >= 2:
                    ins = top_two(c - 2)
            link1(ins)
            dve.tensor_tensor(top_w[:, 1, :], top8[:, :, 1], top8[:, :, 0], ALU.subtract).then_inc(gap_ready, 1)
            for k in range(2):
                ins = dve.tensor_copy(choice[:, k, :], top8_at[:, :, k])
            link2(ins)
            for k in range(2):
                link2(dve.tensor_tensor(chosen[:, :, k * NT:(k + 1) * NT],
                                        iota_f[:, 0:NE].unsqueeze(2).to_broadcast([P, NE, NT]),
                                        choice[:, k, :].unsqueeze(1).to_broadcast([P, NE, NT]), ALU.is_equal))
            dve.tensor_copy(chosen_bf, chosen.rearrange("p e s -> p (e s)")).then_inc(chosen_ready, 1)
            dve.wait_ge(gap_exp, 1)
            link2(dve.tensor_scalar(top_w[:, 0, :], top_w[:, 1, :], 1.0, None, ALU.add))
            link2(dve.reciprocal(top_w[:, 0, :], top_w[:, 0, :]))
            link2(dve.tensor_tensor(top_w[:, 1, :], top_w[:, 1, :], top_w[:, 0, :], ALU.mult))
            dve.wait_ge(tile_sums, 1)
            q = W // 4
            for k in range(4):
                ins = dve.tensor_copy(taken[:, k * q:(k + 1) * q], bank[k][:, 0:q])
            ins.then_inc(tile_sums_kept, 1)
            dve.wait_ge(tile_sums_kept, 1)
            link2(dve.tensor_tensor_scan(running, restart, taken, 0.0, ALU.mult, ALU.add))
            need, upto, base = ends[:, 0, :], ends[:, 1, :], ends[:, 2, :]
            need_i = ends[:, 3, :].bitcast(I32)
            totals = running.rearrange("p (e s) -> p e s", e=NE)[:, :, S2 - 1]
            link2(dve.tensor_scalar(need, totals, float(P - 1), None, ALU.add))
            link2(dve.tensor_copy(need_i, need))
            link2(dve.tensor_single_scalar(need_i, need_i, 7, op=ALU.arith_shift_right))
            link2(dve.tensor_copy(need, need_i))
            link2(dve.tensor_tensor_scan(upto, ones[:, 0:NE], need, 0.0, ALU.mult, ALU.add))
            link2(dve.tensor_tensor(base, upto, need, ALU.subtract))
            link2(dve.tensor_scalar(base, base, float(P), None, ALU.mult))
            link2(dve.tensor_tensor(running, running, taken, ALU.subtract))
            dve.wait_ge(ranks, 1)
            for k in range(4):
                ins = dve.tensor_tensor(place[:, k * q:(k + 1) * q], bank[4 + k][:, 0:q], running[:, k * q:(k + 1) * q], ALU.add)
            link2(ins)
            place3 = place.rearrange("p (e s) -> p e s", e=NE)
            link2(dve.tensor_tensor(place3, place3, base.unsqueeze(2).to_broadcast([P, NE, S2]), ALU.add))
            link2(dve.tensor_tensor(place3, place3, chosen, ALU.mult))
            link2(dve.tensor_reduce(taken[:, 0:S2], place3.rearrange("p e s -> p s e"), AX.X, ALU.add))
            dve.tensor_copy(slot[:, :], taken[:, 0:S2]).then_inc(slot_ready, 1)
            dve.wait_ge(slot_ready, 1)
            link2(dve.memset(tile_of, 0.0))
            for k in range(2):
                e3 = restart[:, 0:MT * 8].rearrange("p (i e) -> p i e", e=8)
                link2(dve.tensor_tensor(e3, iota_f[:, 0:MT].unsqueeze(2).to_broadcast([P, MT, 8]),
                                        upto[:, 8 * k:8 * k + 8].unsqueeze(1).to_broadcast([P, MT, 8]), ALU.is_ge))
                link2(dve.tensor_reduce(taken[:, 200:200 + MT], e3, AX.X, ALU.add))
                link2(dve.tensor_tensor(tile_of, tile_of, taken[:, 200:200 + MT], ALU.add))
            link2(dve.tensor_scalar(tile_of, tile_of, float(NE - 1), None, ALU.min))
            link2(dve.tensor_copy(tile_expert[:, :], tile_of))
            dve.tensor_scalar(e_hot, tile_of[0:NE, :], iota_p[0:NE, 0:1], None, ALU.is_equal).then_inc(e_hot_ready, 1)
            c3 = fd1f[:, 0:NT * NE].rearrange("p (e t) -> p e t", e=NE)
            c4 = fd1f[:, NT * NE:2 * NT * NE].rearrange("p (e t) -> p e t", e=NE)
            for k, v in enumerate((c3, c4)):
                link2(dve.tensor_tensor(v, chosen[:, :, k * NT:(k + 1) * NT],
                                        top_w[:, k, :].unsqueeze(1).to_broadcast([P, NE, NT]), ALU.mult))
            link2(dve.tensor_tensor(share.rearrange("p t e -> p e t"), c3, c4, ALU.add))
            dve.wait_ge(b1_turned, 1)
            dve.tensor_copy(b1_of[:, :, :].rearrange("p k i -> p (k i)"), bank[0][:, 0:FB * MT]).then_inc(routing_done, 1)

            dve.wait_ge(ffn_loaded, 16 * 4)
            link2(dve.tensor_tensor(node_x[:, :, :], node_x[:, :, :],
                                    beta_sb.unsqueeze(1).to_broadcast([P, NT, D]), ALU.add))
            for c in range(NBATCH):
                dve.wait_ge(first_sent[c], 16 * TB)
                own_row = node_rows[:, c * TB:(c + 1) * TB, D]
                dve.tensor_scalar(own_row, own_row, float(NT * P), None, ALU.add).then_inc(second_rows, 1)
            for c in range(NBATCH):
                dve.wait_ge(b2_ready, c + 1)
                dve.wait_ge(tokens_sent[c], 16 * TB)
                v = node_h[:, c * TB:(c + 1) * TB, :]
                dve.tensor_tensor(v, v, b2_ps.rearrange("p (t d) -> p t d", t=TB), ALU.add).then_inc(base_ready, 1)
            dve.wait_ge(base_ready, NBATCH)

            def place_rows(i, turns, off):
                b, before = turns(2, off)
                dve.wait_ge(tok_loaded[b], before * 16 + 16)
                dve.tensor_tensor(result_row[turns(2 * ER, off)[0]][:, :], tok[b][:, D:D + 1], spare_row[:, bass.ds(i, 1)],
                                  ALU.max).then_inc(rows_known, 1)
            for i in range(2):
                place_rows(i, lambda n, off: (off, 0), i)

            def keep_eout(i, turns, least, last):
                b, before = turns(ER)
                if least >= ER:
                    dve.wait_ge(eout_stored[b], before * 16)
                if least < MT - 2:
                    place_rows(i + 2, turns, 2)
                dve.wait_ge(expert_done, i + 1)
                dve.tensor_copy(eout[b], bank[4 + turns(2)[0]][:, 0:D]).then_inc(eout_ready, 1)
            expert_tiles(dve, keep_eout)

            for c in range(len(sizes) + 1):
                if c < len(sizes):
                    g0, g1 = got[c % GR]
                    tiles = range(*last_batches[c])
                    dve.wait_ge(out_gathered[c % GR], 16 * 2 * (c // GR + 1))
                    for k, t in enumerate(tiles):
                        ins = dve.scalar_tensor_tensor(out=g1[:, k, :], in0=g1[:, k, :], scalar=top_w[:, 1, t:t + 1],
                                                       in1=node_h[:, t, :], op0=ALU.mult, op1=ALU.add)
                    link2(ins)
                    for k, t in enumerate(tiles):
                        ins = dve.scalar_tensor_tensor(out=g0[:, k, :], in0=g0[:, k, :], scalar=top_w[:, 0, t:t + 1],
                                                       in1=g1[:, k, :], op0=ALU.mult, op1=ALU.add)
                    link2(ins)
                    for k, t in enumerate(tiles):
                        ins = dve.bn_stats(stats[:, t, :], g0[:, k, :])
                    link2(ins)
                    for t in tiles:
                        ins = dve.bn_aggr(mv[:, t, :], stats[:, t, :])
                    ins.then_inc(y_var, 1)
                if c:
                    g0 = got[(c - 1) % GR][0]
                    tiles = range(*last_batches[c - 1])
                    dve.wait_ge(y_sd, c)
                    link2(dve.reciprocal(rstd[:, tiles.start:tiles.stop], sd[:, tiles.start:tiles.stop]))
                    for k, t in enumerate(tiles):
                        ins = dve.scalar_tensor_tensor(out=g0[:, k, :], in0=g0[:, k, :], scalar=mv[:, t, 0:1],
                                                       in1=gamma_sb, op0=ALU.subtract, op1=ALU.mult)
                    link2(ins)
                    for k, t in enumerate(tiles):
                        ins = dve.scalar_tensor_tensor(out=g0[:, k, :], in0=g0[:, k, :], scalar=rstd[:, t:t + 1],
                                                       in1=node_x[:, t, :], op0=ALU.mult, op1=ALU.add)
                    ins.then_inc(out_ready, 1)


_NAMES = {"x": "x", "src": "src", "dst": "dst", "Wsrc": "L0_gnn_Wsrc", "bsrc": "L0_gnn_bsrc", "Wdst": "L0_gnn_Wdst",
          "bdst": "L0_gnn_bdst", "Wval": "L0_gnn_Wval", "bval": "L0_gnn_bval", "attn": "L0_gnn_attn",
          "gate_w": "L0_ffn_gate_w", "gate_b": "L0_ffn_gate_b", "w1": "L0_ffn_w1", "b1": "L0_ffn_b1",
          "w2": "L0_ffn_w2", "b2": "L0_ffn_b2", "gamma": "L0_ffn_gamma", "beta": "L0_ffn_beta"}


def kernel(**inputs):
    import numpy as _np
    import concourse.bacc as _bacc
    from concourse.bass_utils import run_bass_kernel_spmd as _run

    nc = _bacc.Bacc("TRN2", target_bir_lowering=False, num_devices=1)
    arrays, args = {}, {}
    for short, name in _NAMES.items():
        a = _np.ascontiguousarray(inputs[name])
        arrays[f"in_{short}"] = a
        args[short] = nc.dram_tensor(f"in_{short}", a.shape, mybir.dt.from_np(a.dtype), kind="ExternalInput").ap()
    shape = inputs["x"].shape
    out = nc.dram_tensor("out_0", shape, F32, kind="ExternalOutput").ap()
    build_gnn_moe(nc, out=out, **args)
    r = _run(nc, [arrays], core_ids=[0])
    return r.results[0]["out_0"]
```
